# Optimizing a Trainium2 kernel written in Bass

```python
import numpy as np
import jax
import jax.numpy as jnp

def _softmax(x, axis=-1):
    return jax.nn.softmax(x, axis=axis)

def _gelu(x):
    return jax.nn.gelu(x, approximate=True)

def _silu(x):
    return jax.nn.silu(x)

def _sigmoid(x):
    return jax.nn.sigmoid(x)

def _layernorm(x, axis=-1, eps=1e-05):
    m = jnp.mean(x, axis=axis, keepdims=True)
    v = jnp.var(x, axis=axis, keepdims=True)
    return (x - m) / jnp.sqrt(v + eps)

def _scatter_add(tgt, idx, src, axis=0):
    return tgt.at[idx].add(src)

def _segment_sum(src, seg, n):
    return jax.ops.segment_sum(src, seg, n)
kernel_name = 'mk_seq_preln_d1_jaxref_r8_ee266e'

def setup_inputs(seed: int=0):
    np.random.seed(seed)
    _w = jnp.asarray

    def _L0_attn_setup():
        import jax, jax.numpy as jnp
        import numpy as np
        HID, NH, NOPE, ROPE, VD = (256, 16, 128, 64, 128)
        QC, KVC = (192, 64)
        BASE = 10000.0
        EPS = 1e-06

        def _rms(x, w):
            return x * jax.lax.rsqrt(jnp.mean(x * x, axis=-1, keepdims=True) + EPS) * w

        def _rotate_half(x):
            h = x.shape[-1] // 2
            return jnp.concatenate([-x[..., h:], x[..., :h]], axis=-1)

        def _rope_tables(seq_len, dtype):
            inv_freq = 1.0 / BASE ** (jnp.arange(0, ROPE, 2, dtype=jnp.float32) / ROPE)
            t = jnp.arange(seq_len, dtype=jnp.float32)
            freqs = t[:, None] * inv_freq[None, :]
            emb = jnp.concatenate([freqs, freqs], axis=-1)
            return (jnp.cos(emb).astype(dtype), jnp.sin(emb).astype(dtype))
        key = jax.random.key(seed)
        ks = jax.random.split(key, 10)
        s = 0.02
        B, S = (2, 256)
        return {'x': jax.random.normal(ks[0], (B, S, HID), jnp.float32), 'w_q_down': jax.random.normal(ks[1], (QC, HID), jnp.float32) * s, 'q_norm_w': jnp.ones((QC,), jnp.float32), 'w_q_nope': jax.random.normal(ks[2], (NH * NOPE, QC), jnp.float32) * s, 'w_q_rope': jax.random.normal(ks[3], (NH * ROPE, QC), jnp.float32) * s, 'w_kv_down': jax.random.normal(ks[4], (KVC, HID), jnp.float32) * s, 'kv_norm_w': jnp.ones((KVC,), jnp.float32), 'w_k_nope': jax.random.normal(ks[5], (NH * NOPE, KVC), jnp.float32) * s, 'w_v_up': jax.random.normal(ks[6], (NH * VD, KVC), jnp.float32) * s, 'w_k_rope': jax.random.normal(ks[7], (ROPE, HID), jnp.float32) * s, 'w_o': jax.random.normal(ks[8], (HID, NH * VD), jnp.float32) * s}
    _L0_attn_in = _L0_attn_setup()

    def _L0_ffn_setup():
        import jax, jax.numpy as jnp
        import numpy as np
        BLOCK_SIZE = 32
        FP4_GRID = jnp.array([0.0, 0.5, 1.0, 1.5, 2.0, 3.0, 4.0, 6.0], dtype=jnp.float32)
        FP4_MIDS = jnp.array([0.25, 0.75, 1.25, 1.75, 2.5, 3.5, 5.0], dtype=jnp.float32)

        def quantize_to_mxfp4(w, block_size=BLOCK_SIZE):
            K, N = w.shape
            wb = w.reshape(K // block_size, block_size, N)
            amax = jnp.max(jnp.abs(wb), axis=1, keepdims=True)
            exp = jnp.floor(jnp.log2(jnp.maximum(amax, 1e-30))) - 2.0
            scales = jnp.exp2(exp)
            x = wb / scales
            idx = jnp.digitize(jnp.abs(x), FP4_MIDS)
            q = jnp.sign(x) * FP4_GRID[idx]
            return (q, scales)

        def mxfp4_matmul(inputs, q, scales, block_size=BLOCK_SIZE):
            K = inputs.shape[-1]
            N = q.shape[-1]
            w = (q * scales).reshape(K, N)
            return inputs @ w
        key = jax.random.key(seed)
        ks = jax.random.split(key, 3)
        B, S, D, F = (4, 256, 256, 1024)
        inputs = jax.random.normal(ks[0], (B, S, D), dtype=jnp.float32)
        up_kernel = jax.random.normal(ks[1], (D, F), dtype=jnp.float32) * (1.0 / np.sqrt(D))
        down_kernel = jax.random.normal(ks[2], (F, D), dtype=jnp.float32) * (1.0 / np.sqrt(F))
        up_bias = jnp.zeros((F,), dtype=jnp.float32)
        down_bias = jnp.zeros((D,), dtype=jnp.float32)
        return {'inputs': inputs, 'up_kernel': up_kernel, 'up_bias': up_bias, 'down_kernel': down_kernel, 'down_bias': down_bias}
    _L0_ffn_in = _L0_ffn_setup()
    _d = {'L0_attn_x': _L0_attn_in['x'], 'L0_attn_w_q_down': _L0_attn_in['w_q_down'], 'L0_attn_q_norm_w': _L0_attn_in['q_norm_w'], 'L0_attn_w_q_nope': _L0_attn_in['w_q_nope'], 'L0_attn_w_q_rope': _L0_attn_in['w_q_rope'], 'L0_attn_w_kv_down': _L0_attn_in['w_kv_down'], 'L0_attn_kv_norm_w': _L0_attn_in['kv_norm_w'], 'L0_attn_w_k_nope': _L0_attn_in['w_k_nope'], 'L0_attn_w_v_up': _L0_attn_in['w_v_up'], 'L0_attn_w_k_rope': _L0_attn_in['w_k_rope'], 'L0_attn_w_o': _L0_attn_in['w_o'], 'L0_ffn_up_kernel': _L0_ffn_in['up_kernel'], 'L0_ffn_up_bias': _L0_ffn_in['up_bias'], 'L0_ffn_down_kernel': _L0_ffn_in['down_kernel'], 'L0_ffn_down_bias': _L0_ffn_in['down_bias']}
    _x0 = _d['L0_attn_x']
    _d['L0_attn_x'] = jax.random.normal(jax.random.fold_in(jax.random.key(seed), 1), (16, 256, 256), dtype=_x0.dtype)
    del _x0
    return _d

def reference(L0_attn_x, L0_attn_w_q_down, L0_attn_q_norm_w, L0_attn_w_q_nope, L0_attn_w_q_rope, L0_attn_w_kv_down, L0_attn_kv_norm_w, L0_attn_w_k_nope, L0_attn_w_v_up, L0_attn_w_k_rope, L0_attn_w_o, L0_ffn_up_kernel, L0_ffn_up_bias, L0_ffn_down_kernel, L0_ffn_down_bias):

    def _L0_attn_ref(x, w_q_down, q_norm_w, w_q_nope, w_q_rope, w_kv_down, kv_norm_w, w_k_nope, w_v_up, w_k_rope, w_o):
        import jax, jax.numpy as jnp
        import numpy as np
        HID, NH, NOPE, ROPE, VD = (256, 16, 128, 64, 128)
        QC, KVC = (192, 64)
        BASE = 10000.0
        EPS = 1e-06

        def _rms(x, w):
            return x * jax.lax.rsqrt(jnp.mean(x * x, axis=-1, keepdims=True) + EPS) * w

        def _rotate_half(x):
            h = x.shape[-1] // 2
            return jnp.concatenate([-x[..., h:], x[..., :h]], axis=-1)

        def _rope_tables(seq_len, dtype):
            inv_freq = 1.0 / BASE ** (jnp.arange(0, ROPE, 2, dtype=jnp.float32) / ROPE)
            t = jnp.arange(seq_len, dtype=jnp.float32)
            freqs = t[:, None] * inv_freq[None, :]
            emb = jnp.concatenate([freqs, freqs], axis=-1)
            return (jnp.cos(emb).astype(dtype), jnp.sin(emb).astype(dtype))
        B, S, _ = x.shape
        scale = (NOPE + ROPE) ** (-0.5)
        c_q = _rms(jnp.einsum('bsh,qh->bsq', x, w_q_down), q_norm_w)
        q_nope = jnp.einsum('bsq,dq->bsd', c_q, w_q_nope).reshape(B, S, NH, NOPE).transpose(0, 2, 1, 3)
        q_rope = jnp.einsum('bsq,dq->bsd', c_q, w_q_rope).reshape(B, S, NH, ROPE).transpose(0, 2, 1, 3)
        c_kv = _rms(jnp.einsum('bsh,ch->bsc', x, w_kv_down), kv_norm_w)
        k_rope = jnp.einsum('bsh,rh->bsr', x, w_k_rope)
        cos, sin = _rope_tables(S, x.dtype)
        k_rope = k_rope * cos[None] + _rotate_half(k_rope) * sin[None]
        q_rope = q_rope * cos[None, None] + _rotate_half(q_rope) * sin[None, None]
        k_nope = jnp.einsum('bsc,dc->bsd', c_kv, w_k_nope).reshape(B, S, NH, NOPE).transpose(0, 2, 1, 3)
        v = jnp.einsum('bsc,dc->bsd', c_kv, w_v_up).reshape(B, S, NH, VD).transpose(0, 2, 1, 3)
        k_rope_h = jnp.broadcast_to(k_rope[:, None], (B, NH, S, ROPE))
        q = jnp.concatenate([q_nope, q_rope], axis=-1)
        k = jnp.concatenate([k_nope, k_rope_h], axis=-1)
        attn = jnp.einsum('bhqd,bhkd->bhqk', q, k) * scale
        attn = jax.nn.softmax(attn.astype(jnp.float32), axis=-1).astype(q.dtype)
        out = jnp.einsum('bhqk,bhkd->bhqd', attn, v)
        out = out.transpose(0, 2, 1, 3).reshape(B, S, NH * VD)
        return jnp.einsum('bsd,hd->bsh', out, w_o)

    def _L0_ffn_ref(inputs, up_kernel, up_bias, down_kernel, down_bias):
        import jax, jax.numpy as jnp
        import numpy as np
        BLOCK_SIZE = 32
        FP4_GRID = jnp.array([0.0, 0.5, 1.0, 1.5, 2.0, 3.0, 4.0, 6.0], dtype=jnp.float32)
        FP4_MIDS = jnp.array([0.25, 0.75, 1.25, 1.75, 2.5, 3.5, 5.0], dtype=jnp.float32)

        def quantize_to_mxfp4(w, block_size=BLOCK_SIZE):
            K, N = w.shape
            wb = w.reshape(K // block_size, block_size, N)
            amax = jnp.max(jnp.abs(wb), axis=1, keepdims=True)
            exp = jnp.floor(jnp.log2(jnp.maximum(amax, 1e-30))) - 2.0
            scales = jnp.exp2(exp)
            x = wb / scales
            idx = jnp.digitize(jnp.abs(x), FP4_MIDS)
            q = jnp.sign(x) * FP4_GRID[idx]
            return (q, scales)

        def mxfp4_matmul(inputs, q, scales, block_size=BLOCK_SIZE):
            K = inputs.shape[-1]
            N = q.shape[-1]
            w = (q * scales).reshape(K, N)
            return inputs @ w
        q_up, s_up = quantize_to_mxfp4(up_kernel, BLOCK_SIZE)
        x = mxfp4_matmul(inputs, q_up, s_up, BLOCK_SIZE) + up_bias
        x = jax.nn.gelu(x)
        q_dn, s_dn = quantize_to_mxfp4(down_kernel, BLOCK_SIZE)
        x = mxfp4_matmul(x, q_dn, s_dn, BLOCK_SIZE) + down_bias
        return x
    x = L0_attn_x
    x = x + _L0_attn_ref(_layernorm(x, axis=-1), L0_attn_w_q_down, L0_attn_q_norm_w, L0_attn_w_q_nope, L0_attn_w_q_rope, L0_attn_w_kv_down, L0_attn_kv_norm_w, L0_attn_w_k_nope, L0_attn_w_v_up, L0_attn_w_k_rope, L0_attn_w_o)
    x = x + _L0_ffn_ref(_layernorm(x, axis=-1), L0_ffn_up_kernel, L0_ffn_up_bias, L0_ffn_down_kernel, L0_ffn_down_bias)
    return x

_drawn_inputs = setup_inputs


def setup_inputs(seed=0):
    import zlib

    import numpy as np

    out = dict(_drawn_inputs(seed))
    spreads = {'L0_attn_q_norm_w': (1.0, 0.6),
     'L0_attn_kv_norm_w': (1.0, 0.6),
     'L0_ffn_up_bias': (0.0, 0.708),
     'L0_ffn_down_bias': (0.0, 0.424)}
    factors = {'L0_attn_w_q_down': 8.0,
     'L0_attn_w_q_nope': 8.0,
     'L0_attn_w_q_rope': 8.0,
     'L0_attn_w_kv_down': 6.487,
     'L0_attn_w_k_nope': 8.0,
     'L0_attn_w_v_up': 6.337,
     'L0_attn_w_k_rope': 8.0,
     'L0_attn_w_o': 6.281}
    for name, (base, spread) in spreads.items():
        noise = np.random.default_rng([zlib.crc32(name.encode()), seed]).standard_normal(out[name].shape)
        drawn = base * np.exp(spread * noise) if base else spread * noise
        out[name] = jnp.asarray(drawn.astype(out[name].dtype))
    for name, factor in factors.items():
        out[name] = (out[name] * factor).astype(out[name].dtype)
    return out
```

```python
import math
from contextlib import ExitStack

import concourse.bass as bass
from concourse import mybir

F32, F16, BF16, I32 = mybir.dt.float32, mybir.dt.float16, mybir.dt.bfloat16, mybir.dt.int32
ALU, ACT, AX = mybir.AluOpType, mybir.ActivationFunctionType, mybir.AxisListType

P = 128
B, S, HID = 16, 256, 256
NH, NOPE, ROPE, VD = 16, 128, 64, 128
QC, KVC, FF = 192, 64, 1024
HD = KVC + ROPE
QT = S // P
CT = HID // P
QB = QC - P
QUAD = 4
NQ = NH // QUAD
PAIRS = NH // 2
FT = FF // P
BLOCK = 32
DOWN = QC + KVC + ROPE
SCALE = (NOPE + ROPE) ** -0.5
LN_EPS, RMS_EPS = 1e-5, 1e-6
UP = 64.0
WMAX = 2.0 ** 7
PLIFT = 14 * math.log(2.0)
GELU_C = math.sqrt(2.0 / math.pi)
GELU_A = 0.044715

SLOTS = [
    ([("OT", 0), ("ln1", 0)], [("OT", 1), ("ln1x", 0)]),
    ([("OT", 2)], [("xT", 0)]),
    ([("D", 0)], [("OT", 3)]),
    ([("D", 1), ("scale", 0)], [("proj", 0)]),
    ([("scale", 1), ("ln2", 0)], [("KT", 0)]),
    ([("cT", 0)], [("Q", 0)]),
    ([("Q", 1)], [("x2T", 0)]),
    ([("Q", 2)], [("QT", 0)]),
    ([("up", 0)], [("Q", 3)]),
    ([("QT", 1), ("gelu", 0)], [("up", 1), ("split", 0)]),
    ([("Q", 4), ("gelu", 1)], [("QT", 2), ("split", 1)]),
    ([("up", 2)], [("Q", 5)]),
    ([("QT", 3), ("gelu", 2)], [("up", 3), ("split", 2)]),
    ([("Q", 6), ("gelu", 3)], [("QT", 4), ("split", 3)]),
    ([("down", 0)], [("Q", 7)]),
    ([("QT", 5)], [("QT", 6), ("QT", 7)]),
]
FRONT = [j for s in SLOTS for part in s for j in part if j[0] in ("xT", "D", "KT", "cT", "Q", "QT")]
BACK = [j for s in SLOTS for part in s for j in part if j[0] in ("OT", "proj", "x2T", "up", "down")]
FRONT_TASKS = ("ln1", "ln1x", "xT", "D", "scale", "KT", "cT", "Q", "QT")
BACK_TASKS = ("OT", "proj", "ln2", "x2T", "up", "gelu", "split", "down")
ACT_LAST = ("xT", "D", "up")
FRONT_DVE = [j for j in FRONT if j[0] not in ACT_LAST]
BACK_ACT = [j for j in BACK if j[0] not in ("proj", "down")]
BACK_DVE = [j for j in BACK if j[0] not in ACT_LAST]
NF, NFD, NB_, NBA, NBD = len(FRONT), len(FRONT_DVE), len(BACK), len(BACK_ACT), len(BACK_DVE)


class Batch:

    def __init__(self, const, pair=None):
        self.const, self.pair, self.parity = const, pair, const % 2

    def plus(self, d):
        return Batch(self.const + d, self.pair)

    def at(self, per, extra):
        v = per * self.const + extra
        return v if self.pair is None else self.pair * (2 * per) + v

    def first(self):
        return self.pair is None and self.const == 0


def wait(eng, sem, value):
    if isinstance(value, int) and value <= 0:
        return
    eng.wait_ge(sem, value)


def build(nc, x, w_q_down, q_norm_w, w_q_nope, w_q_rope, w_kv_down, kv_norm_w, w_k_nope, w_v_up,
          w_k_rope, w_o, up_kernel, up_bias, down_kernel, down_bias, rope_table, out):
    ctx = ExitStack()
    with ctx:
        def sb(name, shape, dt=F32):
            return ctx.enter_context(nc.sbuf_tensor(name, shape, dt))

        def sem(name):
            return ctx.enter_context(nc.semaphore(name))

        ident = sb("ident", [P, P])
        ident16 = sb("ident16", [P, P], BF16)
        rope = sb("rope", [P, QT, 2, ROPE])
        wdT = sb("wdT", [P, CT, DOWN])
        wa_hi = sb("wa_hi", [P, NH * HD], F16)
        wa_lo = sb("wa_lo", [P, NH * HD], F16)
        wb_hh = sb("wb_hh", [P, NH * HD], F16)
        wb_lo = sb("wb_lo", [QB, NH * HD], F16)
        n_hi = sb("n_hi", [P, PAIRS, HID], F16)
        n_lo = sb("n_lo", [P, PAIRS, HID], F16)
        up_q = sb("up_q", [P, CT, FF], BF16)
        dn_q = sb("dn_q", [P, FT, HID], BF16)
        ub = sb("ub", [P, FT])
        db = sb("db", [P, HID])
        small = sb("small", [P, 64])
        inv_kr, inv_s, inv_n, s_g, inv_g = (small[:, i:i + 1] for i in range(5))
        ln_eps, rms_eps, neg_half = (small[:, 8 + 2 * i:10 + 2 * i] for i in range(3))
        plift = small[:, 14:15]

        xf = sb("xf", [P, QT, HID])
        xb = sb("xb", [P, QT, HID])
        nothing = sb("nothing", [P, 1])
        st = sb("st", [P, 2, QT, 6])
        mv = sb("mv", [P, 2, QT, 2])
        va = sb("va", [P, 2, QT])
        rstd = sb("rstd", [P, 2, QT])
        xn = sb("xn", [P, QT, HID])
        xT = sb("xT", [P, CT, S])
        raw = sb("raw", [P, QT, DOWN])
        sq = sb("sq", [P, QT, QC + KVC])
        ssq = sb("ssq", [P, QT, 2])
        sse = sb("sse", [P, QT, 2])
        rms = sb("rms", [P, QT, 2])
        cq = sb("cq", [P, QT, QC])
        kt = sb("kt", [P, QT, HD])
        kr = sb("kr", [P, 2, ROPE])
        c_hi = [sb(f"c_hi{i}", [P, QT, KVC], F16) for i in range(2)]
        c_lo = [sb(f"c_lo{i}", [P, QT, KVC], F16) for i in range(2)]
        k_hi = [sb(f"k_hi{i}", [P, S], F16) for i in range(2)]
        k_lo = [sb(f"k_lo{i}", [P, S], F16) for i in range(2)]
        ca_hi = sb("ca_hi", [P, S], F16)
        ca_lo = sb("ca_lo", [P, S], F16)
        cb = sb("cb", [P, S], F16)
        qtok = [sb(f"qtok{i}", [P, QUAD, HD]) for i in range(4)]
        qr = [sb(f"qr{i}", [P, 2, QUAD, ROPE]) for i in range(2)]
        nmax = sb("nmax", [P, 2, QT])
        ebias = sb("ebias", [P, 2, QT])
        rsum = sb("rsum", [P, NH, QT])
        rinv = sb("rinv", [P, NH, QT])
        pr = [sb(f"pr{i}", [P, QT, S]) for i in range(2)]
        pt_hi = [sb(f"pt_hi{i}", [P, QT, S], F16) for i in range(2)]
        pt_lo = [sb(f"pt_lo{i}", [P, QT, S], F16) for i in range(2)]
        x1 = sb("x1", [P, QT, HID])
        x1b = sb("x1b", [P, QT, HID])
        x2n = sb("x2n", [P, QT, HID])
        x2_hi = sb("x2_hi", [P, CT, S], F16)
        x2_lo = sb("x2_lo", [P, CT, S], F16)
        gu = [sb(f"gu{i}", [P, 2, S]) for i in range(2)]
        gv = sb("gv", [P, 2, S])
        gz = sb("gz", [P, 2, S])
        gt = sb("gt", [P, 2, S])
        ob = sb("ob", [P, QT, HID])

        late = sb("late", [P, 12288])
        q_hi0, q_lo0 = sb("q_hi0", [P, NH, S], F16), sb("q_lo0", [P, NH, S], F16)

        def carve(at, n, dt=F32):
            a = late[:, at:at + n]
            return a if dt is F32 else a.bitcast(dt)

        q_hi = [q_hi0, carve(0, 2048, F16).rearrange("p (h s) -> p h s", h=NH)]
        q_lo = [q_lo0, carve(2048, 2048, F16).rearrange("p (h s) -> p h s", h=NH)]
        otok = carve(4096, 2048).rearrange("p (t h c) -> p t h c", t=QT, h=NH // 2)
        otok = carve(4096, 2 * NH * KVC).rearrange("p (t h c) -> p t h c", t=QT, h=NH)
        ot_hi = carve(6144, 1024, F16).rearrange("p (j s) -> p j s", j=PAIRS)
        ot_lo = carve(7168, 1024, F16).rearrange("p (j s) -> p j s", j=PAIRS)
        g_hi = carve(8192, 1024, F16).rearrange("p (f s) -> p f s", f=FT)
        g_lo = carve(9216, 1024, F16).rearrange("p (f s) -> p f s", f=FT)
        wf_a = carve(8192, 2048).rearrange("p (h c) -> p h c", h=NH)
        wf_b = carve(10240, 2048).rearrange("p (h c) -> p h c", h=NH)
        wo_n = carve(0, 4096).rearrange("p (m d) -> p m d", m=CT)
        woT = carve(4096, 4096).rearrange("p (h c) -> p h c", h=NH)

        quant = sb("quant", [P, 8704])
        wqn = quant[:, 0:3072].rearrange("p (h c) -> p h c", h=NH)
        wkn = quant[:, 3072:4096].rearrange("p (h c) -> p h c", h=NH)
        wqr = quant[:, 4096:5632].rearrange("p (j c) -> p j c", j=PAIRS)
        wvn = quant[:, 5632:6656].rearrange("p (h c) -> p h c", h=NH)
        nf = quant[:, 6656:8704].rearrange("p (j c) -> p j c", j=PAIRS)
        w_nat = quant[:, 0:2048]
        w_T = quant[:, 2048:4096]
        w_c = quant[:, 4096:6144]
        w_x = quant[:, 6144:8192]
        w_16 = sb("w_16", [P, 2048], BF16)
        blk = sb("blk", [P, 4, 64])
        wd_n = sb("wd_n", [P, 3, HID])
        qn_a, qn_b = small[:, 16:17], small[0:QB, 17:18]
        qs_a, qs_b = small[:, 18:19], small[0:QB, 19:20]
        qr_a, qr_b = small[:, 20:21], small[0:QB, 21:22]
        kvn_c = small[:, 22:23]
        kvn_r = sb("kvn_r", [P, KVC])
        mx = sb("mx", [P, 16])

        bank = [ctx.enter_context(nc.psum_tensor(f"bank{i}", [P, 512], F32)) for i in range(8)]
        l_bank, t_bank, o_bank, f_bank, b_bank = bank[0:2], bank[2:4], bank[4], bank[5:7], bank[7]

        ident_zeroed, ident_made, ident16_made = sem("ident_zeroed"), sem("ident_made"), sem("ident16_made")
        wd_loaded, wq_loaded, wo_loaded = sem("wd_loaded"), sem("wq_loaded"), sem("wo_loaded")
        vec_loaded, up_loaded, dn_loaded = sem("vec_loaded"), sem("up_loaded"), sem("dn_loaded")
        consts_set = sem("consts_set")
        prep_filled, prep_act, prep_dve = sem("prep_filled"), sem("prep_act"), sem("prep_dve")
        prep_step = sem("prep_step")
        max_asked, max_given = sem("max_asked"), sem("max_given")
        kr_scaled, quantised = sem("kr_scaled"), sem("quantised")
        xf_loaded = sem("xf_loaded")
        xb_loaded = sem("xb_loaded")
        ln_stats = [sem("ln1_stats"), sem("ln2_stats")]
        ln_aggr = [sem("ln1_aggr"), sem("ln2_aggr")]
        ln_eps_added = [sem("ln1_eps_added"), sem("ln2_eps_added")]
        ln_rstd = [sem("ln1_rstd"), sem("ln2_rstd")]
        xn_ready, x2n_ready = sem("xn_ready"), sem("x2n_ready")
        front_filled, front_act, front_dve = sem("front_filled"), sem("front_act"), sem("front_dve")
        back_filled, back_act, back_dve = sem("back_filled"), sem("back_act"), sem("back_dve")
        rms_eps_added, rms_ready = sem("rms_eps_added"), sem("rms_ready")
        kr_parts, kr_ready = sem("kr_parts"), sem("kr_ready")
        latents_ready, c_hi_ready, c_ready = sem("latents_ready"), sem("c_hi_ready"), sem("c_ready")
        qr_ready, qtok_ready = sem("qr_ready"), sem("qtok_ready")
        logits_ready, max_found, bias_ready = sem("logits_ready"), sem("max_found"), sem("bias_ready")
        probs_ready, probsT_ready = sem("probs_ready"), sem("probsT_ready")
        pt_hi_ready, pt_lo_ready = sem("pt_hi_ready"), sem("pt_lo_ready")
        pv_done, rinv_ready, o_ready = sem("pv_done"), sem("rinv_ready"), sem("o_ready")
        x1_ready, x1b_ready = sem("x1_ready"), sem("x1b_ready")
        gv_ready, gz_ready, gt_ready, g_raw, g_hi_ready, g_ready = (
            sem(n) for n in ("gv_ready", "gz_ready", "gt_ready", "g_raw", "g_hi_ready", "g_ready"))
        ob_ready, stored = sem("ob_ready"), sem("stored")

        block = ctx.enter_context(nc.Block())

        prep = ([("wd", k, "act") for k in range(CT)] + [("ma", k, "dve") for k in range(2)]
                + [("mb", k, "dve") for k in range(2)] + [("ra", k, "dve") for k in range(2)]
                + [("rb", k, "dve") for k in range(2)]
                + [("wo", k, "act") for k in range(8)] + [("n", k, "dve") for k in range(4)]
                + [("upT", k, "act") for k in range(4)] + [("upB", k, "act") for k in range(2)]
                + [("dnT", k, "act") for k in range(4)] + [("dnB", k, "act") for k in range(2)])
        prep_at = {(j[0], j[1]): i for i, j in enumerate(prep)}

        def prep_count(i):
            return sum(j[2] == prep[i][2] for j in prep[:i + 1])

        def front_bank(n, j):
            return f_bank[(NF * n.parity + FRONT.index(j)) % 2]

        def free_front(pe, n, j):
            k = FRONT.index(j) - 2
            m = n if k >= 0 else n.plus(-1)
            if m.pair is None and m.const < 0:
                return
            old = FRONT[k]
            if old[0] in ACT_LAST:
                pe.wait_ge(front_act, m.at(NF, FRONT.index(old) + 1))
            else:
                pe.wait_ge(front_dve, m.at(NFD, FRONT_DVE.index(old) + 1))

        def free_back(pe, n, j):
            k = BACK.index(j) - 1
            m = n if k >= 0 else n.plus(-1)
            if m.pair is None and m.const < 0:
                return
            old = BACK[k]
            if old[0] in ACT_LAST:
                pe.wait_ge(back_act, m.at(NBA, BACK_ACT.index(old) + 1))
            else:
                pe.wait_ge(back_dve, m.at(NBD, BACK_DVE.index(old) + 1))

        def tok(t):
            return slice(t * P, (t + 1) * P)

        xr = x.rearrange("b (t p) c -> b p t c", p=P)
        outr = out.rearrange("b (t p) c -> b p t c", p=P)

        @block.sync
        def _(sp):
            def load_front(n):
                wait(sp, xn_ready, n.at(QT, 0))
                sp.dma_start(xf[:], dram(xr, n)).then_inc(xf_loaded, 16)

            def dram(a, n):
                if n.pair is None:
                    return a[n.const]
                return a[bass.ds(n.pair * 2 + n.const, 1)].rearrange("o p t c -> p (o t) c")

            def load_back(n):
                wait(sp, x1_ready, n.at(1, 0))
                sp.dma_start(xb[:], dram(xr, n)).then_inc(xb_loaded, 16)

            def store(n):
                sp.wait_ge(ob_ready, n.at(1, 1))
                sp.dma_start(dram(outr, n), ob[:]).then_inc(stored, 16)

            sp.dma_start(wd_n[:, 0, :], w_q_down[0:P, :]).then_inc(wd_loaded, 16)
            sp.dma_start(wd_n[0:QB, 1, :], w_q_down[P:QC, :]).then_inc(wd_loaded, 16)
            sp.dma_start(wd_n[QB:P, 1, :], w_kv_down).then_inc(wd_loaded, 16)
            sp.dma_start(wd_n[0:ROPE, 2, :], w_k_rope).then_inc(wd_loaded, 16)
            load_front(Batch(0))
            sp.dma_start(wqn, w_q_nope.rearrange("(h p) c -> p h c", p=P)).then_inc(wq_loaded, 16)
            sp.dma_start(wkn, w_k_nope.rearrange("(h p) c -> p h c", p=P)).then_inc(wq_loaded, 16)
            sp.dma_start(wqr, w_q_rope.rearrange("(j p) c -> p j c", p=P)).then_inc(wq_loaded, 16)
            sp.dma_start(wo_n, w_o.rearrange("(m p) d -> p m d", p=P)).then_inc(wo_loaded, 16)
            sp.dma_start(wvn, w_v_up.rearrange("(h p) c -> p h c", p=P)).then_inc(wo_loaded, 16)
            sp.wait_ge(prep_filled, prep_at["n", 3] + 1)
            sp.wait_ge(prep_dve, 12)
            sp.dma_start(w_nat.rearrange("p (m f) -> p m f", m=CT),
                         up_kernel.rearrange("(m p) f -> p m f", p=P)).then_inc(up_loaded, 16)
            sp.wait_ge(prep_filled, prep_at["upT", 3] + 1)
            sp.dma_start(w_nat.rearrange("p (m d) -> p m d", m=FT),
                         down_kernel.rearrange("(m p) d -> p m d", p=P)).then_inc(dn_loaded, 16)

            def iteration(b, front, back):
                if front:
                    load_front(b.plus(1))
                if back:
                    load_back(b.plus(-1))
                    store(b.plus(-1))

            iteration(Batch(0), True, False)
            iteration(Batch(1), True, True)
            with sp.Fori(0, B // 2 - 2) as pair:
                iteration(Batch(2, pair), True, True)
                iteration(Batch(3, pair), True, True)
            iteration(Batch(B - 2), True, True)
            iteration(Batch(B - 1), False, True)
            load_back(Batch(B - 1))
            store(Batch(B - 1))
            sp.wait_ge(stored, 16 * B)

        @block.gpsimd
        def _(pool):
            pool.memset(ident[:], 0.0).then_inc(ident_zeroed, 1)
            pool.wait_ge(ident_zeroed, 1)
            pool.affine_select(out=ident[:], in_=ident[:], compare_op=ALU.not_equal, fill=1.0, base=0,
                               pattern=[[-1, P]], channel_multiplier=1).then_inc(ident_made, 1)
            for ap, v in ((ln_eps, LN_EPS), (rms_eps, RMS_EPS), (neg_half, -0.5), (plift, PLIFT)):
                pool.memset(ap, v).then_inc(consts_set, 1)
            for k in range(4):
                pool.wait_ge(max_asked, k + 1)
                pool.partition_all_reduce(mx[:, 2 * k + 8:2 * k + 10], mx[:, 2 * k:2 * k + 2], P,
                                          bass.bass_isa.ReduceOp.max).then_inc(max_given, 1)

            def ln(n, which):
                pool.wait_ge(ln_aggr[which], n.at(QT, QT))
                pool.tensor_tensor(va[:, which, :], mv[:, which, :, 1], ln_eps,
                                   ALU.add).then_inc(ln_eps_added[which], 1)
                pool.wait_ge(ln_eps_added[which], n.at(1, 1))
                pool.tensor_tensor(rstd[:, which, :], va[:, which, :], neg_half,
                                   ALU.pow).then_inc(ln_rstd[which], 1)

            def task(n, j):
                kind, k = j
                if kind == "ln1" or kind == "ln2":
                    if kind == "ln2":
                        pool.wait_ge(x1_ready, n.at(1, 1))
                        if not n.first():
                            pool.wait_ge(ob_ready, n.at(1, 0))
                        pool.tensor_tensor(x1b[:], x1[:], db[:].unsqueeze(1).to_broadcast([P, QT, HID]),
                                           ALU.add).then_inc(x1b_ready, 1)
                    ln(n, int(kind == "ln2"))
                elif kind == "D":
                    pool.wait_ge(front_act, n.at(NF, FRONT.index(j) + 1))
                    pool.tensor_tensor(sse[:, k, :], ssq[:, k, :], rms_eps, ALU.add).then_inc(rms_eps_added, 1)
                    pool.wait_ge(rms_eps_added, n.at(QT, k + 1))
                    pool.tensor_tensor(rms[:, k, :], sse[:, k, :], neg_half, ALU.pow).then_inc(rms_ready, 1)
                    r = raw[:, k, QC + KVC:DOWN]
                    pool.tensor_tensor(kr[:, 0, :], r, rope[:, k, 0, :], ALU.mult).then_inc(kr_parts, 1)
                    h = ROPE // 2
                    pool.tensor_tensor(kr[:, 1, 0:h], r[:, h:ROPE], rope[:, k, 1, 0:h],
                                       ALU.mult).then_inc(kr_parts, 1)
                    pool.tensor_tensor(kr[:, 1, h:ROPE], r[:, 0:h], rope[:, k, 1, h:ROPE],
                                       ALU.mult).then_inc(kr_parts, 1)
                    pool.wait_ge(kr_parts, n.at(3 * QT, 3 * k + 3))
                    pool.tensor_tensor(kt[:, k, KVC:HD], kr[:, 0, :], kr[:, 1, :],
                                       ALU.add).then_inc(kr_ready, 1)
                elif kind == "Q":
                    pool.wait_ge(qr_ready, n.at(8, k + 1))
                    pool.tensor_tensor(qtok[k % 4][:, :, KVC:HD], qr[k % 2][:, 0], qr[k % 2][:, 1],
                                       ALU.add).then_inc(qtok_ready, 1)
                elif kind == "up":
                    pool.wait_ge(back_act, n.at(NBA, BACK_ACT.index(j) + 1))
                    wait(pool, gz_ready, n.at(4, k))
                    pool.tensor_tensor(gv[:], gu[k % 2][:], gu[k % 2][:], ALU.mult).then_inc(gv_ready, 1)

            for s in SLOTS:
                for j in s[0] + s[1]:
                    if j[0] in FRONT_TASKS:
                        task(Batch(0), j)

            def iteration(b, front, back):
                for h in range(NH):
                    for part in SLOTS[h]:
                        for j in part:
                            if j[0] in FRONT_TASKS and front:
                                task(b.plus(1), j)
                            if j[0] in BACK_TASKS and back:
                                task(b.plus(-1), j)

            iteration(Batch(0), True, False)
            iteration(Batch(1), True, True)
            with pool.Fori(0, B // 2 - 2) as pair:
                iteration(Batch(2, pair), True, True)
                iteration(Batch(3, pair), True, True)
            iteration(Batch(B - 2), True, True)
            iteration(Batch(B - 1), False, True)
            for s in SLOTS:
                for j in s[0] + s[1]:
                    if j[0] in BACK_TASKS:
                        task(Batch(B - 1), j)

        @block.scalar
        def _(act):
            act.dma_start(rope[:], rope_table.rearrange("(t p) w c -> p t w c", p=P)).then_inc(vec_loaded, 16)
            act.dma_start(qn_a, q_norm_w[0:P].unsqueeze(1)).then_inc(vec_loaded, 16)
            act.dma_start(qn_b, q_norm_w[P:QC].unsqueeze(1)).then_inc(vec_loaded, 16)
            act.dma_start(kvn_c[0:KVC], kv_norm_w.unsqueeze(1)).then_inc(vec_loaded, 16)
            act.dma_start(kvn_c[KVC:P], kv_norm_w.unsqueeze(1)).then_inc(vec_loaded, 16)
            act.dma_start(kvn_r[:], kv_norm_w.unsqueeze(0).to_broadcast([P, KVC])).then_inc(vec_loaded, 16)
            act.dma_start(ub[:], up_bias.rearrange("(f p) -> p f", p=P), allow_slow_non_contiguous=True).then_inc(vec_loaded, 16)
            act.dma_start(db[:], down_bias.unsqueeze(0).to_broadcast([P, HID])).then_inc(vec_loaded, 16)
            act.wait_ge(ident_made, 1)
            act.activation(ident16[:], ident[:], ACT.Copy).then_inc(ident16_made, 1)

            for i, (kind, k, who) in enumerate(prep):
                if who != "act":
                    continue
                act.wait_ge(prep_filled, i + 1)
                src = bank[i % 8]
                if kind == "wd":
                    act.activation(wdT[:, k, :], src[:, 0:DOWN], ACT.Copy).then_inc(prep_act, 1)
                elif kind == "wo":
                    act.activation(woT[:, 2 * k:2 * k + 2, :].rearrange("p h c -> p (h c)"), src[:],
                                   ACT.Copy).then_inc(prep_act, 1)
                elif kind in ("upT", "dnT"):
                    if kind == "upT" and k == 0:
                        act.wait_ge(prep_dve, 12)
                    if kind == "dnT" and k == 0:
                        act.wait_ge(quantised, 1)
                    act.activation(w_T[:, 512 * k:512 * (k + 1)], src[:], ACT.Copy).then_inc(prep_act, 1)
                elif kind == "upB":
                    act.activation(up_q[:, k, :], src[:].bitcast(BF16), ACT.Copy).then_inc(prep_act, 1)
                else:
                    act.activation(dn_q[:, 4 * k:4 * k + 4, :].rearrange("p f d -> p (f d)"),
                                   src[:].bitcast(BF16), ACT.Copy).then_inc(prep_act, 1)

            def task(n, j):
                kind, k = j
                if kind in ("xT", "D", "KT", "cT", "Q", "QT"):
                    src = front_bank(n, j)
                    act.wait_ge(front_filled, n.at(NF, FRONT.index(j) + 1))
                    if kind == "xT":
                        act.activation(xT[:], src[:].rearrange("p (m s) -> p m s", m=CT),
                                       ACT.Copy).then_inc(front_act, 1)
                    elif kind == "D":
                        act.activation(sq[:, k, 0:QC], src[:, 0:QC], ACT.Square, scale=QC ** -0.5,
                                       accum_out=ssq[:, k, 0:1])
                        act.activation(sq[:, k, QC:QC + KVC], src[:, QC:QC + KVC], ACT.Square, scale=KVC ** -0.5,
                                       accum_out=ssq[:, k, 1:2])
                        act.activation(raw[:, k, :], src[:, 0:DOWN], ACT.Copy).then_inc(front_act, 1)
                    elif kind == "KT":
                        act.activation(k_hi[n.parity][:], src[:, 0:S], ACT.Copy,
                                       scale=UP).then_inc(front_act, 1)
                    elif kind == "cT":
                        act.activation(ca_hi[:], src[:, 0:S], ACT.Copy, scale=UP)
                        act.activation(cb[0:QB, :], src[0:QB, S:2 * S], ACT.Copy,
                                       scale=UP).then_inc(front_act, 1)
                    elif kind == "Q":
                        act.activation(qtok[k % 4][:, :, 0:KVC],
                                       src[:].rearrange("p (h c) -> p h c", h=QUAD)[:, :, 0:KVC],
                                       ACT.Copy).then_inc(front_act, 1)
                    else:
                        g, t = k // 2, k % 2
                        act.activation(q_hi[n.parity][:, QUAD * g:QUAD * g + QUAD, tok(t)],
                                       src[:].rearrange("p (h s) -> p h s", h=QUAD),
                                       ACT.Copy, scale=1.0 / UP).then_inc(front_act, 1)
                elif kind in ("OT", "x2T", "up"):
                    act.wait_ge(back_filled, n.at(NB_, BACK.index(j) + 1))
                    if kind == "OT":
                        t, half = k % 2, k // 2
                        act.activation(ot_hi[:, 4 * half:4 * half + 4, tok(t)],
                                       b_bank[:].rearrange("p (j s) -> p j s", j=4),
                                       ACT.Copy).then_inc(back_act, 1)
                    elif kind == "x2T":
                        act.activation(x2_hi[:], b_bank[:].rearrange("p (m s) -> p m s", m=CT), ACT.Copy,
                                       scale=UP).then_inc(back_act, 1)
                    else:
                        if k >= 2:
                            act.wait_ge(g_ready, n.at(4, k - 1))
                        for i in range(2):
                            last = act.activation(gu[k % 2][:, i, :], b_bank[:, S * i:S * (i + 1)],
                                                  ACT.Identity, scale=1.0 / UP,
                                                  bias=ub[:, 2 * k + i:2 * k + i + 1])
                        last.then_inc(back_act, 1)
                elif kind == "gelu":
                    act.wait_ge(gz_ready, n.at(4, k + 1))
                    wait(act, g_ready, n.at(4, k))
                    act.activation(gt[:], gz[:], ACT.Tanh, scale=GELU_C * GELU_A).then_inc(gt_ready, 1)

            def exps(n, h):
                act.wait_ge(bias_ready, n.at(NH, h + 1))
                wait(act, probsT_ready, n.at(NH, h - 1))
                for t in range(QT):
                    last = act.activation(pr[h % 2][:, t, :], l_bank[h % 2][:, S * t:S * (t + 1)], ACT.Exp,
                                          scale=inv_s, bias=ebias[:, h % 2, t:t + 1],
                                          accum_out=rsum[:, h, t:t + 1])
                last.then_inc(probs_ready, 1)

            def pt_high(n, h):
                act.wait_ge(probsT_ready, n.at(NH, h + 1))
                wait(act, pv_done, n.at(NH, h - 1))
                act.activation(pt_hi[h % 2][:].rearrange("p k s -> p (k s)"), t_bank[h % 2][:],
                               ACT.Copy).then_inc(pt_hi_ready, 1)

            for j in FRONT:
                task(Batch(0), j)
            exps(Batch(0), 0)

            def iteration(b, front, back):
                for h in range(NH):
                    pt_high(b, h)
                    if h + 1 < NH or front:
                        exps(b, h + 1) if h + 1 < NH else exps(b.plus(1), 0)
                    for part in SLOTS[h]:
                        for j in part:
                            if j[0] in FRONT_TASKS and front:
                                task(b.plus(1), j)
                            if j[0] in BACK_TASKS and back:
                                task(b.plus(-1), j)

            iteration(Batch(0), True, False)
            iteration(Batch(1), True, True)
            with act.Fori(0, B // 2 - 2) as pair:
                iteration(Batch(2, pair), True, True)
                iteration(Batch(3, pair), True, True)
            iteration(Batch(B - 2), True, True)
            iteration(Batch(B - 1), False, True)
            for s in SLOTS:
                for j in s[0] + s[1]:
                    if j[0] in BACK_TASKS:
                        task(Batch(B - 1), j)

        @block.vector
        def _(dve):
            steps = [0]

            def step(ins):
                steps[0] += 1
                ins.then_inc(prep_step, 1)
                dve.wait_ge(prep_step, steps[0])

            def over_partitions(k, *cols):
                step(dve.tensor_scalar(mx[:, 2 * k:2 * k + 2], mx[:, 2 * k:2 * k + 2], 1e-30, None, ALU.max))
                dve.sem_inc(max_asked, 1)
                dve.wait_ge(max_given, k + 1)
                return mx[:, 2 * k + 8:2 * k + 9], mx[:, 2 * k + 9:2 * k + 10]

            def power(ap):
                step(dve.tensor_scalar(ap.bitcast(I32), ap.bitcast(I32), 0x7F800000, None, ALU.bitwise_and))

            def scale_of(m, s, inv, top):
                power(m)
                step(dve.reciprocal(s, m))
                step(dve.tensor_scalar(s, s, top, None, ALU.mult))
                step(dve.tensor_scalar(inv, m, 1.0 / top, None, ALU.mult))

            step(dve.memset(mx[:], 0.0))
            dve.wait_ge(consts_set, 4)
            dve.wait_ge(vec_loaded, 16 * 8)
            dve.wait_ge(wd_loaded, 16 * 4)
            step(dve.tensor_reduce(mx[0:ROPE, 0:1], wd_n[0:ROPE, 2, :], AX.X, ALU.max,
                                   apply_absolute_value=True))
            m, _m = over_partitions(0)
            scale_of(m, small[:, 32:33], inv_kr, 1.0)
            step(dve.tensor_scalar(wd_n[0:ROPE, 2, :], wd_n[0:ROPE, 2, :], small[0:ROPE, 32:33], None,
                                   ALU.mult))
            dve.sem_inc(kr_scaled, 1)
            for q, s, r in ((qn_a, qs_a, qr_a), (qn_b, qs_b, qr_b)):
                step(dve.tensor_scalar(s, q, SCALE, None, ALU.mult))
                step(dve.tensor_scalar(r, s, inv_kr[0:q.shape[0]], None, ALU.mult))

            def read_out(names):
                for i, (kind, k, who) in enumerate(prep):
                    if who != "dve" or kind not in names:
                        continue
                    dve.wait_ge(prep_filled, i + 1)
                    src = bank[i % 8]
                    hs = slice(8 * k, 8 * k + 8)
                    if kind in ("ma", "mb"):
                        rows, s, dst = (P, qs_a, wf_a) if kind == "ma" else (QB, qs_b, wf_b)
                        ins = dve.scalar_tensor_tensor(
                            out=dst[0:rows, hs, 0:KVC], in0=src[0:rows].rearrange("p (h c) -> p h c", h=8),
                            scalar=s, in1=kvn_r[0:rows].unsqueeze(1).to_broadcast([rows, 8, KVC]),
                            op0=ALU.mult, op1=ALU.mult)
                    elif kind in ("ra", "rb"):
                        rows, s, dst = (P, qr_a, wf_a) if kind == "ra" else (QB, qr_b, wf_b)
                        ins = dve.tensor_scalar(dst[0:rows, hs, KVC:HD],
                                                src[0:rows].rearrange("p (h c) -> p h c", h=8), s, None,
                                                ALU.mult)
                    else:
                        ins = dve.tensor_scalar(nf[:, 2 * k:2 * k + 2, :].rearrange("p j c -> p (j c)"),
                                                src[:], kvn_c, None, ALU.mult)
                    ins.then_inc(prep_dve, 1)

            read_out(("ma", "mb", "ra", "rb"))
            dve.wait_ge(prep_dve, 8)
            step(dve.tensor_reduce(mx[:, 2:3], wf_a[:].rearrange("p h c -> p (h c)"), AX.X, ALU.max,
                                   apply_absolute_value=True))
            step(dve.tensor_reduce(mx[0:QB, 3:4], wf_b[0:QB].rearrange("p h c -> p (h c)"), AX.X, ALU.max,
                                   apply_absolute_value=True))
            m, m2 = over_partitions(1)
            step(dve.tensor_tensor(m, m, m2, ALU.max))
            s_w = small[:, 33:34]
            scale_of(m, s_w, inv_s, WMAX)
            step(dve.tensor_scalar(inv_s, inv_s, 1.0 / UP, None, ALU.mult))
            fa = wf_a.rearrange("p h c -> p (h c)")
            fb = wf_b.rearrange("p h c -> p (h c)")[0:QB]
            dve.tensor_scalar(wb_hh[QB:P, :], fb, s_w[0:QB], None, ALU.mult)
            dve.tensor_scalar(wb_hh[0:QB, :], fb, s_w[0:QB], None, ALU.mult)
            step(dve.tensor_scalar(wa_hi[:], fa, s_w, None, ALU.mult))
            dve.scalar_tensor_tensor(out=wb_lo[:], in0=fb, scalar=s_w[0:QB], in1=wb_hh[0:QB, :],
                                     op0=ALU.mult, op1=ALU.subtract)
            step(dve.scalar_tensor_tensor(out=wa_lo[:], in0=fa, scalar=s_w, in1=wa_hi[:],
                                          op0=ALU.mult, op1=ALU.subtract))
            read_out(("n",))
            dve.wait_ge(prep_dve, 12)
            nfl = nf.rearrange("p j c -> p (j c)")
            step(dve.tensor_reduce(mx[:, 4:5], nfl, AX.X, ALU.max, apply_absolute_value=True))
            m, _m = over_partitions(2)
            s_n = small[:, 34:35]
            scale_of(m, s_n, inv_n, WMAX)
            step(dve.tensor_scalar(inv_n, inv_n, 1.0 / UP, None, ALU.mult))
            nh, nl = (a[:].rearrange("p j c -> p (j c)") for a in (n_hi, n_lo))
            step(dve.tensor_scalar(nh, nfl, s_n, None, ALU.mult))
            step(dve.scalar_tensor_tensor(out=nl, in0=nfl, scalar=s_n, in1=nh, op0=ALU.mult,
                                          op1=ALU.subtract))

            def quantise(with_max):
                b3 = w_T.rearrange("p (n e) -> p n e", e=BLOCK)

                def spread(v):
                    return v.unsqueeze(2).to_broadcast([P, 2048 // BLOCK, BLOCK])

                amax, sc, inv, half = (blk[:, i, :] for i in range(4))
                step(dve.tensor_reduce(amax, b3, AX.X, ALU.max, apply_absolute_value=True))
                if with_max:
                    step(dve.tensor_reduce(mx[:, 6:7], amax, AX.X, ALU.max))
                step(dve.tensor_scalar(sc, amax, 1e-30, None, ALU.max))
                power(sc)
                step(dve.tensor_scalar(sc, sc, 0.25, None, ALU.mult))
                step(dve.reciprocal(inv, sc))
                step(dve.tensor_scalar(half, sc, 0.5, None, ALU.mult))
                x3 = w_x.rearrange("p (n e) -> p n e", e=BLOCK)
                step(dve.tensor_tensor(x3, b3, spread(inv), ALU.mult))
                step(dve.tensor_scalar(w_x.bitcast(I32), w_x.bitcast(I32), 0x7FFFFFFF, None,
                                       ALU.bitwise_and))
                step(dve.tensor_scalar(w_c, w_x, 5.0, 2.0, ALU.is_ge, ALU.mult))
                for mid in (3.5, 2.5):
                    step(dve.scalar_tensor_tensor(out=w_c, in0=w_x, scalar=mid, in1=w_c, op0=ALU.is_ge,
                                                  op1=ALU.add))
                step(dve.tensor_scalar(w_c, w_c, 2.0, None, ALU.mult))
                for mid in (1.75, 1.25, 0.75, 0.25):
                    step(dve.scalar_tensor_tensor(out=w_c, in0=w_x, scalar=mid, in1=w_c, op0=ALU.is_ge,
                                                  op1=ALU.add))
                step(dve.tensor_tensor(x3, w_c.rearrange("p (n e) -> p n e", e=BLOCK), spread(half), ALU.mult))
                step(dve.tensor_scalar(w_c.bitcast(I32), w_T.bitcast(I32), -0x80000000, None,
                                       ALU.bitwise_and))
                step(dve.tensor_tensor(w_c.bitcast(I32), w_c.bitcast(I32), w_x.bitcast(I32),
                                       ALU.bitwise_or))
                step(dve.tensor_copy(w_16[:], w_c))
                dve.sem_inc(quantised, 1)

            dve.wait_ge(prep_act, 2 + 8 + 4)
            quantise(True)
            step(dve.tensor_reduce(mx[:, 7:8], ub[:], AX.X, ALU.max, apply_absolute_value=True))
            m, m2 = over_partitions(3)
            step(dve.tensor_scalar(m, m, 2 * 1.5 * HID, None, ALU.mult))
            step(dve.tensor_scalar(m2, m2, 2.0, None, ALU.mult))
            step(dve.tensor_tensor(m, m, m2, ALU.add))
            scale_of(m, s_g, inv_g, 2.0 ** 14)
            step(dve.tensor_scalar(inv_g, inv_g, 0.5, None, ALU.mult))
            dve.wait_ge(prep_act, 2 + 8 + 4 + 2 + 4)
            quantise(False)

            def ln(n, which, src):
                for t in range(QT):
                    dve.bn_stats(st[:, which, t, :], src[:, t, :]).then_inc(ln_stats[which], 1)
                dve.wait_ge(ln_stats[which], n.at(QT, QT))
                dve.memset(nothing[:], 0.0)
                for t in range(QT):
                    dve.bn_aggr(mv[:, which, t, :], st[:, which, t, :]).then_inc(ln_aggr[which], 1)

            def ln_apply(n, which, src, dst, ready):
                dve.wait_ge(ln_rstd[which], n.at(1, 1))
                for t in range(QT):
                    dve.tensor_scalar(dst[:, t, :], src[:, t, :], mv[:, which, t, 0:1],
                                      rstd[:, which, t:t + 1], ALU.subtract, ALU.mult).then_inc(ready, 1)

            def low(dst, src, high, factor):
                return dve.scalar_tensor_tensor(out=dst, in0=src, scalar=factor, in1=high, op0=ALU.mult,
                                                op1=ALU.subtract)

            def task(n, j):
                kind, k = j
                if kind == "ln1":
                    dve.wait_ge(xf_loaded, n.at(16, 16))
                    ln(n, 0, xf)
                elif kind == "ln1x":
                    ln_apply(n, 0, xf, xn, xn_ready)
                elif kind in ("KT", "cT", "Q", "QT"):
                    dve.wait_ge(front_act, n.at(NF, FRONT.index(j) + 1))
                    src = front_bank(n, j)
                    if kind == "KT":
                        low(k_lo[n.parity][:], src[:, 0:S], k_hi[n.parity][:], UP).then_inc(front_dve, 1)
                    elif kind == "cT":
                        low(cb[QB:P, :], src[0:QB, S:2 * S], cb[0:QB, :], UP)
                        low(ca_lo[:], src[:, 0:S], ca_hi[:], UP).then_inc(front_dve, 1)
                    elif kind == "Q":
                        t, hf = k % 2, ROPE // 2
                        q = src[:].rearrange("p (h c) -> p h c", h=QUAD)[:, :, KVC:HD]
                        if not (n.first() and k < 2):
                            dve.wait_ge(qtok_ready, n.at(8, k - 1))
                        cos, sin = rope[:, t, 0, :], rope[:, t, 1, :]
                        dve.tensor_tensor(qr[k % 2][:, 0], q,
                                          cos.unsqueeze(1).to_broadcast([P, QUAD, ROPE]), ALU.mult)
                        dve.tensor_tensor(qr[k % 2][:, 1, :, 0:hf], q[:, :, hf:ROPE],
                                          sin[:, 0:hf].unsqueeze(1).to_broadcast([P, QUAD, hf]), ALU.mult)
                        dve.tensor_tensor(qr[k % 2][:, 1, :, hf:ROPE], q[:, :, 0:hf],
                                          sin[:, hf:ROPE].unsqueeze(1).to_broadcast([P, QUAD, hf]),
                                          ALU.mult).then_inc(qr_ready, 1)
                        dve.wait_ge(qr_ready, n.at(8, k + 1))
                        dve.sem_inc(front_dve, 1)
                    else:
                        g, t = k // 2, k % 2
                        low(q_lo[n.parity][:, QUAD * g:QUAD * g + QUAD, tok(t)],
                            src[:].rearrange("p (h s) -> p h s", h=QUAD),
                            q_hi[n.parity][:, QUAD * g:QUAD * g + QUAD, tok(t)],
                            1.0 / UP).then_inc(front_dve, 1)
                elif kind == "scale":
                    dve.wait_ge(rms_ready, n.at(QT, k + 1))
                    dve.tensor_scalar(cq[:, k, :], raw[:, k, 0:QC], rms[:, k, 0:1], None,
                                      ALU.mult)
                    dve.tensor_scalar(kt[:, k, 0:KVC], raw[:, k, QC:QC + KVC], rms[:, k, 1:2], None,
                                      ALU.mult).then_inc(latents_ready, 1)
                    dve.wait_ge(latents_ready, n.at(QT, k + 1))
                    dve.tensor_scalar(c_hi[n.parity][:, k, :], kt[:, k, 0:KVC], UP, None,
                                      ALU.mult).then_inc(c_hi_ready, 1)
                    dve.wait_ge(c_hi_ready, n.at(QT, k + 1))
                    low(c_lo[n.parity][:, k, :], kt[:, k, 0:KVC], c_hi[n.parity][:, k, :],
                        UP).then_inc(c_ready, 1)
                elif kind == "OT":
                    t, half = k % 2, k // 2
                    dve.wait_ge(back_act, n.at(NBA, BACK_ACT.index(j) + 1))
                    hs = slice(4 * half, 4 * half + 4)
                    low(ot_lo[:, hs, tok(t)], b_bank[:].rearrange("p (j s) -> p j s", j=4),
                        ot_hi[:, hs, tok(t)], 1.0).then_inc(back_dve, 1)
                elif kind == "proj":
                    dve.wait_ge(back_filled, n.at(NB_, BACK.index(j) + 1))
                    dve.wait_ge(xb_loaded, n.at(16, 16))
                    dve.scalar_tensor_tensor(out=x1[:], in0=b_bank[:].rearrange("p (t c) -> p t c", t=QT),
                                             scalar=inv_n, in1=xb[:], op0=ALU.mult,
                                             op1=ALU.add).then_inc(x1_ready, 1)
                    dve.wait_ge(x1_ready, n.at(1, 1))
                    dve.sem_inc(back_dve, 1)
                    ln(n, 1, x1)
                elif kind == "ln2":
                    ln_apply(n, 1, x1, x2n, x2n_ready)
                elif kind == "x2T":
                    dve.wait_ge(back_act, n.at(NBA, BACK_ACT.index(j) + 1))
                    low(x2_lo[:], b_bank[:].rearrange("p (m s) -> p m s", m=CT), x2_hi[:],
                        UP).then_inc(back_dve, 1)
                elif kind == "up":
                    dve.wait_ge(gv_ready, n.at(4, k + 1))
                    wait(dve, gt_ready, n.at(4, k))
                    dve.scalar_tensor_tensor(out=gz[:], in0=gv[:], scalar=1.0 / GELU_A, in1=gu[k % 2][:],
                                             op0=ALU.add, op1=ALU.mult).then_inc(gz_ready, 1)
                elif kind == "split":
                    dve.wait_ge(gt_ready, n.at(4, k + 1))
                    dve.scalar_tensor_tensor(out=gt[:], in0=gt[:], scalar=1.0, in1=gu[k % 2][:],
                                             op0=ALU.add, op1=ALU.mult).then_inc(g_raw, 1)
                    dve.wait_ge(g_raw, n.at(4, k + 1))
                    dve.tensor_scalar(g_hi[:, 2 * k:2 * k + 2, :], gt[:], s_g, None,
                                      ALU.mult).then_inc(g_hi_ready, 1)
                    dve.wait_ge(g_hi_ready, n.at(4, k + 1))
                    low(g_lo[:, 2 * k:2 * k + 2, :], gt[:], g_hi[:, 2 * k:2 * k + 2, :],
                        s_g).then_inc(g_ready, 1)
                elif kind == "down":
                    dve.wait_ge(back_filled, n.at(NB_, BACK.index(j) + 1))
                    dve.wait_ge(x1b_ready, n.at(1, 1))
                    wait(dve, stored, n.at(16, 0))
                    dve.scalar_tensor_tensor(out=ob[:], in0=b_bank[:].rearrange("p (t c) -> p t c", t=QT),
                                             scalar=inv_g, in1=x1b[:], op0=ALU.mult,
                                             op1=ALU.add).then_inc(ob_ready, 1)
                    dve.wait_ge(ob_ready, n.at(1, 1))
                    dve.sem_inc(back_dve, 1)

            def maxes(n, h):
                dve.wait_ge(logits_ready, n.at(NH, h + 1))
                dve.tensor_reduce(nmax[:, h % 2, :], l_bank[h % 2][:].rearrange("p (t s) -> p t s", t=QT),
                                  AX.X, ALU.max, negate=True).then_inc(max_found, 1)
                dve.wait_ge(max_found, n.at(NH, h + 1))
                dve.tensor_scalar(ebias[:, h % 2, :], nmax[:, h % 2, :], inv_s, PLIFT, ALU.mult,
                                  ALU.add).then_inc(bias_ready, 1)

            def pt_low(n, h):
                dve.wait_ge(pt_hi_ready, n.at(NH, h + 1))
                low(pt_lo[h % 2][:].rearrange("p k s -> p (k s)"), t_bank[h % 2][:],
                    pt_hi[h % 2][:].rearrange("p k s -> p (k s)"), 1.0).then_inc(pt_lo_ready, 1)

            def normalise(n, g):
                hs = slice(QUAD * g, QUAD * g + QUAD)
                dve.wait_ge(pv_done, n.at(NH, QUAD * g + QUAD))
                if g == 0 and not n.first():
                    dve.wait_ge(back_filled, n.at(NB_, 4 - NB_))
                dve.reciprocal(rinv[:, hs, :], rsum[:, hs, :]).then_inc(rinv_ready, 1)
                dve.wait_ge(rinv_ready, n.at(NQ, g + 1))
                dve.tensor_tensor(otok[:, :, hs, :].rearrange("p t h c -> p h t c"),
                                  o_bank[:].rearrange("p (h t c) -> p h t c", h=QUAD, t=QT),
                                  rinv[:, hs, :].unsqueeze(3).to_broadcast([P, QUAD, QT, KVC]),
                                  ALU.mult).then_inc(o_ready, 1)

            for s in SLOTS:
                for j in s[0] + s[1]:
                    if j[0] in FRONT_TASKS:
                        task(Batch(0), j)
            maxes(Batch(0), 0)

            def iteration(b, front, back):
                for h in range(NH):
                    if h + 1 < NH or front:
                        maxes(b, h + 1) if h + 1 < NH else maxes(b.plus(1), 0)
                    pt_low(b, h)
                    if h == 0 and back:
                        normalise(b.plus(-1), NQ - 1)
                    if h % QUAD == 0 and h:
                        normalise(b, h // QUAD - 1)
                    for part in SLOTS[h]:
                        for j in part:
                            if j[0] in FRONT_TASKS and front:
                                task(b.plus(1), j)
                            if j[0] in BACK_TASKS and back:
                                task(b.plus(-1), j)

            iteration(Batch(0), True, False)
            iteration(Batch(1), True, True)
            with dve.Fori(0, B // 2 - 2) as pair:
                iteration(Batch(2, pair), True, True)
                iteration(Batch(3, pair), True, True)
            iteration(Batch(B - 2), True, True)
            iteration(Batch(B - 1), False, True)
            normalise(Batch(B - 1), NQ - 1)
            for s in SLOTS:
                for j in s[0] + s[1]:
                    if j[0] in BACK_TASKS:
                        task(Batch(B - 1), j)

        @block.tensor
        def _(pe):
            def pairs(out_, terms):
                for i, (a, b) in enumerate(terms):
                    last = pe.matmul(out_, a, b, start=(i == 0), stop=(i == len(terms) - 1))
                return last

            pe.wait_ge(ident_made, 1)
            pe.wait_ge(ident16_made, 1)
            for i, (kind, k, who) in enumerate(prep):
                if i >= 8:
                    pe.wait_ge(prep_act if prep[i - 8][2] == "act" else prep_dve, prep_count(i - 8))
                dst = bank[i % 8]
                if kind == "wd":
                    if k == 0:
                        pe.wait_ge(wd_loaded, 16 * 4)
                        pe.wait_ge(kr_scaled, 1)
                    for r, rows in enumerate((P, P, ROPE)):
                        last = pe.transpose(dst[:, P * r:P * r + rows], wd_n[0:rows, r, tok(k)],
                                            ident[0:rows, 0:rows])
                elif kind in ("ma", "mb"):
                    pe.wait_ge(wq_loaded, 16 * 3)
                    rows, cols = (P, slice(0, P)) if kind == "ma" else (QB, slice(P, QC))
                    for h in range(8):
                        last = pe.matmul(dst[0:rows, KVC * h:KVC * (h + 1)], wqn[:, 8 * k + h, cols],
                                         wkn[:, 8 * k + h, :], start=True, stop=True)
                elif kind in ("ra", "rb"):
                    rows, cols = (P, slice(0, P)) if kind == "ra" else (QB, slice(P, QC))
                    for j in range(4):
                        last = pe.transpose(dst[0:rows, P * j:P * (j + 1)], wqr[:, 4 * k + j, cols], ident[:])
                elif kind == "wo":
                    pe.wait_ge(wo_loaded, 16 * 2)
                    for h in range(2):
                        for m in range(CT):
                            last = pe.transpose(dst[:, HID * h + P * m:HID * h + P * (m + 1)],
                                                wo_n[:, m, P * (2 * k + h):P * (2 * k + h + 1)], ident[:])
                elif kind == "n":
                    if k == 0:
                        pe.wait_ge(prep_act, 2 + 8)
                    for j in range(2):
                        for odd in range(2):
                            h = 2 * (2 * k + j) + odd
                            last = pe.matmul(dst[KVC * odd:KVC * (odd + 1), HID * j:HID * (j + 1)],
                                             wvn[:, h, :], woT[:, h, :], start=True, stop=True)
                elif kind == "upT":
                    pe.wait_ge(up_loaded, 16)
                    for f in range(2):
                        for m in range(CT):
                            at = FF * m + P * (2 * k + f)
                            last = pe.transpose(dst[:, HID * f + P * m:HID * f + P * (m + 1)],
                                                w_nat[:, at:at + P], ident[:])
                elif kind == "upB":
                    pe.wait_ge(quantised, 1)
                    for f in range(FT):
                        at = HID * f + P * k
                        last = pe.transpose(dst[:].bitcast(BF16)[:, P * f:P * (f + 1)], w_16[:, at:at + P],
                                            ident16[:])
                elif kind == "dnT":
                    pe.wait_ge(dn_loaded, 16)
                    for f in range(4):
                        at = HID * (4 * (k % 2) + f) + P * (k // 2)
                        last = pe.transpose(dst[:, P * f:P * (f + 1)], w_nat[:, at:at + P], ident[:])
                else:
                    pe.wait_ge(quantised, 2)
                    for f in range(4):
                        for d in range(CT):
                            at = FF * d + P * (4 * k + f)
                            to = HID * f + P * d
                            last = pe.transpose(dst[:].bitcast(BF16)[:, to:to + P], w_16[:, at:at + P],
                                                ident16[:])
                last.then_inc(prep_filled, 1)
            pe.wait_ge(prep_act, sum(j[2] == "act" for j in prep))

            def job(n, j):
                kind, k = j
                if j in FRONT:
                    free_front(pe, n, j)
                    dst = front_bank(n, j)
                    if kind == "xT":
                        pe.wait_ge(xn_ready, n.at(QT, QT))
                        for t in range(QT):
                            for m in range(CT):
                                last = pe.transpose(dst[:, S * m + P * t:S * m + P * (t + 1)],
                                                    xn[:, t, tok(m)], ident[:])
                    elif kind == "D":
                        pe.wait_ge(front_act, n.at(NF, 1))
                        last = pairs(dst[:, 0:DOWN], [(xT[:, m, tok(k)], wdT[:, m, :]) for m in range(CT)])
                    elif kind == "KT":
                        pe.wait_ge(latents_ready, n.at(QT, QT))
                        pe.wait_ge(kr_ready, n.at(QT, QT))
                        for t in range(QT):
                            last = pe.transpose(dst[:, tok(t)], kt[:, t, :], ident[:])
                    elif kind == "cT":
                        for t in range(QT):
                            pe.transpose(dst[:, tok(t)], cq[:, t, 0:P], ident[:])
                            last = pe.transpose(dst[0:QB, S + P * t:S + P * (t + 1)], cq[:, t, P:QC], ident[:])
                    elif kind == "Q":
                        g, t = k // 2, k % 2
                        if k == 0:
                            pe.wait_ge(front_dve, n.at(NFD, FRONT_DVE.index(("cT", 0)) + 1))
                        cols = slice(512 * g, 512 * (g + 1))
                        last = pairs(dst[:], [(ca_hi[:, tok(t)], wa_hi[:, cols]),
                                              (ca_hi[:, tok(t)], wa_lo[:, cols]),
                                              (ca_lo[:, tok(t)], wa_hi[:, cols]),
                                              (cb[:, tok(t)], wb_hh[:, cols]),
                                              (cb[0:QB, tok(t)], wb_lo[:, cols])])
                    else:
                        pe.wait_ge(qtok_ready, n.at(8, k + 1))
                        for h in range(QUAD):
                            last = pe.transpose(dst[:, tok(h)], qtok[k % 4][:, h, :], ident[:])
                    last.then_inc(front_filled, 1)
                else:
                    free_back(pe, n, j)
                    if kind == "OT":
                        t, half = k % 2, k // 2
                        if t == 0:
                            pe.wait_ge(o_ready, n.at(NQ, 2 * half + 2))
                        for i in range(4):
                            h = 8 * half + 2 * i
                            last = pe.transpose(b_bank[:, tok(i)],
                                                otok[:, t, h:h + 2, :].rearrange("p h c -> p (h c)"), ident[:])
                    elif kind == "proj":
                        for t in range(QT):
                            last = pairs(b_bank[:, HID * t:HID * (t + 1)],
                                         [(a[:, i, tok(t)], w[:, i, :]) for i in range(PAIRS)
                                          for a, w in ((ot_hi, n_hi), (ot_hi, n_lo), (ot_lo, n_hi))])
                    elif kind == "x2T":
                        pe.wait_ge(x2n_ready, n.at(QT, QT))
                        for t in range(QT):
                            for m in range(CT):
                                last = pe.transpose(b_bank[:, S * m + P * t:S * m + P * (t + 1)],
                                                    x2n[:, t, tok(m)], ident[:])
                    elif kind == "up":
                        for i in range(2):
                            f = 2 * k + i
                            last = pairs(b_bank[:, S * i:S * (i + 1)],
                                         [(up_q[:, m, tok(f)], a[:, m, :]) for m in range(CT)
                                          for a in (x2_hi, x2_lo)])
                    else:
                        pe.wait_ge(g_ready, n.at(4, 4))
                        for t in range(QT):
                            last = pairs(b_bank[:, HID * t:HID * (t + 1)],
                                         [(a[:, f, tok(t)], dn_q[:, f, :]) for f in range(FT)
                                          for a in (g_hi, g_lo)])
                    last.then_inc(back_filled, 1)

            def logits(n, h):
                if h % QUAD == 0:
                    pe.wait_ge(front_dve, n.at(NFD, FRONT_DVE.index(("QT", 2 * (h // QUAD) + 1)) + 1))
                wait(pe, probs_ready, n.at(NH, h - 1))
                p = n.parity
                for t in range(QT):
                    last = pairs(l_bank[h % 2][:, S * t:S * (t + 1)],
                                 [(q_hi[p][:, h, tok(t)], k_hi[p][:]), (q_hi[p][:, h, tok(t)], k_lo[p][:]),
                                  (q_lo[p][:, h, tok(t)], k_hi[p][:])])
                last.then_inc(logits_ready, 1)

            def transpose_probs(n, h):
                pe.wait_ge(probs_ready, n.at(NH, h + 1))
                wait(pe, pt_lo_ready, n.at(NH, h - 1))
                for t in range(QT):
                    for k in range(QT):
                        last = pe.transpose(t_bank[h % 2][:, S * k + P * t:S * k + P * (t + 1)],
                                            pr[h % 2][:, t, tok(k)], ident[:])
                last.then_inc(probsT_ready, 1)

            def values(n, h):
                pe.wait_ge(pt_lo_ready, n.at(NH, h + 1))
                if h == 0:
                    pe.wait_ge(c_ready, n.at(QT, QT))
                if h % QUAD == 0:
                    wait(pe, o_ready, n.at(NQ, h // QUAD))
                p = n.parity
                for t in range(QT):
                    at = KVC * (2 * (h % QUAD) + t)
                    last = pairs(o_bank[:, at:at + KVC],
                                 [(w[h % 2][:, k, tok(t)], c[p][:, k, :]) for k in range(QT)
                                  for w, c in ((pt_hi, c_hi), (pt_hi, c_lo), (pt_lo, c_hi))])
                last.then_inc(pv_done, 1)

            for j in FRONT:
                job(Batch(0), j)
            logits(Batch(0), 0)

            def iteration(b, front, back):
                for h in range(NH):
                    if h + 1 < NH or front:
                        logits(b, h + 1) if h + 1 < NH else logits(b.plus(1), 0)
                    transpose_probs(b, h)
                    for i, part in enumerate(SLOTS[h]):
                        for j in part:
                            if j in FRONT and front:
                                job(b.plus(1), j)
                            if j in BACK and back:
                                job(b.plus(-1), j)
                        if i == 0 and (h or back):
                            values(b, h - 1) if h else values(b.plus(-1), NH - 1)

            iteration(Batch(0), True, False)
            iteration(Batch(1), True, True)
            with pe.Fori(0, B // 2 - 2) as pair:
                iteration(Batch(2, pair), True, True)
                iteration(Batch(3, pair), True, True)
            iteration(Batch(B - 2), True, True)
            iteration(Batch(B - 1), False, True)
            values(Batch(B - 1), NH - 1)
            for j in BACK:
                job(Batch(B - 1), j)


_NAMES = ["L0_attn_x", "L0_attn_w_q_down", "L0_attn_q_norm_w", "L0_attn_w_q_nope", "L0_attn_w_q_rope",
          "L0_attn_w_kv_down", "L0_attn_kv_norm_w", "L0_attn_w_k_nope", "L0_attn_w_v_up", "L0_attn_w_k_rope",
          "L0_attn_w_o", "L0_ffn_up_kernel", "L0_ffn_up_bias", "L0_ffn_down_kernel", "L0_ffn_down_bias"]


def _rope_table():
    import numpy as np
    inv = (np.float32(1.0) / np.power(np.float32(10000.0), np.arange(0, ROPE, 2, dtype=np.float32)
                                      / np.float32(ROPE))).astype(np.float32)
    f = np.arange(S, dtype=np.float32)[:, None] * inv[None, :]
    c, s = np.cos(f).astype(np.float32), np.sin(f).astype(np.float32)
    return np.stack([np.concatenate([c, c], 1), np.concatenate([-s, s], 1)], 1)


def kernel(**inputs):
    import numpy as np
    import concourse.bacc as bacc
    from concourse.bass_utils import run_bass_kernel_spmd

    nc = bacc.Bacc("TRN2", target_bir_lowering=False, num_devices=1)
    arrays, args = {}, []
    for name in _NAMES:
        a = np.ascontiguousarray(inputs[name])
        arrays[name + "_in"] = a
        args.append(nc.dram_tensor(name + "_in", a.shape, mybir.dt.from_np(a.dtype), kind="ExternalInput").ap())
    table = _rope_table()
    arrays["rope_table"] = table
    args.append(nc.dram_tensor("rope_table", table.shape, F32, kind="ExternalInput").ap())
    args.append(nc.dram_tensor("out", (B, S, HID), F32, kind="ExternalOutput").ap())
    build(nc, *args)
    r = run_bass_kernel_spmd(nc, [arrays], core_ids=[0])
    return r.results[0]["out"]
```

```python
import math
from contextlib import ExitStack

import concourse.bass as bass
from concourse import mybir

F32, F16, BF16, I32 = mybir.dt.float32, mybir.dt.float16, mybir.dt.bfloat16, mybir.dt.int32
ALU, ACT, AX = mybir.AluOpType, mybir.ActivationFunctionType, mybir.AxisListType

P = 128
B, S, HID = 16, 256, 256
NH, NOPE, ROPE, VD = 16, 128, 64, 128
QC, KVC, FF = 192, 64, 1024
HD = KVC + ROPE
QT = S // P
CT = HID // P
QB = QC - P
QUAD = 4
NQ = NH // QUAD
PAIRS = NH // 2
FT = FF // P
BLOCK = 32
DOWN = QC + KVC + ROPE
SCALE = (NOPE + ROPE) ** -0.5
LN_EPS, RMS_EPS = 1e-5, 1e-6
UP = 64.0
WMAX = 2.0 ** 7
PLIFT = 2.0 ** 14
GELU_C = math.sqrt(2.0 / math.pi)
GELU_A = 0.044715

SLOTS = [
    ([("OT", 0), ("ln1", 0)], [("OT", 1)]),
    ([("ln1x", 0)], [("xT", 0)]),
    ([("OT", 2)], [("D", 0)]),
    ([("OT", 3)], [("D", 1), ("scale", 0)]),
    ([("proj", 0)], [("scale", 1)]),
    ([("KT", 0), ("ln2", 0)], [("cT", 0)]),
    ([("Q", 0)], [("x2T", 0)]),
    ([("Q", 1)], [("up", 0)]),
    ([("Q", 2)], [("QT", 0)]),
    ([("up", 1), ("gelu", 0)], [("Q", 3), ("split", 0)]),
    ([("QT", 1), ("gelu", 1)], [("Q", 4), ("split", 1)]),
    ([("up", 2)], [("QT", 2)]),
    ([("Q", 5), ("gelu", 2)], [("up", 3), ("split", 2)]),
    ([("QT", 3), ("gelu", 3)], [("Q", 6), ("split", 3)]),
    ([("Q", 7)], [("down", 0), ("QT", 4)]),
    ([("QT", 5)], [("QT", 6), ("QT", 7)]),
]
PREP_SLOTS = [
    ([("upT", 0)], [("upT", 1)]),
    ([("upT", 2)], [("upT", 3)]),
    ([("blocks", 0), ("wo", 0)], [("abs", 0), ("wo", 1)]),
    ([("n", 0)], [("wo", 2)]),
    ([("wo", 3), ("levels", 0)], [("n", 1)]),
    ([("wo", 4), ("levels", 1)], [("wo", 5)]),
    ([("n", 2), ("levels", 2)], [("wo", 6)]),
    ([("wo", 7), ("values", 0)], [("n", 3)]),
    ([("upB", 0)], [("upB", 1), ("bound", 0)]),
    ([("dnT", 0)], [("dnT", 1)]),
    ([("dnT", 2)], [("dnT", 3)]),
    ([("blocks", 1)], [("abs", 1), ("nscale", 0)]),
    ([("levels", 3)], []),
    ([("levels", 4)], []),
    ([("levels", 5)], [("values", 1)]),
    ([("dnB", 0)], [("dnB", 1)]),
]
PREP_ROLES = ("upT", "wo", "n", "upB", "dnT", "dnB")
FRONT = [j for s in SLOTS for part in s for j in part if j[0] in ("xT", "D", "KT", "cT", "Q", "QT")]
BACK = [j for s in SLOTS for part in s for j in part if j[0] in ("OT", "proj", "x2T", "up", "down")]
FRONT_TASKS = ("ln1", "ln1x", "xT", "D", "scale", "KT", "cT", "Q", "QT")
BACK_TASKS = ("OT", "proj", "ln2", "x2T", "up", "gelu", "split", "down")
ACT_LAST = ("xT", "D", "Q", "up")
FRONT_DVE = [j for j in FRONT if j[0] not in ACT_LAST]
BACK_ACT = [j for j in BACK if j[0] not in ("proj", "down")]
BACK_DVE = [j for j in BACK if j[0] not in ACT_LAST]
NF, NFD, NB_, NBA, NBD = len(FRONT), len(FRONT_DVE), len(BACK), len(BACK_ACT), len(BACK_DVE)


class Batch:

    def __init__(self, const, pair=None):
        self.const, self.pair, self.parity = const, pair, const % 2

    def plus(self, d):
        return Batch(self.const + d, self.pair)

    def at(self, per, extra):
        v = per * self.const + extra
        return v if self.pair is None else self.pair * (2 * per) + v

    def first(self):
        return self.pair is None and self.const == 0


def wait(eng, sem, value):
    if isinstance(value, int) and value <= 0:
        return
    eng.wait_ge(sem, value)


def build(nc, x, w_q_down, q_norm_w, w_q_nope, w_q_rope, w_kv_down, kv_norm_w, w_k_nope, w_v_up,
          w_k_rope, w_o, up_kernel, up_bias, down_kernel, down_bias, rope_table, out):
    ctx = ExitStack()
    with ctx:
        def sb(name, shape, dt=F32):
            return ctx.enter_context(nc.sbuf_tensor(name, shape, dt))

        def sem(name):
            return ctx.enter_context(nc.semaphore(name))

        ident = sb("ident", [P, P])
        ident16 = sb("ident16", [P, P], BF16)
        rope = sb("rope", [P, QT, 2, ROPE])
        wdT = sb("wdT", [P, CT, DOWN])
        wa_hi = sb("wa_hi", [P, NH * HD], F16)
        wa_lo = sb("wa_lo", [P, NH * HD], F16)
        wb_hh = sb("wb_hh", [P, NH * HD], F16)
        wb_lo = sb("wb_lo", [QB, NH * HD], F16)
        n_hi = sb("n_hi", [P, PAIRS, HID], F16)
        n_lo = sb("n_lo", [P, PAIRS, HID], F16)
        up_q = sb("up_q", [P, CT, FF], BF16)
        dn_q = sb("dn_q", [P, FT, HID], BF16)
        ub = sb("ub", [P, FT])
        db = sb("db", [P, HID])
        small = sb("small", [P, 64])
        inv_kr, inv_s, inv_n, s_g, inv_g = (small[:, i:i + 1] for i in range(5))
        ln_eps, rms_eps, neg_half = (small[:, 8 + 2 * i:10 + 2 * i] for i in range(3))

        xf = sb("xf", [P, QT, HID])
        xb = sb("xb", [P, QT, HID])
        nothing = sb("nothing", [P, 1])
        st = sb("st", [P, 2, QT, 6])
        mv = sb("mv", [P, 2, QT, 2])
        va = sb("va", [P, 2, QT])
        rstd = sb("rstd", [P, 2, QT])
        xn = sb("xn", [P, QT, HID])
        xT = sb("xT", [P, CT, S])
        raw = sb("raw", [P, QT, DOWN])
        sq = sb("sq", [P, QT, QC + KVC])
        ssq = sb("ssq", [P, QT, 2])
        sse = sb("sse", [P, QT, 2])
        rms = sb("rms", [P, QT, 2])
        cq = sb("cq", [P, QT, QC])
        kt = sb("kt", [P, QT, HD])
        kr = sb("kr", [P, 2, ROPE])
        c_hi = [sb(f"c_hi{i}", [P, QT, KVC], F16) for i in range(2)]
        c_lo = [sb(f"c_lo{i}", [P, QT, KVC], F16) for i in range(2)]
        k_hi = [sb(f"k_hi{i}", [P, S], F16) for i in range(2)]
        k_lo = [sb(f"k_lo{i}", [P, S], F16) for i in range(2)]
        ca_hi = sb("ca_hi", [P, S], F16)
        ca_lo = sb("ca_lo", [P, S], F16)
        cb = sb("cb", [P, S], F16)
        qtok = [sb(f"qtok{i}", [P, QUAD, HD]) for i in range(4)]
        qr = [sb(f"qr{i}", [P, 2, QUAD, ROPE]) for i in range(2)]
        nmax = sb("nmax", [P, 2, QT])
        ebias = sb("ebias", [P, 2, QT])
        rsum = sb("rsum", [P, NH, QT])
        rinv = sb("rinv", [P, NH, QT])
        pr = [sb(f"pr{i}", [P, QT, S]) for i in range(2)]
        pt_hi = [sb(f"pt_hi{i}", [P, QT, S], F16) for i in range(2)]
        pt_lo = [sb(f"pt_lo{i}", [P, QT, S], F16) for i in range(2)]
        x1 = sb("x1", [P, QT, HID])
        x1b = sb("x1b", [P, QT, HID])
        x2n = sb("x2n", [P, QT, HID])
        x2_hi = sb("x2_hi", [P, CT, S], F16)
        x2_lo = sb("x2_lo", [P, CT, S], F16)
        gu = [sb(f"gu{i}", [P, 2, S]) for i in range(2)]
        gv = sb("gv", [P, 2, S])
        gw = sb("gw", [P, 2, S])
        gz = sb("gz", [P, 2, S])
        gt = sb("gt", [P, 2, S])
        ob = sb("ob", [P, QT, HID])

        late = sb("late", [P, 10240])
        q_hi0, q_lo0 = sb("q_hi0", [P, NH, S], F16), sb("q_lo0", [P, NH, S], F16)

        def carve(at, n, dt=F32):
            a = late[:, at:at + n]
            return a if dt is F32 else a.bitcast(dt)

        q_hi = [q_hi0, carve(0, 2048, F16).rearrange("p (h s) -> p h s", h=NH)]
        q_lo = [q_lo0, carve(2048, 2048, F16).rearrange("p (h s) -> p h s", h=NH)]
        otok = carve(4096, 2 * NH * KVC).rearrange("p (t h c) -> p t h c", t=QT, h=NH)
        ot_hi = carve(6144, 1024, F16).rearrange("p (j s) -> p j s", j=PAIRS)
        ot_lo = carve(7168, 1024, F16).rearrange("p (j s) -> p j s", j=PAIRS)
        g_hi = carve(8192, 1024, F16).rearrange("p (f s) -> p f s", f=FT)
        g_lo = carve(9216, 1024, F16).rearrange("p (f s) -> p f s", f=FT)
        wf_a = carve(0, 2048).rearrange("p (h c) -> p h c", h=NH)
        wf_b = carve(2048, 2048).rearrange("p (h c) -> p h c", h=NH)
        wvn = carve(6144, 1024).rearrange("p (h c) -> p h c", h=NH)
        woT = carve(7168, 1024).rearrange("p (k h c) -> p k h c", k=2, h=2)
        nf = carve(8192, 2048).rearrange("p (j c) -> p j c", j=PAIRS)
        wo_n = sb("wo_n", [P, 2, CT, 4 * VD])

        quant = sb("quant", [P, 8192])
        wqn = quant[:, 0:3072].rearrange("p (h c) -> p h c", h=NH)
        wkn = quant[:, 3072:4096].rearrange("p (h c) -> p h c", h=NH)
        wqr = quant[:, 4096:5632].rearrange("p (j c) -> p j c", j=PAIRS)
        w_nat = quant[:, 0:2048]
        w_T = quant[:, 2048:4096]
        w_c = quant[:, 4096:6144]
        w_x = quant[:, 6144:8192]
        w_16 = sb("w_16", [P, 2048], BF16)
        blk = sb("blk", [P, 4, 64])
        ub_n = sb("ub_n", [FT, P])
        gelu_k = sb("gelu_k", [P, 1])
        wd_n = sb("wd_n", [P, 3, HID])
        qn_a, qn_b = small[:, 16:17], small[0:QB, 17:18]
        qs_a, qs_b = small[:, 18:19], small[0:QB, 19:20]
        qr_a, qr_b = small[:, 20:21], small[0:QB, 21:22]
        kvn_c = small[:, 22:23]
        kvn_r = sb("kvn_r", [P, KVC])
        mx = sb("mx", [P, 16])

        bank = [ctx.enter_context(nc.psum_tensor(f"bank{i}", [P, 512], F32)) for i in range(8)]
        l_bank, t_bank, o_bank, f_bank, b_bank = bank[0:2], bank[2:4], bank[4], bank[5:7], bank[7]

        ident_zeroed, ident_made, ident16_made = sem("ident_zeroed"), sem("ident_made"), sem("ident16_made")
        wd_loaded, wq_loaded, wv_loaded = sem("wd_loaded"), sem("wq_loaded"), sem("wv_loaded")
        wo_loaded = [sem(f"wo_loaded{i}") for i in range(2)]
        norms_loaded, vec_loaded, rope_loaded = sem("norms_loaded"), sem("vec_loaded"), sem("rope_loaded")
        up_loaded, dn_loaded = sem("up_loaded"), sem("dn_loaded")
        consts_set = sem("consts_set")
        prep_filled, prep_act, prep_dve = sem("prep_filled"), sem("prep_act"), sem("prep_dve")
        prep_step = sem("prep_step")
        max_asked, max_given = sem("max_asked"), sem("max_given")
        kr_scaled, w_scaled, w_high, w_split = (sem(n) for n in ("kr_scaled", "w_scaled", "w_high", "w_split"))
        blocks_ready, x_scaled, x_abs, sign_ready, step_ready, quantised, n_split, g_scaled = (
            sem(n) for n in ("blocks_ready", "x_scaled", "x_abs", "sign_ready", "step_ready", "quantised",
                             "n_split", "g_scaled"))
        xf_loaded = sem("xf_loaded")
        xb_loaded = sem("xb_loaded")
        ln_stats = [sem("ln1_stats"), sem("ln2_stats")]
        ln_aggr = [sem("ln1_aggr"), sem("ln2_aggr")]
        ln_eps_added = [sem("ln1_eps_added"), sem("ln2_eps_added")]
        ln_rstd = [sem("ln1_rstd"), sem("ln2_rstd")]
        xn_ready, x2n_ready = sem("xn_ready"), sem("x2n_ready")
        front_filled, front_act, front_dve = sem("front_filled"), sem("front_act"), sem("front_dve")
        back_filled, back_act, back_dve = sem("back_filled"), sem("back_act"), sem("back_dve")
        rms_eps_added, rms_ready = sem("rms_eps_added"), sem("rms_ready")
        kr_parts, kr_ready = sem("kr_parts"), sem("kr_ready")
        latents_ready, c_hi_ready, c_ready = sem("latents_ready"), sem("c_hi_ready"), sem("c_ready")
        qr_parts, qtok_ready = sem("qr_parts"), sem("qtok_ready")
        logits_ready, max_found, bias_ready = sem("logits_ready"), sem("max_found"), sem("bias_ready")
        probs_ready, probsT_ready = sem("probs_ready"), sem("probsT_ready")
        pt_hi_ready, pt_lo_ready = sem("pt_hi_ready"), sem("pt_lo_ready")
        pv_done, rinv_ready, o_ready = sem("pv_done"), sem("rinv_ready"), sem("o_ready")
        x1_ready, x1b_ready = sem("x1_ready"), sem("x1b_ready")
        gv_ready, gw_ready, gz_ready, gt_ready, g_raw, g_hi_ready, g_ready = (
            sem(n) for n in ("gv_ready", "gw_ready", "gz_ready", "gt_ready", "g_raw", "g_hi_ready", "g_ready"))
        ob_ready, stored = sem("ob_ready"), sem("stored")

        block = ctx.enter_context(nc.Block())

        prep = ([("wd", k, "act") for k in range(CT)] + [("ma", k, "dve") for k in range(2)]
                + [("mb", k, "dve") for k in range(2)] + [("ra", k, "dve") for k in range(2)]
                + [("rb", k, "dve") for k in range(2)] + [("ub", 0, "act")])
        early = len(prep)
        prep += [(kind, k, "act") for slot in PREP_SLOTS for part in slot for kind, k in part
                 if kind in PREP_ROLES]
        prep_at = {(j[0], j[1]): i for i, j in enumerate(prep)}
        prep_banks = [bank[i] for i in (0, 1, 2, 3, 4, 7)]

        def prep_bank(i):
            return prep_banks[i % 6] if i < early else b_bank

        def before(i):
            if i < early:
                return i - 6 if i >= 6 else None
            return i - 1 if i > early else early - 1 - (early - 1 - 5) % 6

        def prep_count(i):
            return sum(j[2] == prep[i][2] for j in prep[:i + 1])

        def prep_free(pe, i):
            if before(i) is not None:
                pe.wait_ge(prep_act if prep[before(i)][2] == "act" else prep_dve, prep_count(before(i)))

        def front_bank(n, j):
            return f_bank[(NF * n.parity + FRONT.index(j)) % 2]

        def free_front(pe, n, j):
            k = FRONT.index(j) - 2
            m = n if k >= 0 else n.plus(-1)
            if m.pair is None and m.const < 0:
                return
            old = FRONT[k]
            if old[0] in ACT_LAST:
                pe.wait_ge(front_act, m.at(NF, FRONT.index(old) + 1))
            else:
                pe.wait_ge(front_dve, m.at(NFD, FRONT_DVE.index(old) + 1))

        def free_back(pe, n, j):
            k = BACK.index(j) - 1
            m = n if k >= 0 else n.plus(-1)
            if m.pair is None and m.const < 0:
                pe.wait_ge(prep_act, prep_count(len(prep) - 1))
                return
            old = BACK[k]
            if old[0] in ACT_LAST:
                pe.wait_ge(back_act, m.at(NBA, BACK_ACT.index(old) + 1))
            else:
                pe.wait_ge(back_dve, m.at(NBD, BACK_DVE.index(old) + 1))

        def flat(a):
            return a.rearrange("p a b -> p (a b)")

        def blocks_of(a):
            return a.rearrange("p (n e) -> p n e", e=BLOCK)

        def spread(v):
            return v.unsqueeze(2).to_broadcast([P, 2048 // BLOCK, BLOCK])

        s_w = small[:, 33:34]

        def tok(t):
            return slice(t * P, (t + 1) * P)

        xr = x.rearrange("b (t p) c -> b p t c", p=P)
        outr = out.rearrange("b (t p) c -> b p t c", p=P)

        @block.sync
        def _(sp):
            def load_front(n):
                wait(sp, xn_ready, n.at(QT, 0))
                sp.dma_start(xf[:], dram(xr, n)).then_inc(xf_loaded, 16)

            def dram(a, n):
                if n.pair is None:
                    return a[n.const]
                return a[bass.ds(n.pair * 2 + n.const, 1)].rearrange("o p t c -> p (o t) c")

            def load_back(n):
                wait(sp, x1_ready, n.at(1, 0))
                sp.dma_start(xb[:], dram(xr, n)).then_inc(xb_loaded, 16)

            def store(n):
                sp.wait_ge(ob_ready, n.at(1, 1))
                sp.dma_start(dram(outr, n), ob[:]).then_inc(stored, 16)

            sp.dma_start(wd_n[0:ROPE, 2, :], w_k_rope).then_inc(wd_loaded, 16)
            sp.dma_start(wd_n[:, 0, :], w_q_down[0:P, :]).then_inc(wd_loaded, 16)
            sp.dma_start(wd_n[0:QB, 1, :], w_q_down[P:QC, :]).then_inc(wd_loaded, 16)
            sp.dma_start(wd_n[QB:P, 1, :], w_kv_down).then_inc(wd_loaded, 16)
            load_front(Batch(0))
            sp.dma_start(wqn, w_q_nope.rearrange("(h p) c -> p h c", p=P)).then_inc(wq_loaded, 16)
            sp.dma_start(wkn, w_k_nope.rearrange("(h p) c -> p h c", p=P)).then_inc(wq_loaded, 16)
            sp.dma_start(wqr, w_q_rope.rearrange("(j p) c -> p j c", p=P)).then_inc(wq_loaded, 16)
            sp.dma_start(wvn, w_v_up.rearrange("(h p) c -> p h c", p=P)).then_inc(wv_loaded, 16)
            wo_r = w_o.rearrange("(m p) d -> p m d", p=P)

            def load_wo(k):
                sp.dma_start(wo_n[:, k % 2], wo_r[:, :, 512 * k:512 * (k + 1)]).then_inc(wo_loaded[k % 2], 16)

            load_wo(0)
            load_wo(1)
            sp.wait_ge(prep_filled, prep_at["rb", 1] + 1)
            sp.dma_start(w_nat.rearrange("p (m f) -> p m f", m=CT),
                         up_kernel.rearrange("(m p) f -> p m f", p=P)).then_inc(up_loaded, 16)
            load_front(Batch(1))
            sp.wait_ge(prep_filled, prep_at["upT", 3] + 1)
            sp.dma_start(w_nat.rearrange("p (m d) -> p m d", m=FT),
                         down_kernel.rearrange("(m p) d -> p m d", p=P)).then_inc(dn_loaded, 16)
            for k in (2, 3):
                sp.wait_ge(prep_filled, prep_at["wo", 2 * k - 3] + 1)
                load_wo(k)

            def iteration(b, front, back):
                if front:
                    load_front(b.plus(1))
                if back:
                    load_back(b.plus(-1))
                    store(b.plus(-1))

            iteration(Batch(1), True, True)
            with sp.Fori(0, B // 2 - 2) as pair:
                iteration(Batch(2, pair), True, True)
                iteration(Batch(3, pair), True, True)
            iteration(Batch(B - 2), True, True)
            iteration(Batch(B - 1), False, True)
            load_back(Batch(B - 1))
            store(Batch(B - 1))
            sp.wait_ge(stored, 16 * B)

        @block.gpsimd
        def _(pool):
            pool.memset(ident[:], 0.0).then_inc(ident_zeroed, 1)
            pool.wait_ge(ident_zeroed, 1)
            pool.affine_select(out=ident[:], in_=ident[:], compare_op=ALU.not_equal, fill=1.0, base=0,
                               pattern=[[-1, P]], channel_multiplier=1).then_inc(ident_made, 1)
            for ap, v in ((ln_eps, LN_EPS), (rms_eps, RMS_EPS), (neg_half, -0.5), (gelu_k[:], 1.0 / GELU_A)):
                pool.memset(ap, v).then_inc(consts_set, 1)

            def maximum(k):
                pool.wait_ge(max_asked, k + 1)
                pool.partition_all_reduce(mx[:, 2 * k + 8:2 * k + 10], mx[:, 2 * k:2 * k + 2], P,
                                          bass.bass_isa.ReduceOp.max).then_inc(max_given, 1)

            def prep_task(j):
                kind, k = j
                if kind == "bound":
                    maximum(2)
                elif kind == "nscale":
                    maximum(3)
                elif kind == "blocks":
                    pool.wait_ge(blocks_ready, k + 1)
                    pool.tensor_tensor(blocks_of(w_x), blocks_of(w_T), spread(blk[:, 2, :]),
                                       ALU.mult).then_inc(x_scaled, 1)
                    pool.wait_ge(sign_ready, k + 1)
                    pool.tensor_tensor(blocks_of(w_16[:]), blocks_of(w_16[:]), spread(blk[:, 3, :]),
                                       ALU.mult).then_inc(step_ready, 1)

            def ln(n, which):
                pool.wait_ge(ln_aggr[which], n.at(QT, QT))
                pool.tensor_tensor(va[:, which, :], mv[:, which, :, 1], ln_eps,
                                   ALU.add).then_inc(ln_eps_added[which], 1)
                pool.wait_ge(ln_eps_added[which], n.at(1, 1))
                pool.tensor_tensor(rstd[:, which, :], va[:, which, :], neg_half,
                                   ALU.pow).then_inc(ln_rstd[which], 1)

            def task(n, j):
                kind, k = j
                if kind == "ln1" or kind == "ln2":
                    if kind == "ln2":
                        pool.wait_ge(x1_ready, n.at(1, 1))
                        if not n.first():
                            pool.wait_ge(ob_ready, n.at(1, 0))
                        pool.tensor_tensor(x1b[:], x1[:], db[:].unsqueeze(1).to_broadcast([P, QT, HID]),
                                           ALU.add).then_inc(x1b_ready, 1)
                    ln(n, int(kind == "ln2"))
                elif kind == "D":
                    pool.wait_ge(front_act, n.at(NF, FRONT.index(j) + 1))
                    pool.tensor_tensor(sse[:, k, :], ssq[:, k, :], rms_eps, ALU.add).then_inc(rms_eps_added, 1)
                    pool.wait_ge(rms_eps_added, n.at(QT, k + 1))
                    pool.tensor_tensor(rms[:, k, :], sse[:, k, :], neg_half, ALU.pow).then_inc(rms_ready, 1)
                    r = raw[:, k, QC + KVC:DOWN]
                    pool.tensor_tensor(kr[:, 0, :], r, rope[:, k, 0, :], ALU.mult).then_inc(kr_parts, 1)
                    h = ROPE // 2
                    pool.tensor_tensor(kr[:, 1, 0:h], r[:, h:ROPE], rope[:, k, 1, 0:h],
                                       ALU.mult).then_inc(kr_parts, 1)
                    pool.tensor_tensor(kr[:, 1, h:ROPE], r[:, 0:h], rope[:, k, 1, h:ROPE],
                                       ALU.mult).then_inc(kr_parts, 1)
                    pool.wait_ge(kr_parts, n.at(3 * QT, 3 * k + 3))
                    pool.tensor_tensor(kt[:, k, KVC:HD], kr[:, 0, :], kr[:, 1, :],
                                       ALU.add).then_inc(kr_ready, 1)
                elif kind == "Q":
                    pool.wait_ge(front_act, n.at(NF, FRONT.index(j) + 1))
                    q, t, hf = qtok[k % 4][:, :, KVC:HD], k % 2, ROPE // 2
                    cos, sin = rope[:, t, 0, :], rope[:, t, 1, :]
                    pool.tensor_tensor(qr[k % 2][:, 0], q, cos.unsqueeze(1).to_broadcast([P, QUAD, ROPE]),
                                       ALU.mult).then_inc(qr_parts, 1)
                    pool.tensor_tensor(qr[k % 2][:, 1, :, 0:hf], q[:, :, hf:ROPE],
                                       sin[:, 0:hf].unsqueeze(1).to_broadcast([P, QUAD, hf]),
                                       ALU.mult).then_inc(qr_parts, 1)
                    pool.tensor_tensor(qr[k % 2][:, 1, :, hf:ROPE], q[:, :, 0:hf],
                                       sin[:, hf:ROPE].unsqueeze(1).to_broadcast([P, QUAD, hf]),
                                       ALU.mult).then_inc(qr_parts, 1)
                    pool.wait_ge(qr_parts, n.at(24, 3 * k + 3))
                    pool.tensor_tensor(q, qr[k % 2][:, 0], qr[k % 2][:, 1], ALU.add).then_inc(qtok_ready, 1)
                elif kind == "up":
                    pool.wait_ge(back_act, n.at(NBA, BACK_ACT.index(j) + 1))
                    wait(pool, gt_ready, n.at(4, k))
                    u = gu[k % 2][:]
                    pool.tensor_tensor(gv[:], u, u, ALU.mult).then_inc(gv_ready, 1)
                    pool.wait_ge(gv_ready, n.at(4, k + 1))
                    pool.tensor_tensor(gw[:], gv[:], gelu_k[:].unsqueeze(1).to_broadcast([P, 2, S]),
                                       ALU.add).then_inc(gw_ready, 1)
                    pool.wait_ge(gw_ready, n.at(4, k + 1))
                    pool.tensor_tensor(gz[:], gw[:], u, ALU.mult).then_inc(gz_ready, 1)

            maximum(0)
            pool.wait_ge(consts_set, 4)
            pool.wait_ge(rope_loaded, 16)
            for s in SLOTS[:6]:
                for j in s[0] + s[1]:
                    if j[0] in FRONT_TASKS:
                        task(Batch(0), j)
            maximum(1)
            for s in SLOTS[6:]:
                for j in s[0] + s[1]:
                    if j[0] in FRONT_TASKS:
                        task(Batch(0), j)

            def iteration(b, front, back):
                for h in range(NH):
                    for i, part in enumerate(SLOTS[h]):
                        if b.first():
                            for j in PREP_SLOTS[h][i]:
                                prep_task(j)
                        for j in part:
                            if j[0] in FRONT_TASKS and front:
                                task(b.plus(1), j)
                            if j[0] in BACK_TASKS and back:
                                task(b.plus(-1), j)

            pool.wait_ge(vec_loaded, 16 * 2)
            iteration(Batch(0), True, False)
            iteration(Batch(1), True, True)
            with pool.Fori(0, B // 2 - 2) as pair:
                iteration(Batch(2, pair), True, True)
                iteration(Batch(3, pair), True, True)
            iteration(Batch(B - 2), True, True)
            iteration(Batch(B - 1), False, True)
            for s in SLOTS:
                for j in s[0] + s[1]:
                    if j[0] in BACK_TASKS:
                        task(Batch(B - 1), j)

        @block.scalar
        def _(act):
            act.dma_start(qn_a, q_norm_w[0:P].unsqueeze(1)).then_inc(norms_loaded, 16)
            act.dma_start(qn_b, q_norm_w[P:QC].unsqueeze(1)).then_inc(norms_loaded, 16)
            act.dma_start(kvn_r[:], kv_norm_w.unsqueeze(0).to_broadcast([P, KVC])).then_inc(norms_loaded, 16)
            act.dma_start(kvn_c[0:KVC], kv_norm_w.unsqueeze(1)).then_inc(norms_loaded, 16)
            act.dma_start(kvn_c[KVC:P], kv_norm_w.unsqueeze(1)).then_inc(norms_loaded, 16)
            act.dma_start(rope[:], rope_table.rearrange("(t p) w c -> p t w c", p=P)).then_inc(rope_loaded, 16)
            act.dma_start(ub_n[:], up_bias.rearrange("(f p) -> f p", p=P)).then_inc(vec_loaded, 16)
            act.dma_start(db[:], down_bias.unsqueeze(0).to_broadcast([P, HID])).then_inc(vec_loaded, 16)
            act.wait_ge(ident_made, 1)
            act.activation(ident16[:], ident[:], ACT.Copy).then_inc(ident16_made, 1)

            def read_out(kind, k):
                i = prep_at[kind, k]
                act.wait_ge(prep_filled, i + 1)
                src = prep_bank(i)
                if kind == "wd":
                    ins = act.activation(wdT[:, k, :], src[:, 0:DOWN], ACT.Copy)
                elif kind == "ub":
                    ins = act.activation(ub[:], src[:, 0:FT], ACT.Copy)
                elif kind == "wo":
                    ins = act.activation(woT[:, k % 2].rearrange("p h c -> p (h c)"), src[:], ACT.Copy)
                elif kind == "n":
                    if k == 0:
                        act.wait_ge(norms_loaded, 16 * 5)
                    ins = act.activation(nf[:, 2 * k:2 * k + 2, :].rearrange("p j c -> p (j c)"), src[:],
                                         ACT.Copy, scale=kvn_c)
                elif kind in ("upT", "dnT"):
                    ins = act.activation(w_T[:, 512 * k:512 * (k + 1)], src[:], ACT.Copy)
                elif kind == "upB":
                    ins = act.activation(up_q[:, k, :], src[:].bitcast(BF16), ACT.Copy)
                else:
                    ins = act.activation(dn_q[:, 4 * k:4 * k + 4, :].rearrange("p f d -> p (f d)"),
                                         src[:].bitcast(BF16), ACT.Copy)
                ins.then_inc(prep_act, 1)

            def prep_task(j):
                kind, k = j
                if kind in PREP_ROLES:
                    read_out(kind, k)
                elif kind == "abs":
                    act.wait_ge(prep_act, prep_count(prep_at["upT" if k == 0 else "dnT", 3]))
                    if k:
                        act.wait_ge(prep_filled, prep_at["upB", CT - 1] + 1)
                    act.activation(w_16[:], w_T, ACT.Sign).then_inc(sign_ready, 1)
                    act.wait_ge(x_scaled, k + 1)
                    act.activation(w_x, w_x, ACT.Abs).then_inc(x_abs, 1)

            def task(n, j):
                kind, k = j
                if kind in ("xT", "D", "KT", "cT", "Q", "QT"):
                    src = front_bank(n, j)
                    act.wait_ge(front_filled, n.at(NF, FRONT.index(j) + 1))
                    if kind == "xT":
                        act.activation(xT[:], src[:].rearrange("p (m s) -> p m s", m=CT),
                                       ACT.Copy).then_inc(front_act, 1)
                    elif kind == "D":
                        act.activation(sq[:, k, 0:QC], src[:, 0:QC], ACT.Square, scale=QC ** -0.5,
                                       accum_out=ssq[:, k, 0:1])
                        act.activation(sq[:, k, QC:QC + KVC], src[:, QC:QC + KVC], ACT.Square, scale=KVC ** -0.5,
                                       accum_out=ssq[:, k, 1:2])
                        act.activation(raw[:, k, :], src[:, 0:DOWN], ACT.Copy).then_inc(front_act, 1)
                    elif kind == "KT":
                        act.activation(k_hi[n.parity][:], src[:, 0:S], ACT.Copy,
                                       scale=UP).then_inc(front_act, 1)
                    elif kind == "cT":
                        act.activation(ca_hi[:], src[:, 0:S], ACT.Copy, scale=UP)
                        act.activation(cb[0:QB, :], src[0:QB, S:2 * S], ACT.Copy,
                                       scale=UP).then_inc(front_act, 1)
                    elif kind == "Q":
                        act.activation(qtok[k % 4][:].rearrange("p h c -> p (h c)"), src[:],
                                       ACT.Copy).then_inc(front_act, 1)
                    else:
                        g, t = k // 2, k % 2
                        act.activation(q_hi[n.parity][:, QUAD * g:QUAD * g + QUAD, tok(t)],
                                       src[:].rearrange("p (h s) -> p h s", h=QUAD),
                                       ACT.Copy, scale=1.0 / UP).then_inc(front_act, 1)
                elif kind in ("OT", "x2T", "up"):
                    act.wait_ge(back_filled, n.at(NB_, BACK.index(j) + 1))
                    if kind == "OT":
                        t, half = k % 2, k // 2
                        act.activation(ot_hi[:, 4 * half:4 * half + 4, tok(t)],
                                       b_bank[:].rearrange("p (j s) -> p j s", j=4),
                                       ACT.Copy, scale=1.0 / PLIFT).then_inc(back_act, 1)
                    elif kind == "x2T":
                        act.activation(x2_hi[:], b_bank[:].rearrange("p (m s) -> p m s", m=CT), ACT.Copy,
                                       scale=UP).then_inc(back_act, 1)
                    else:
                        if k >= 2:
                            act.wait_ge(g_ready, n.at(4, k - 1))
                        for i in range(2):
                            last = act.activation(gu[k % 2][:, i, :], b_bank[:, S * i:S * (i + 1)],
                                                  ACT.Identity, scale=1.0 / UP,
                                                  bias=ub[:, 2 * k + i:2 * k + i + 1])
                        last.then_inc(back_act, 1)
                elif kind == "gelu":
                    act.wait_ge(gz_ready, n.at(4, k + 1))
                    wait(act, g_ready, n.at(4, k))
                    act.activation(gt[:], gz[:], ACT.Tanh, scale=GELU_C * GELU_A).then_inc(gt_ready, 1)

            def exps(n, h):
                act.wait_ge(bias_ready, n.at(NH, h + 1))
                wait(act, probsT_ready, n.at(NH, h - 1))
                for t in range(QT):
                    last = act.activation(pr[h % 2][:, t, :], l_bank[h % 2][:, S * t:S * (t + 1)], ACT.Exp,
                                          scale=inv_s, bias=ebias[:, h % 2, t:t + 1],
                                          accum_out=rsum[:, h, t:t + 1])
                last.then_inc(probs_ready, 1)

            def pt_high(n, h):
                act.wait_ge(probsT_ready, n.at(NH, h + 1))
                wait(act, pv_done, n.at(NH, h - 1))
                act.activation(pt_hi[h % 2][:].rearrange("p k s -> p (k s)"), t_bank[h % 2][:],
                               ACT.Copy, scale=PLIFT).then_inc(pt_hi_ready, 1)

            def split_high(g):
                cols = slice(512 * g, 512 * (g + 1))
                if g == 0:
                    act.wait_ge(w_scaled, 1)
                act.activation(wa_hi[:, cols], flat(wf_a)[:, cols], ACT.Copy, scale=s_w)
                act.activation(wb_hh[0:QB, cols], flat(wf_b)[0:QB, cols], ACT.Copy, scale=s_w[0:QB])
                act.activation(wb_hh[QB:P, cols], flat(wf_b)[0:QB, cols], ACT.Copy,
                               scale=s_w[0:QB]).then_inc(w_high, 1)

            for k in range(CT):
                read_out("wd", k)
            for s in SLOTS[:6]:
                for j in s[0] + s[1]:
                    if j[0] in FRONT_TASKS:
                        task(Batch(0), j)
            for g in range(NQ):
                split_high(g)
            read_out("ub", 0)
            for s in SLOTS[6:]:
                for j in s[0] + s[1]:
                    if j[0] in FRONT_TASKS:
                        task(Batch(0), j)
            exps(Batch(0), 0)

            def iteration(b, front, back):
                for h in range(NH):
                    if h + 1 < NH or front:
                        exps(b, h + 1) if h + 1 < NH else exps(b.plus(1), 0)
                    for i, part in enumerate(SLOTS[h]):
                        if b.first():
                            for j in PREP_SLOTS[h][i]:
                                prep_task(j)
                        for j in part:
                            if j[0] in FRONT_TASKS and front:
                                task(b.plus(1), j)
                            if j[0] in BACK_TASKS and back:
                                task(b.plus(-1), j)
                        if i == 0:
                            pt_high(b, h)

            iteration(Batch(0), True, False)
            iteration(Batch(1), True, True)
            with act.Fori(0, B // 2 - 2) as pair:
                iteration(Batch(2, pair), True, True)
                iteration(Batch(3, pair), True, True)
            iteration(Batch(B - 2), True, True)
            iteration(Batch(B - 1), False, True)
            for s in SLOTS:
                for j in s[0] + s[1]:
                    if j[0] in BACK_TASKS:
                        task(Batch(B - 1), j)

        @block.vector
        def _(dve):
            steps = [0]

            def step(ins):
                steps[0] += 1
                ins.then_inc(prep_step, 1)
                dve.wait_ge(prep_step, steps[0])

            def low(dst, src, high, factor):
                return dve.scalar_tensor_tensor(out=dst, in0=src, scalar=factor, in1=high, op0=ALU.mult,
                                                op1=ALU.subtract)

            def over_partitions(k):
                step(dve.tensor_scalar(mx[:, 2 * k:2 * k + 2], mx[:, 2 * k:2 * k + 2], 1e-30, None, ALU.max))
                dve.sem_inc(max_asked, 1)
                dve.wait_ge(max_given, k + 1)
                return mx[:, 2 * k + 8:2 * k + 9], mx[:, 2 * k + 9:2 * k + 10]

            def power(ap):
                step(dve.tensor_scalar(ap.bitcast(I32), ap.bitcast(I32), 0x7F800000, None, ALU.bitwise_and))

            def scale_of(m, s, inv, top):
                power(m)
                step(dve.reciprocal(s, m))
                step(dve.tensor_scalar(s, s, top, None, ALU.mult))
                step(dve.tensor_scalar(inv, m, 1.0 / top, None, ALU.mult))

            step(dve.memset(mx[:], 0.0))
            dve.wait_ge(wd_loaded, 16 * 4)
            step(dve.tensor_reduce(mx[0:ROPE, 0:1], wd_n[0:ROPE, 2, :], AX.X, ALU.max,
                                   apply_absolute_value=True))
            m, _m = over_partitions(0)
            scale_of(m, small[:, 32:33], inv_kr, 1.0)
            step(dve.tensor_scalar(wd_n[0:ROPE, 2, :], wd_n[0:ROPE, 2, :], small[0:ROPE, 32:33], None,
                                   ALU.mult))
            dve.sem_inc(kr_scaled, 1)

            def products():
                dve.wait_ge(norms_loaded, 16 * 5)
                for q, s, r in ((qn_a, qs_a, qr_a), (qn_b, qs_b, qr_b)):
                    step(dve.tensor_scalar(s, q, SCALE, None, ALU.mult))
                    step(dve.tensor_scalar(r, s, inv_kr[0:q.shape[0]], None, ALU.mult))
                for i, (kind, k, who) in enumerate(prep):
                    if who != "dve":
                        continue
                    dve.wait_ge(prep_filled, i + 1)
                    src = prep_bank(i)
                    hs = slice(8 * k, 8 * k + 8)
                    if kind in ("ma", "mb"):
                        rows, s, dst = (P, qs_a, wf_a) if kind == "ma" else (QB, qs_b, wf_b)
                        ins = dve.scalar_tensor_tensor(
                            out=dst[0:rows, hs, 0:KVC], in0=src[0:rows].rearrange("p (h c) -> p h c", h=8),
                            scalar=s, in1=kvn_r[0:rows].unsqueeze(1).to_broadcast([rows, 8, KVC]),
                            op0=ALU.mult, op1=ALU.mult)
                    else:
                        rows, s, dst = (P, qr_a, wf_a) if kind == "ra" else (QB, qr_b, wf_b)
                        ins = dve.tensor_scalar(dst[0:rows, hs, KVC:HD],
                                                src[0:rows].rearrange("p (h c) -> p h c", h=8), s, None,
                                                ALU.mult)
                    ins.then_inc(prep_dve, 1)
                dve.wait_ge(prep_dve, 8)
                step(dve.tensor_reduce(mx[:, 2:3], flat(wf_a), AX.X, ALU.max, apply_absolute_value=True))
                step(dve.tensor_reduce(mx[0:QB, 3:4], flat(wf_b)[0:QB], AX.X, ALU.max,
                                       apply_absolute_value=True))
                m, m2 = over_partitions(1)
                step(dve.tensor_tensor(m, m, m2, ALU.max))
                scale_of(m, s_w, inv_s, WMAX)
                step(dve.tensor_scalar(inv_s, inv_s, 1.0 / UP, None, ALU.mult))
                dve.sem_inc(w_scaled, 1)

            def split_low(g):
                cols = slice(512 * g, 512 * (g + 1))
                dve.wait_ge(w_high, g + 1)
                low(wb_lo[:, cols], flat(wf_b)[0:QB, cols], wb_hh[0:QB, cols], s_w[0:QB])
                low(wa_lo[:, cols], flat(wf_a)[:, cols], wa_hi[:, cols], s_w).then_inc(w_split, 1)

            def prep_task(j):
                kind, k = j
                if kind == "blocks":
                    amax, sc, inv, half = (blk[:, i, :] for i in range(4))
                    dve.wait_ge(prep_act, prep_count(prep_at["upT" if k == 0 else "dnT", 3]))
                    if k:
                        dve.wait_ge(step_ready, k)
                    step(dve.tensor_reduce(amax, blocks_of(w_T), AX.X, ALU.max, apply_absolute_value=True))
                    if k == 0:
                        step(dve.tensor_reduce(mx[:, 4:5], amax, AX.X, ALU.max))
                    step(dve.tensor_scalar(sc, amax, 1e-30, None, ALU.max))
                    power(sc)
                    step(dve.tensor_scalar(sc, sc, 0.25, None, ALU.mult))
                    step(dve.reciprocal(inv, sc))
                    step(dve.tensor_scalar(half, sc, 0.5, None, ALU.mult))
                    dve.sem_inc(blocks_ready, 1)
                elif kind == "levels":
                    if k % 3 == 0:
                        dve.wait_ge(x_abs, k // 3 + 1)
                        step(dve.tensor_scalar(w_c, w_x, 5.0, 2.0, ALU.is_ge, ALU.mult))
                        mids = (3.5, 2.5)
                    elif k % 3 == 1:
                        step(dve.tensor_scalar(w_c, w_c, 2.0, None, ALU.mult))
                        mids = (1.75, 1.25)
                    else:
                        mids = (0.75, 0.25)
                    for mid in mids:
                        step(dve.scalar_tensor_tensor(out=w_c, in0=w_x, scalar=mid, in1=w_c, op0=ALU.is_ge,
                                                      op1=ALU.add))
                elif kind == "values":
                    dve.wait_ge(step_ready, k + 1)
                    dve.tensor_tensor(w_16[:], w_16[:], w_c, ALU.mult).then_inc(quantised, 1)
                elif kind == "bound":
                    dve.wait_ge(prep_act, prep_count(prep_at["ub", 0]))
                    step(dve.tensor_reduce(mx[:, 5:6], ub[:], AX.X, ALU.max, apply_absolute_value=True))
                    m, m2 = over_partitions(2)
                    step(dve.tensor_scalar(m, m, 2 * 1.5 * HID, None, ALU.mult))
                    step(dve.tensor_scalar(m2, m2, 2.0, None, ALU.mult))
                    step(dve.tensor_tensor(m, m, m2, ALU.add))
                    scale_of(m, s_g, inv_g, 2.0 ** 14)
                    step(dve.tensor_scalar(inv_g, inv_g, 0.5, None, ALU.mult))
                elif kind == "nscale":
                    dve.wait_ge(prep_act, prep_count(prep_at["n", 3]))
                    step(dve.tensor_reduce(mx[:, 6:7], flat(nf), AX.X, ALU.max, apply_absolute_value=True))
                    m, _m = over_partitions(3)
                    s_n = small[:, 34:35]
                    scale_of(m, s_n, inv_n, WMAX)
                    step(dve.tensor_scalar(inv_n, inv_n, 1.0 / UP, None, ALU.mult))
                    step(dve.tensor_scalar(flat(n_hi[:]), flat(nf), s_n, None, ALU.mult))
                    low(flat(n_lo[:]), flat(nf), flat(n_hi[:]), s_n).then_inc(n_split, 1)

            def ln(n, which, src):
                for t in range(QT):
                    dve.bn_stats(st[:, which, t, :], src[:, t, :]).then_inc(ln_stats[which], 1)
                dve.wait_ge(ln_stats[which], n.at(QT, QT))
                dve.memset(nothing[:], 0.0)
                for t in range(QT):
                    dve.bn_aggr(mv[:, which, t, :], st[:, which, t, :]).then_inc(ln_aggr[which], 1)

            def ln_apply(n, which, src, dst, ready):
                dve.wait_ge(ln_rstd[which], n.at(1, 1))
                for t in range(QT):
                    dve.tensor_scalar(dst[:, t, :], src[:, t, :], mv[:, which, t, 0:1],
                                      rstd[:, which, t:t + 1], ALU.subtract, ALU.mult).then_inc(ready, 1)

            def task(n, j):
                kind, k = j
                if kind == "ln1":
                    dve.wait_ge(xf_loaded, n.at(16, 16))
                    ln(n, 0, xf)
                elif kind == "ln1x":
                    ln_apply(n, 0, xf, xn, xn_ready)
                elif kind in ("KT", "cT", "QT"):
                    dve.wait_ge(front_act, n.at(NF, FRONT.index(j) + 1))
                    src = front_bank(n, j)
                    if kind == "KT":
                        low(k_lo[n.parity][:], src[:, 0:S], k_hi[n.parity][:], UP).then_inc(front_dve, 1)
                    elif kind == "cT":
                        low(cb[QB:P, :], src[0:QB, S:2 * S], cb[0:QB, :], UP)
                        low(ca_lo[:], src[:, 0:S], ca_hi[:], UP).then_inc(front_dve, 1)
                    else:
                        g, t = k // 2, k % 2
                        low(q_lo[n.parity][:, QUAD * g:QUAD * g + QUAD, tok(t)],
                            src[:].rearrange("p (h s) -> p h s", h=QUAD),
                            q_hi[n.parity][:, QUAD * g:QUAD * g + QUAD, tok(t)],
                            1.0 / UP).then_inc(front_dve, 1)
                elif kind == "scale":
                    dve.wait_ge(rms_ready, n.at(QT, k + 1))
                    dve.tensor_scalar(cq[:, k, :], raw[:, k, 0:QC], rms[:, k, 0:1], None,
                                      ALU.mult)
                    dve.tensor_scalar(kt[:, k, 0:KVC], raw[:, k, QC:QC + KVC], rms[:, k, 1:2], None,
                                      ALU.mult).then_inc(latents_ready, 1)
                    dve.wait_ge(latents_ready, n.at(QT, k + 1))
                    dve.tensor_scalar(c_hi[n.parity][:, k, :], kt[:, k, 0:KVC], UP, None,
                                      ALU.mult).then_inc(c_hi_ready, 1)
                    dve.wait_ge(c_hi_ready, n.at(QT, k + 1))
                    low(c_lo[n.parity][:, k, :], kt[:, k, 0:KVC], c_hi[n.parity][:, k, :],
                        UP).then_inc(c_ready, 1)
                elif kind == "OT":
                    t, half = k % 2, k // 2
                    dve.wait_ge(back_act, n.at(NBA, BACK_ACT.index(j) + 1))
                    hs = slice(4 * half, 4 * half + 4)
                    low(ot_lo[:, hs, tok(t)], b_bank[:].rearrange("p (j s) -> p j s", j=4),
                        ot_hi[:, hs, tok(t)], 1.0 / PLIFT).then_inc(back_dve, 1)
                elif kind == "proj":
                    dve.wait_ge(back_filled, n.at(NB_, BACK.index(j) + 1))
                    dve.wait_ge(xb_loaded, n.at(16, 16))
                    dve.scalar_tensor_tensor(out=x1[:], in0=b_bank[:].rearrange("p (t c) -> p t c", t=QT),
                                             scalar=inv_n, in1=xb[:], op0=ALU.mult,
                                             op1=ALU.add).then_inc(x1_ready, 1)
                    dve.wait_ge(x1_ready, n.at(1, 1))
                    dve.sem_inc(back_dve, 1)
                    ln(n, 1, x1)
                elif kind == "ln2":
                    ln_apply(n, 1, x1, x2n, x2n_ready)
                elif kind == "x2T":
                    dve.wait_ge(back_act, n.at(NBA, BACK_ACT.index(j) + 1))
                    low(x2_lo[:], b_bank[:].rearrange("p (m s) -> p m s", m=CT), x2_hi[:],
                        UP).then_inc(back_dve, 1)
                elif kind == "split":
                    dve.wait_ge(gt_ready, n.at(4, k + 1))
                    dve.scalar_tensor_tensor(out=gt[:], in0=gt[:], scalar=1.0, in1=gu[k % 2][:],
                                             op0=ALU.add, op1=ALU.mult).then_inc(g_raw, 1)
                    dve.wait_ge(g_raw, n.at(4, k + 1))
                    dve.tensor_scalar(g_hi[:, 2 * k:2 * k + 2, :], gt[:], s_g, None,
                                      ALU.mult).then_inc(g_hi_ready, 1)
                    dve.wait_ge(g_hi_ready, n.at(4, k + 1))
                    low(g_lo[:, 2 * k:2 * k + 2, :], gt[:], g_hi[:, 2 * k:2 * k + 2, :],
                        s_g).then_inc(g_ready, 1)
                elif kind == "down":
                    dve.wait_ge(back_filled, n.at(NB_, BACK.index(j) + 1))
                    dve.wait_ge(x1b_ready, n.at(1, 1))
                    wait(dve, stored, n.at(16, 0))
                    dve.scalar_tensor_tensor(out=ob[:], in0=b_bank[:].rearrange("p (t c) -> p t c", t=QT),
                                             scalar=inv_g, in1=x1b[:], op0=ALU.mult,
                                             op1=ALU.add).then_inc(ob_ready, 1)
                    dve.wait_ge(ob_ready, n.at(1, 1))
                    dve.sem_inc(back_dve, 1)

            def maxes(n, h):
                dve.wait_ge(logits_ready, n.at(NH, h + 1))
                dve.tensor_reduce(nmax[:, h % 2, :], l_bank[h % 2][:].rearrange("p (t s) -> p t s", t=QT),
                                  AX.X, ALU.max, negate=True).then_inc(max_found, 1)
                dve.wait_ge(max_found, n.at(NH, h + 1))
                dve.tensor_scalar(ebias[:, h % 2, :], nmax[:, h % 2, :], inv_s, None, ALU.mult).then_inc(bias_ready, 1)

            def pt_low(n, h):
                dve.wait_ge(pt_hi_ready, n.at(NH, h + 1))
                low(pt_lo[h % 2][:].rearrange("p k s -> p (k s)"), t_bank[h % 2][:],
                    pt_hi[h % 2][:].rearrange("p k s -> p (k s)"), PLIFT).then_inc(pt_lo_ready, 1)

            def normalise(n, g):
                hs = slice(QUAD * g, QUAD * g + QUAD)
                dve.wait_ge(pv_done, n.at(NH, QUAD * g + QUAD))
                if g == 0 and not n.first():
                    dve.wait_ge(back_filled, n.at(NB_, 4 - NB_))
                dve.reciprocal(rinv[:, hs, :], rsum[:, hs, :]).then_inc(rinv_ready, 1)
                dve.wait_ge(rinv_ready, n.at(NQ, g + 1))
                dve.tensor_tensor(otok[:, :, hs, :].rearrange("p t h c -> p h t c"),
                                  o_bank[:].rearrange("p (h t c) -> p h t c", h=QUAD, t=QT),
                                  rinv[:, hs, :].unsqueeze(3).to_broadcast([P, QUAD, QT, KVC]),
                                  ALU.mult).then_inc(o_ready, 1)

            for j in (("ln1", 0), ("ln1x", 0)):
                task(Batch(0), j)
            products()
            for s in SLOTS[2:6]:
                for j in s[0] + s[1]:
                    if j[0] in FRONT_TASKS:
                        task(Batch(0), j)
            for g in range(NQ):
                split_low(g)
            for s in SLOTS[6:]:
                for j in s[0] + s[1]:
                    if j[0] in FRONT_TASKS:
                        task(Batch(0), j)
            maxes(Batch(0), 0)

            def iteration(b, front, back):
                for h in range(NH):
                    if h + 1 < NH or front:
                        maxes(b, h + 1) if h + 1 < NH else maxes(b.plus(1), 0)
                    if h == 1 and back:
                        normalise(b.plus(-1), NQ - 1)
                    if h % QUAD == 1 and h > QUAD:
                        normalise(b, h // QUAD - 1)
                    for i in range(2):
                        late = SLOTS[h][0] if i else SLOTS[h - 1][1]
                        if b.first():
                            for j in PREP_SLOTS[h][i]:
                                prep_task(j)
                        if h or i:
                            for j in late:
                                if j[0] in FRONT_TASKS and front:
                                    task(b.plus(1), j)
                                if j[0] in BACK_TASKS and back:
                                    task(b.plus(-1), j)
                        elif back:
                            for j in late:
                                task(b, j)
                        if i:
                            pt_low(b, h)

            iteration(Batch(0), True, False)
            iteration(Batch(1), True, True)
            with dve.Fori(0, B // 2 - 2) as pair:
                iteration(Batch(2, pair), True, True)
                iteration(Batch(3, pair), True, True)
            iteration(Batch(B - 2), True, True)
            iteration(Batch(B - 1), False, True)
            normalise(Batch(B - 1), NQ - 1)
            for s in SLOTS:
                for j in s[0] + s[1]:
                    if j[0] in BACK_TASKS:
                        task(Batch(B - 1), j)

        @block.tensor
        def _(pe):
            def pairs(out_, terms):
                for i, (a, b) in enumerate(terms):
                    last = pe.matmul(out_, a, b, start=(i == 0), stop=(i == len(terms) - 1))
                return last

            pe.wait_ge(ident_made, 1)
            pe.wait_ge(ident16_made, 1)

            def prepare(kind, k):
                i = prep_at[kind, k]
                prep_free(pe, i)
                dst = prep_bank(i)
                if kind == "wd":
                    if k == 0:
                        pe.wait_ge(wd_loaded, 16 * 4)
                        pe.wait_ge(kr_scaled, 1)
                    for r, rows in enumerate((P, P, ROPE)):
                        last = pe.transpose(dst[:, P * r:P * r + rows], wd_n[0:rows, r, tok(k)],
                                            ident[0:rows, 0:rows])
                elif kind in ("ma", "mb"):
                    pe.wait_ge(wq_loaded, 16 * 3)
                    rows, cols = (P, slice(0, P)) if kind == "ma" else (QB, slice(P, QC))
                    for h in range(8):
                        last = pe.matmul(dst[0:rows, KVC * h:KVC * (h + 1)], wqn[:, 8 * k + h, cols],
                                         wkn[:, 8 * k + h, :], start=True, stop=True)
                elif kind in ("ra", "rb"):
                    rows, cols = (P, slice(0, P)) if kind == "ra" else (QB, slice(P, QC))
                    for j in range(4):
                        last = pe.transpose(dst[0:rows, P * j:P * (j + 1)], wqr[:, 4 * k + j, cols], ident[:])
                elif kind == "ub":
                    pe.wait_ge(vec_loaded, 16 * 2)
                    last = pe.transpose(dst[:, 0:FT], ub_n[:], ident[0:FT, 0:FT])
                elif kind == "wo":
                    pe.wait_ge(wo_loaded[k // 2 % 2], 16 * (k // 4 + 1))
                    for h in range(2):
                        for m in range(CT):
                            at = P * (2 * (k % 2) + h)
                            last = pe.transpose(dst[:, HID * h + P * m:HID * h + P * (m + 1)],
                                                wo_n[:, k // 2 % 2, m, at:at + P], ident[:])
                elif kind == "n":
                    pe.wait_ge(prep_act, prep_count(prep_at["wo", 2 * k + 1]))
                    pe.wait_ge(wv_loaded, 16)
                    for j in range(2):
                        for odd in range(2):
                            h = 2 * (2 * k + j) + odd
                            last = pe.matmul(dst[KVC * odd:KVC * (odd + 1), HID * j:HID * (j + 1)],
                                             wvn[:, h, :], woT[:, j, odd, :], start=True, stop=True)
                elif kind == "upT":
                    pe.wait_ge(up_loaded, 16)
                    for f in range(2):
                        for m in range(CT):
                            at = FF * m + P * (2 * k + f)
                            last = pe.transpose(dst[:, HID * f + P * m:HID * f + P * (m + 1)],
                                                w_nat[:, at:at + P], ident[:])
                elif kind == "upB":
                    pe.wait_ge(quantised, 1)
                    for f in range(FT):
                        at = HID * f + P * k
                        last = pe.transpose(dst[:].bitcast(BF16)[:, P * f:P * (f + 1)], w_16[:, at:at + P],
                                            ident16[:])
                elif kind == "dnT":
                    pe.wait_ge(dn_loaded, 16)
                    for f in range(4):
                        at = HID * (4 * (k % 2) + f) + P * (k // 2)
                        last = pe.transpose(dst[:, P * f:P * (f + 1)], w_nat[:, at:at + P], ident[:])
                else:
                    pe.wait_ge(quantised, 2)
                    for f in range(4):
                        for d in range(CT):
                            at = FF * d + P * (4 * k + f)
                            to = HID * f + P * d
                            last = pe.transpose(dst[:].bitcast(BF16)[:, to:to + P], w_16[:, at:at + P],
                                                ident16[:])
                last.then_inc(prep_filled, 1)

            def job(n, j):
                kind, k = j
                if j in FRONT:
                    free_front(pe, n, j)
                    dst = front_bank(n, j)
                    if kind == "xT":
                        pe.wait_ge(xn_ready, n.at(QT, QT))
                        for t in range(QT):
                            for m in range(CT):
                                last = pe.transpose(dst[:, S * m + P * t:S * m + P * (t + 1)],
                                                    xn[:, t, tok(m)], ident[:])
                    elif kind == "D":
                        pe.wait_ge(front_act, n.at(NF, 1))
                        last = pairs(dst[:, 0:DOWN], [(xT[:, m, tok(k)], wdT[:, m, :]) for m in range(CT)])
                    elif kind == "KT":
                        pe.wait_ge(latents_ready, n.at(QT, QT))
                        pe.wait_ge(kr_ready, n.at(QT, QT))
                        for t in range(QT):
                            last = pe.transpose(dst[:, tok(t)], kt[:, t, :], ident[:])
                    elif kind == "cT":
                        for t in range(QT):
                            pe.transpose(dst[:, tok(t)], cq[:, t, 0:P], ident[:])
                            last = pe.transpose(dst[0:QB, S + P * t:S + P * (t + 1)], cq[:, t, P:QC], ident[:])
                    elif kind == "Q":
                        g, t = k // 2, k % 2
                        if k == 0:
                            pe.wait_ge(front_dve, n.at(NFD, FRONT_DVE.index(("cT", 0)) + 1))
                        if n.first() and t == 0:
                            pe.wait_ge(w_split, g + 1)
                        cols = slice(512 * g, 512 * (g + 1))
                        last = pairs(dst[:], [(ca_hi[:, tok(t)], wa_hi[:, cols]),
                                              (ca_hi[:, tok(t)], wa_lo[:, cols]),
                                              (ca_lo[:, tok(t)], wa_hi[:, cols]),
                                              (cb[:, tok(t)], wb_hh[:, cols]),
                                              (cb[0:QB, tok(t)], wb_lo[:, cols])])
                    else:
                        pe.wait_ge(qtok_ready, n.at(8, k + 1))
                        for h in range(QUAD):
                            last = pe.transpose(dst[:, tok(h)], qtok[k % 4][:, h, :], ident[:])
                    last.then_inc(front_filled, 1)
                else:
                    free_back(pe, n, j)
                    if kind == "OT":
                        t, half = k % 2, k // 2
                        if t == 0:
                            pe.wait_ge(o_ready, n.at(NQ, 2 * half + 2))
                        for i in range(4):
                            h = 8 * half + 2 * i
                            last = pe.transpose(b_bank[:, tok(i)],
                                                otok[:, t, h:h + 2, :].rearrange("p h c -> p (h c)"), ident[:])
                    elif kind == "proj":
                        if n.first():
                            pe.wait_ge(n_split, 1)
                        for t in range(QT):
                            last = pairs(b_bank[:, HID * t:HID * (t + 1)],
                                         [(a[:, i, tok(t)], w[:, i, :]) for i in range(PAIRS)
                                          for a, w in ((ot_hi, n_hi), (ot_hi, n_lo), (ot_lo, n_hi))])
                    elif kind == "x2T":
                        pe.wait_ge(x2n_ready, n.at(QT, QT))
                        for t in range(QT):
                            for m in range(CT):
                                last = pe.transpose(b_bank[:, S * m + P * t:S * m + P * (t + 1)],
                                                    x2n[:, t, tok(m)], ident[:])
                    elif kind == "up":
                        for i in range(2):
                            f = 2 * k + i
                            last = pairs(b_bank[:, S * i:S * (i + 1)],
                                         [(up_q[:, m, tok(f)], a[:, m, :]) for m in range(CT)
                                          for a in (x2_hi, x2_lo)])
                    else:
                        pe.wait_ge(g_ready, n.at(4, 4))
                        for t in range(QT):
                            last = pairs(b_bank[:, HID * t:HID * (t + 1)],
                                         [(a[:, f, tok(t)], dn_q[:, f, :]) for f in range(FT)
                                          for a in (g_hi, g_lo)])
                    last.then_inc(back_filled, 1)

            def logits(n, h):
                if h % QUAD == 0:
                    pe.wait_ge(front_dve, n.at(NFD, FRONT_DVE.index(("QT", 2 * (h // QUAD) + 1)) + 1))
                wait(pe, probs_ready, n.at(NH, h - 1))
                p = n.parity
                for t in range(QT):
                    last = pairs(l_bank[h % 2][:, S * t:S * (t + 1)],
                                 [(q_hi[p][:, h, tok(t)], k_hi[p][:]), (q_hi[p][:, h, tok(t)], k_lo[p][:]),
                                  (q_lo[p][:, h, tok(t)], k_hi[p][:])])
                last.then_inc(logits_ready, 1)

            def transpose_probs(n, h):
                pe.wait_ge(probs_ready, n.at(NH, h + 1))
                wait(pe, pt_lo_ready, n.at(NH, h - 1))
                for t in range(QT):
                    for k in range(QT):
                        last = pe.transpose(t_bank[h % 2][:, S * k + P * t:S * k + P * (t + 1)],
                                            pr[h % 2][:, t, tok(k)], ident[:])
                last.then_inc(probsT_ready, 1)

            def values(n, h):
                pe.wait_ge(pt_lo_ready, n.at(NH, h + 1))
                if h == 0:
                    pe.wait_ge(c_ready, n.at(QT, QT))
                if h % QUAD == 0:
                    wait(pe, o_ready, n.at(NQ, h // QUAD))
                p = n.parity
                for t in range(QT):
                    at = KVC * (2 * (h % QUAD) + t)
                    last = pairs(o_bank[:, at:at + KVC],
                                 [(w[h % 2][:, k, tok(t)], c[p][:, k, :]) for k in range(QT)
                                  for w, c in ((pt_hi, c_hi), (pt_hi, c_lo), (pt_lo, c_hi))])
                last.then_inc(pv_done, 1)

            for k in range(CT):
                prepare("wd", k)
            for j in FRONT[:3]:
                job(Batch(0), j)
            for kind in ("ma", "mb", "ra", "rb"):
                for k in range(2):
                    prepare(kind, k)
            prepare("ub", 0)
            for j in FRONT[3:]:
                job(Batch(0), j)
            logits(Batch(0), 0)

            def iteration(b, front, back):
                for h in range(NH):
                    if h + 1 < NH or front:
                        logits(b, h + 1) if h + 1 < NH else logits(b.plus(1), 0)
                    for i, part in enumerate(SLOTS[h]):
                        if b.first():
                            for kind, k in PREP_SLOTS[h][i]:
                                if kind in PREP_ROLES:
                                    prepare(kind, k)
                        for j in part:
                            if j in FRONT and front:
                                job(b.plus(1), j)
                            if j in BACK and back:
                                job(b.plus(-1), j)
                        if i == 0:
                            transpose_probs(b, h)
                    if h or back:
                        values(b, h - 1) if h else values(b.plus(-1), NH - 1)

            iteration(Batch(0), True, False)
            iteration(Batch(1), True, True)
            with pe.Fori(0, B // 2 - 2) as pair:
                iteration(Batch(2, pair), True, True)
                iteration(Batch(3, pair), True, True)
            iteration(Batch(B - 2), True, True)
            iteration(Batch(B - 1), False, True)
            values(Batch(B - 1), NH - 1)
            for j in BACK:
                job(Batch(B - 1), j)


_NAMES = ["L0_attn_x", "L0_attn_w_q_down", "L0_attn_q_norm_w", "L0_attn_w_q_nope", "L0_attn_w_q_rope",
          "L0_attn_w_kv_down", "L0_attn_kv_norm_w", "L0_attn_w_k_nope", "L0_attn_w_v_up", "L0_attn_w_k_rope",
          "L0_attn_w_o", "L0_ffn_up_kernel", "L0_ffn_up_bias", "L0_ffn_down_kernel", "L0_ffn_down_bias"]


def _rope_table():
    import numpy as np
    inv = (np.float32(1.0) / np.power(np.float32(10000.0), np.arange(0, ROPE, 2, dtype=np.float32)
                                      / np.float32(ROPE))).astype(np.float32)
    f = np.arange(S, dtype=np.float32)[:, None] * inv[None, :]
    c, s = np.cos(f).astype(np.float32), np.sin(f).astype(np.float32)
    return np.stack([np.concatenate([c, c], 1), np.concatenate([-s, s], 1)], 1)


def kernel(**inputs):
    import numpy as np
    import concourse.bacc as bacc
    from concourse.bass_utils import run_bass_kernel_spmd

    nc = bacc.Bacc("TRN2", target_bir_lowering=False, num_devices=1)
    arrays, args = {}, []
    for name in _NAMES:
        a = np.ascontiguousarray(inputs[name])
        arrays[name + "_in"] = a
        args.append(nc.dram_tensor(name + "_in", a.shape, mybir.dt.from_np(a.dtype), kind="ExternalInput").ap())
    table = _rope_table()
    arrays["rope_table"] = table
    args.append(nc.dram_tensor("rope_table", table.shape, F32, kind="ExternalInput").ap())
    args.append(nc.dram_tensor("out", (B, S, HID), F32, kind="ExternalOutput").ap())
    build(nc, *args)
    r = run_bass_kernel_spmd(nc, [arrays], core_ids=[0])
    return r.results[0]["out"]
```

```python
import math
from contextlib import ExitStack

import concourse.bass as bass
from concourse import mybir

F32, F16, BF16, I32 = mybir.dt.float32, mybir.dt.float16, mybir.dt.bfloat16, mybir.dt.int32
ALU, ACT, AX = mybir.AluOpType, mybir.ActivationFunctionType, mybir.AxisListType

P = 128
B, S, HID = 16, 256, 256
NH, NOPE, ROPE, VD = 16, 128, 64, 128
QC, KVC, FF = 192, 64, 1024
HD = KVC + ROPE
QT = S // P
CT = HID // P
QB = QC - P
QUAD = 4
NQ = NH // QUAD
PAIRS = NH // 2
FT = FF // P
BLOCK = 32
DOWN = QC + KVC + ROPE
SCALE = (NOPE + ROPE) ** -0.5
LN_EPS, RMS_EPS = 1e-5, 1e-6
UP = 64.0
WMAX = 2.0 ** 7
PLIFT = 2.0 ** 14
MIDPOINTS = (5.0, 3.5, 2.5, 1.75, 1.25, 0.75, 0.25)
GELU_C = math.sqrt(2.0 / math.pi)
GELU_A = 0.044715

SLOTS = [
    ([("OT", 0)], [("ln1", 0)]),
    ([("QT", 6)], []),
    ([("ln1x", 0)], [("OT", 1)]),
    ([("QT", 7)], []),
    ([("xT", 0), ("OT", 3)], [("D", 0)]),
    ([("OT", 2), ("D", 1), ("scale", 0)], [("scale", 1)]),
    ([("projA", 0)], []),
    ([("cT", 0), ("proj", 0)], [("ln2", 0), ("KT", 0)]),
    ([("Q", 0)], []),
    ([("x2T", 0), ("Q", 1)], [("up", 0), ("QT", 0), ("split", 0)]),
    ([("up", 1), ("Q", 2), ("gelu", 0)], [("QT", 1), ("up", 2)]),
    ([("gelu", 1), ("Q", 3), ("split", 1)], []),
    ([("QT", 2), ("up", 3), ("split", 2), ("gelu", 2)], [("Q", 4)]),
    ([("Q", 5), ("QT", 3), ("gelu", 3), ("split", 3)], [("Q", 6)]),
    ([("Q", 7), ("QT", 4), ("downA", 0), ("down", 0)], []),
    ([("QT", 5)], []),
]
OWN = (("QT", 6), ("QT", 7))
PREP_SLOTS = [
    ([("dnT", 0), ("dnT", 1), ("dnT", 2)], []),
    ([("values", 0)], []),
    ([("dnT", 3), ("upB", 0)], [("upB", 1)]),
    ([("blocks", 1)], [("wo", 0), ("wo", 1)]),
    ([], [("abs", 1), ("levels", 7), ("n", 0), ("levels", 8), ("levels", 9)]),
    ([], [("wo", 2), ("wo", 3)]),
    ([("n", 1)], [("levels", 10), ("levels", 11)]),
    ([], [("levels", 12)]),
    ([("wo", 4), ("wo", 5), ("levels", 13)], [("n", 2)]),
    ([("values", 1), ("wo", 6), ("wo", 7)], []),
    ([("dnB", 0)], []),
    ([("bound", 0)], []),
    ([], [("n", 3), ("nscale", 0)]),
    ([], []),
    ([("dnB", 1)], []),
    ([], []),
]
PROLOGUE = [
    "front", ("wd", 0), "front", "front", ("wd", 1), "front", "front", ("mb", 0), "front", ("ra", 0), ("mb", 1),
    ("rb", 0), "front", ("ma", 0), ("ra", 1), ("ma", 1), ("rb", 1), ("wscale", 0), "front", ("upT", 0),
    ("wsplit", 0), ("upT", 1), "front", ("wsplit", 1), "front", ("upT", 2), ("upT", 3), "front", ("blocks", 0),
    "front", ("wsplit", 2), "front", ("wsplit", 3), "front", ("abs", 0), ("levels", 0), ("levels", 1),
    ("levels", 2), "front", "front", ("levels", 3), "front", "front", "front", "front", ("levels", 4),
    ("levels", 5), "front", ("levels", 6), ("ub", 0), "front", "front",
]
PREP_ROLES = ("wd", "ma", "mb", "ra", "rb", "ub", "upT", "wo", "n", "upB", "dnT", "dnB")
FRONT = [j for s in SLOTS for part in s for j in part
         if j[0] in ("xT", "D", "KT", "cT", "Q", "QT") and j not in OWN] + list(OWN)
BACK = [j for s in SLOTS for part in s for j in part if j[0] in ("OT", "proj", "x2T", "up", "down")]
FRONT_TASKS = ("ln1", "ln1x", "xT", "D", "scale", "KT", "cT", "Q", "QT")
ACT_LAST = ("xT", "D", "Q", "up")
FRONT_DVE = [j for j in FRONT if j[0] not in ACT_LAST]
BACK_ACT = [j for j in BACK if j[0] not in ("proj", "down")]
BACK_DVE = [j for j in BACK if j[0] not in ACT_LAST]
NF, NFD, NB_, NBA, NBD = len(FRONT), len(FRONT_DVE), len(BACK), len(BACK_ACT), len(BACK_DVE)


class Batch:

    def __init__(self, const, pair=None):
        self.const, self.pair, self.parity = const, pair, const % 2

    def plus(self, d):
        return Batch(self.const + d, self.pair)

    def at(self, per, extra):
        v = per * self.const + extra
        return v if self.pair is None else self.pair * (2 * per) + v

    def first(self):
        return self.pair is None and self.const == 0

    def real(self):
        return self.pair is not None or 0 <= self.const < B


def part(b, slot, i):
    if slot < 0:
        b, slot = b.plus(-1), NH - 1
    jobs = []
    if b.pair is None and b.const < 0:
        return jobs
    for j in SLOTS[slot][i]:
        n = b if j in OWN else b.plus(1) if j[0] in FRONT_TASKS else b.plus(-1)
        if n.real():
            jobs.append((n, j))
    return jobs


def prologue():
    front = iter([j for slot in SLOTS for part in slot for j in part
                  if j[0] in FRONT_TASKS and j not in OWN])
    return [(Batch(0), next(front)) if j == "front" else (None, j) for j in PROLOGUE]


def head(b, h):
    n, h = (b, h) if h >= 0 else (b.plus(-1), h + NH)
    return (n, h) if n.real() else None


def preparations(b, slot, i):
    if slot < 0:
        b, slot = b.plus(-1), NH - 1
    return PREP_SLOTS[slot][i] if b.first() else []


def wait(eng, sem, value):
    if isinstance(value, int) and value <= 0:
        return
    eng.wait_ge(sem, value)


def build(nc, x, w_q_down, q_norm_w, w_q_nope, w_q_rope, w_kv_down, kv_norm_w, w_k_nope, w_v_up,
          w_k_rope, w_o, up_kernel, up_bias, down_kernel, down_bias, rope_table, out):
    ctx = ExitStack()
    with ctx:
        def sb(name, shape, dt=F32):
            return ctx.enter_context(nc.sbuf_tensor(name, shape, dt))

        def sem(name):
            return ctx.enter_context(nc.semaphore(name))

        ident = sb("ident", [P, P])
        ident16 = sb("ident16", [P, P], BF16)
        rope = sb("rope", [P, QT, 2, ROPE])
        wdT = sb("wdT", [P, CT, DOWN])
        wa_hi = sb("wa_hi", [P, NH * HD], F16)
        wa_lo = sb("wa_lo", [P, NH * HD], F16)
        wb_hh = sb("wb_hh", [P, NH * HD], F16)
        wb_lo = sb("wb_lo", [QB, NH * HD], F16)
        n_hi = sb("n_hi", [P, PAIRS, HID], F16)
        n_lo = sb("n_lo", [P, PAIRS, HID], F16)
        up_q = sb("up_q", [P, CT, FF], BF16)
        dn_q = sb("dn_q", [P, FT, HID], BF16)
        ub = sb("ub", [P, FT])
        db = sb("db", [P, HID])
        small = sb("small", [P, 64])
        inv_kr, inv_s, inv_n, s_g, inv_g = (small[:, i:i + 1] for i in range(5))
        ln_eps, rms_eps, neg_half = (small[:, 8 + 2 * i:10 + 2 * i] for i in range(3))

        xf = sb("xf", [P, QT, HID])
        xb = sb("xb", [P, QT, HID])
        nothing = sb("nothing", [P, 1])
        st = sb("st", [P, 2, QT, 6])
        mv = sb("mv", [P, 2, QT, 2])
        va = sb("va", [P, 2, QT])
        rstd = sb("rstd", [P, 2, QT])
        xn = sb("xn", [P, QT, HID])
        xT = sb("xT", [P, CT, S])
        raw = sb("raw", [P, QT, DOWN])
        sq = sb("sq", [P, QT, QC + KVC])
        ssq = sb("ssq", [P, QT, 2])
        sse = sb("sse", [P, QT, 2])
        rms = sb("rms", [P, QT, 2])
        cq = sb("cq", [P, QT, QC])
        kt = sb("kt", [P, QT, HD])
        kr = sb("kr", [P, 2, ROPE])
        c_hi = [sb(f"c_hi{i}", [P, QT, KVC], F16) for i in range(2)]
        c_lo = [sb(f"c_lo{i}", [P, QT, KVC], F16) for i in range(2)]
        k_hi = [sb(f"k_hi{i}", [P, S], F16) for i in range(2)]
        k_lo = [sb(f"k_lo{i}", [P, S], F16) for i in range(2)]
        ca_hi = sb("ca_hi", [P, S], F16)
        ca_lo = sb("ca_lo", [P, S], F16)
        cb = sb("cb", [P, S], F16)
        qtok = [sb(f"qtok{i}", [P, QUAD, HD]) for i in range(4)]
        qr = [sb(f"qr{i}", [P, 2, QUAD, ROPE]) for i in range(2)]
        nmax = sb("nmax", [P, 2, QT])
        ebias = sb("ebias", [P, 2, QT])
        rsum = sb("rsum", [P, NH, QT])
        rinv = sb("rinv", [P, NH, QT])
        pr = [sb(f"pr{i}", [P, QT, S]) for i in range(2)]
        pt_hi = [sb(f"pt_hi{i}", [P, QT, S], F16) for i in range(2)]
        pt_lo = [sb(f"pt_lo{i}", [P, QT, S], F16) for i in range(2)]
        x1 = sb("x1", [P, QT, HID])
        x1b = sb("x1b", [P, QT, HID])
        x2n = sb("x2n", [P, QT, HID])
        x2_hi = sb("x2_hi", [P, CT, S], F16)
        x2_lo = sb("x2_lo", [P, CT, S], F16)
        gu = [sb(f"gu{i}", [P, 2, S]) for i in range(2)]
        gv = sb("gv", [P, 2, S])
        gw = sb("gw", [P, 2, S])
        gz = sb("gz", [P, 2, S])
        gt = sb("gt", [P, 2, S])
        ob = sb("ob", [P, QT, HID])

        late = sb("late", [P, 10240])
        q_hi0, q_lo0 = sb("q_hi0", [P, NH, S], F16), sb("q_lo0", [P, NH, S], F16)

        def carve(at, n, dt=F32):
            a = late[:, at:at + n]
            return a if dt is F32 else a.bitcast(dt)

        q_hi = [q_hi0, carve(0, 2048, F16).rearrange("p (h s) -> p h s", h=NH)]
        q_lo = [q_lo0, carve(2048, 2048, F16).rearrange("p (h s) -> p h s", h=NH)]
        otok = carve(4096, 2 * NH * KVC).rearrange("p (t h c) -> p t h c", t=QT, h=NH)
        ot_hi = carve(6144, 1024, F16).rearrange("p (j s) -> p j s", j=PAIRS)
        ot_lo = carve(7168, 1024, F16).rearrange("p (j s) -> p j s", j=PAIRS)
        g_hi = carve(8192, 1024, F16).rearrange("p (f s) -> p f s", f=FT)
        g_lo = carve(9216, 1024, F16).rearrange("p (f s) -> p f s", f=FT)
        wf_a = carve(0, 2048).rearrange("p (h c) -> p h c", h=NH)
        wf_b = carve(2048, 2048).rearrange("p (h c) -> p h c", h=NH)
        wvn = carve(6144, 1024).rearrange("p (h c) -> p h c", h=NH)
        woT = carve(7168, 1024).rearrange("p (k h c) -> p k h c", k=2, h=2)
        nf = carve(8192, 2048).rearrange("p (j c) -> p j c", j=PAIRS)
        wo_n = sb("wo_n", [P, 2, CT, 4 * VD])

        quant = sb("quant", [P, 8192])
        wqn = quant[:, 0:3072].rearrange("p (h c) -> p h c", h=NH)
        wkn = quant[:, 3072:4096].rearrange("p (h c) -> p h c", h=NH)
        wqr = quant[:, 4096:5632].rearrange("p (j c) -> p j c", j=PAIRS)
        w_nat = quant[:, 0:2048]
        w_T = quant[:, 2048:4096]
        w_c = quant[:, 4096:6144]
        w_x = quant[:, 6144:8192]
        w_16 = sb("w_16", [P, 2048], BF16)
        blk = sb("blk", [P, 4, 64])
        ub_n = sb("ub_n", [FT, P])
        gelu_k = sb("gelu_k", [P, 1])
        wd_n = sb("wd_n", [P, 3, HID])
        qn_a, qn_b = small[:, 16:17], small[0:QB, 17:18]
        qs_a, qs_b = small[:, 18:19], small[0:QB, 19:20]
        qr_a, qr_b = small[:, 20:21], small[0:QB, 21:22]
        kvn_c = small[:, 22:23]
        kvn_r = sb("kvn_r", [P, KVC])
        mx = sb("mx", [P, 16])

        bank = [ctx.enter_context(nc.psum_tensor(f"bank{i}", [P, 512], F32)) for i in range(8)]
        l_bank, t_bank, o_bank, f_bank, b_bank = bank[0:2], bank[2:4], bank[4], bank[5:7], bank[7]

        ident_zeroed, ident_made, ident16_made = sem("ident_zeroed"), sem("ident_made"), sem("ident16_made")
        wd_loaded, wq_loaded, wv_loaded = sem("wd_loaded"), sem("wq_loaded"), sem("wv_loaded")
        wo_loaded = [sem(f"wo_loaded{i}") for i in range(2)]
        norms_loaded, vec_loaded, rope_loaded = sem("norms_loaded"), sem("vec_loaded"), sem("rope_loaded")
        up_loaded, dn_loaded = sem("up_loaded"), sem("dn_loaded")
        consts_set = sem("consts_set")
        prep_filled, prep_act, prep_dve = sem("prep_filled"), sem("prep_act"), sem("prep_dve")
        prep_step = sem("prep_step")
        max_asked, max_given = sem("max_asked"), sem("max_given")
        kr_scaled, norms_scaled, w_scaled, w_high, w_split = (
            sem(n) for n in ("kr_scaled", "norms_scaled", "w_scaled", "w_high", "w_split"))
        blocks_ready, x_scaled, x_abs, sign_ready, step_ready, quantised, n_split = (
            sem(n) for n in ("blocks_ready", "x_scaled", "x_abs", "sign_ready", "step_ready", "quantised",
                             "n_split"))
        xf_loaded = sem("xf_loaded")
        xb_loaded = sem("xb_loaded")
        ln_stats = [sem("ln1_stats"), sem("ln2_stats")]
        ln_aggr = [sem("ln1_aggr"), sem("ln2_aggr")]
        ln_eps_added = [sem("ln1_eps_added"), sem("ln2_eps_added")]
        ln_rstd = [sem("ln1_rstd"), sem("ln2_rstd")]
        xn_ready, x2n_ready = sem("xn_ready"), sem("x2n_ready")
        front_filled, front_act, front_dve = sem("front_filled"), sem("front_act"), sem("front_dve")
        back_filled, back_act, back_dve = sem("back_filled"), sem("back_act"), sem("back_dve")
        rms_eps_added, rms_ready = sem("rms_eps_added"), sem("rms_ready")
        kr_parts, kr_ready = sem("kr_parts"), sem("kr_ready")
        latents_ready, c_hi_ready, c_ready = sem("latents_ready"), sem("c_hi_ready"), sem("c_ready")
        qr_parts, qtok_ready = sem("qr_parts"), sem("qtok_ready")
        logits_ready, max_found, bias_ready = sem("logits_ready"), sem("max_found"), sem("bias_ready")
        probs_ready, probsT_ready = sem("probs_ready"), sem("probsT_ready")
        pt_hi_ready, pt_lo_ready = sem("pt_hi_ready"), sem("pt_lo_ready")
        pv_done, rinv_ready, o_ready = sem("pv_done"), sem("rinv_ready"), sem("o_ready")
        x1_ready, x1b_ready = sem("x1_ready"), sem("x1b_ready")
        gv_ready, gw_ready, gz_ready, gt_ready, g_raw, g_hi_ready, g_ready = (
            sem(n) for n in ("gv_ready", "gw_ready", "gz_ready", "gt_ready", "g_raw", "g_hi_ready", "g_ready"))
        ob_ready, stored = sem("ob_ready"), sem("stored")

        block = ctx.enter_context(nc.Block())

        prep = [j for j in PROLOGUE if j[0] in PREP_ROLES]
        early = len(prep)
        prep += [j for slot in PREP_SLOTS for part in slot for j in part if j[0] in PREP_ROLES]
        prep = [(kind, k, "dve" if kind in ("ma", "mb") else "act") for kind, k in prep]
        prep_at = {(j[0], j[1]): i for i, j in enumerate(prep)}
        prep_banks = [bank[i] for i in (0, 1, 2, 3, 4, 7)]

        def prep_bank(i):
            return prep_banks[i % 6] if i < early else b_bank

        def before(i):
            if i < early:
                return i - 6 if i >= 6 else None
            return i - 1 if i > early else early - 1 - (early - 1 - 5) % 6

        def prep_count(i):
            return sum(j[2] == prep[i][2] for j in prep[:i + 1])

        def prep_free(pe, i):
            if before(i) is not None:
                pe.wait_ge(prep_act if prep[before(i)][2] == "act" else prep_dve, prep_count(before(i)))

        def front_bank(n, j):
            return f_bank[(NF * n.parity + FRONT.index(j)) % 2]

        def free_front(pe, n, j):
            k = FRONT.index(j) - 2
            m = n if k >= 0 else n.plus(-1)
            if m.pair is None and m.const < 0:
                return
            old = FRONT[k]
            if old[0] in ACT_LAST:
                pe.wait_ge(front_act, m.at(NF, FRONT.index(old) + 1))
            else:
                pe.wait_ge(front_dve, m.at(NFD, FRONT_DVE.index(old) + 1))

        def free_back(pe, n, j):
            k = BACK.index(j) - 1
            m = n if k >= 0 else n.plus(-1)
            if m.pair is None and m.const < 0:
                pe.wait_ge(prep_act, prep_count(len(prep) - 1))
                return
            old = BACK[k]
            if old[0] in ACT_LAST:
                pe.wait_ge(back_act, m.at(NBA, BACK_ACT.index(old) + 1))
            else:
                pe.wait_ge(back_dve, m.at(NBD, BACK_DVE.index(old) + 1))

        def flat(a):
            return a.rearrange("p a b -> p (a b)")

        def blocks_of(a):
            return a.rearrange("p (n e) -> p n e", e=BLOCK)

        def spread(v):
            return v.unsqueeze(2).to_broadcast([P, 2048 // BLOCK, BLOCK])

        s_w = small[:, 33:34]

        def run_prologue(task, prep_task):
            for n, j in prologue():
                if n:
                    task(n, j)
                else:
                    prep_task(j)

        def tok(t):
            return slice(t * P, (t + 1) * P)

        xr = x.rearrange("b (t p) c -> b p t c", p=P)
        outr = out.rearrange("b (t p) c -> b p t c", p=P)

        def dram(a, n):
            if n.pair is None:
                return a[n.const]
            return a[bass.ds(n.pair * 2 + n.const, 1)].rearrange("o p t c -> p (o t) c")

        @block.sync
        def _(sp):
            def load_front(n):
                wait(sp, xn_ready, n.at(QT, 0))
                sp.dma_start(xf[:], dram(xr, n)).then_inc(xf_loaded, 16)

            def load_back(n):
                wait(sp, x1_ready, n.at(1, 0))
                sp.dma_start(xb[:], dram(xr, n)).then_inc(xb_loaded, 16)

            def store(n):
                sp.wait_ge(ob_ready, n.at(1, 1))
                sp.dma_start(dram(outr, n), ob[:]).then_inc(stored, 16)

            sp.dma_start(wd_n[0:ROPE, 2, :], w_k_rope).then_inc(wd_loaded, 16)
            sp.dma_start(wd_n[:, 0, :], w_q_down[0:P, :]).then_inc(wd_loaded, 16)
            sp.dma_start(wd_n[0:QB, 1, :], w_q_down[P:QC, :]).then_inc(wd_loaded, 16)
            sp.dma_start(wd_n[QB:P, 1, :], w_kv_down).then_inc(wd_loaded, 16)
            sp.dma_start(wqn, w_q_nope.rearrange("(h p) c -> p h c", p=P)).then_inc(wq_loaded, 16)
            sp.dma_start(wkn, w_k_nope.rearrange("(h p) c -> p h c", p=P)).then_inc(wq_loaded, 16)
            sp.dma_start(wqr, w_q_rope.rearrange("(j p) c -> p j c", p=P)).then_inc(wq_loaded, 16)
            sp.dma_start(kvn_c[0:KVC], kv_norm_w.unsqueeze(1)).then_inc(vec_loaded, 16)
            sp.dma_start(kvn_c[KVC:P], kv_norm_w.unsqueeze(1)).then_inc(vec_loaded, 16)
            sp.dma_start(ub_n[:], up_bias.rearrange("(f p) -> f p", p=P)).then_inc(vec_loaded, 16)
            sp.dma_start(db[:], down_bias.unsqueeze(0).to_broadcast([P, HID])).then_inc(vec_loaded, 16)
            sp.wait_ge(prep_filled, prep_at["rb", 1] + 1)
            sp.dma_start(w_nat.rearrange("p (m f) -> p m f", m=CT),
                         up_kernel.rearrange("(m p) f -> p m f", p=P)).then_inc(up_loaded, 16)
            sp.dma_start(wvn, w_v_up.rearrange("(h p) c -> p h c", p=P)).then_inc(wv_loaded, 16)
            wo_r = w_o.rearrange("(m p) d -> p m d", p=P)

            def load_wo(k):
                sp.dma_start(wo_n[:, k % 2], wo_r[:, :, 512 * k:512 * (k + 1)]).then_inc(wo_loaded[k % 2], 16)

            load_wo(0)
            load_wo(1)
            load_front(Batch(1))
            sp.wait_ge(prep_filled, prep_at["upT", 3] + 1)
            sp.dma_start(w_nat.rearrange("p (m d) -> p m d", m=FT),
                         down_kernel.rearrange("(m p) d -> p m d", p=P)).then_inc(dn_loaded, 16)
            for k in (2, 3):
                sp.wait_ge(prep_filled, prep_at["wo", 2 * k - 3] + 1)
                load_wo(k)

            def iteration(b):
                if b.plus(1).real():
                    load_front(b.plus(1))
                load_back(b.plus(-1))
                store(b.plus(-1))

            iteration(Batch(1))
            with sp.Fori(0, B // 2 - 2) as pair:
                iteration(Batch(2, pair))
                iteration(Batch(3, pair))
            for b in range(B - 2, B + 1):
                iteration(Batch(b))
            sp.wait_ge(stored, 16 * B)

        @block.gpsimd
        def _(pool):
            pool.memset(ident[:], 0.0).then_inc(ident_zeroed, 1)
            pool.wait_ge(ident_zeroed, 1)
            pool.affine_select(out=ident[:], in_=ident[:], compare_op=ALU.not_equal, fill=1.0, base=0,
                               pattern=[[-1, P]], channel_multiplier=1).then_inc(ident_made, 1)
            for ap, v in ((ln_eps, LN_EPS), (rms_eps, RMS_EPS), (neg_half, -0.5), (gelu_k[:], 1.0 / GELU_A)):
                pool.memset(ap, v).then_inc(consts_set, 1)

            def maximum(k):
                pool.wait_ge(max_asked, k + 1)
                pool.partition_all_reduce(mx[:, 2 * k + 8:2 * k + 10], mx[:, 2 * k:2 * k + 2], P,
                                          bass.bass_isa.ReduceOp.max).then_inc(max_given, 1)

            def prep_task(j):
                kind, k = j
                if kind == "wscale":
                    maximum(1)
                elif kind == "bound":
                    maximum(2)
                elif kind == "nscale":
                    maximum(3)
                elif kind == "blocks":
                    pool.wait_ge(blocks_ready, k + 1)
                    pool.tensor_tensor(blocks_of(w_x), blocks_of(w_T), spread(blk[:, 2, :]),
                                       ALU.mult).then_inc(x_scaled, 1)
                    pool.wait_ge(sign_ready, k + 1)
                    pool.tensor_tensor(blocks_of(w_16[:]), blocks_of(w_16[:]), spread(blk[:, 3, :]),
                                       ALU.mult).then_inc(step_ready, 1)

            def ln(n, which):
                pool.wait_ge(ln_aggr[which], n.at(QT, QT))
                pool.tensor_tensor(va[:, which, :], mv[:, which, :, 1], ln_eps,
                                   ALU.add).then_inc(ln_eps_added[which], 1)
                pool.wait_ge(ln_eps_added[which], n.at(1, 1))
                pool.tensor_tensor(rstd[:, which, :], va[:, which, :], neg_half,
                                   ALU.pow).then_inc(ln_rstd[which], 1)

            def task(n, j):
                kind, k = j
                if kind == "ln1" or kind == "ln2":
                    if kind == "ln2":
                        pool.wait_ge(x1_ready, n.at(1, 1))
                        if not n.first():
                            pool.wait_ge(ob_ready, n.at(1, 0))
                        pool.tensor_tensor(x1b[:], x1[:], db[:].unsqueeze(1).to_broadcast([P, QT, HID]),
                                           ALU.add).then_inc(x1b_ready, 1)
                    ln(n, int(kind == "ln2"))
                elif kind == "D":
                    pool.wait_ge(front_act, n.at(NF, FRONT.index(j) + 1))
                    pool.tensor_tensor(sse[:, k, :], ssq[:, k, :], rms_eps, ALU.add).then_inc(rms_eps_added, 1)
                    pool.wait_ge(rms_eps_added, n.at(QT, k + 1))
                    pool.tensor_tensor(rms[:, k, :], sse[:, k, :], neg_half, ALU.pow).then_inc(rms_ready, 1)
                    r = raw[:, k, QC + KVC:DOWN]
                    if n.first() and k == 0:
                        pool.wait_ge(rope_loaded, 16)
                    pool.tensor_tensor(kr[:, 0, :], r, rope[:, k, 0, :], ALU.mult).then_inc(kr_parts, 1)
                    h = ROPE // 2
                    pool.tensor_tensor(kr[:, 1, 0:h], r[:, h:ROPE], rope[:, k, 1, 0:h],
                                       ALU.mult).then_inc(kr_parts, 1)
                    pool.tensor_tensor(kr[:, 1, h:ROPE], r[:, 0:h], rope[:, k, 1, h:ROPE],
                                       ALU.mult).then_inc(kr_parts, 1)
                    pool.wait_ge(kr_parts, n.at(3 * QT, 3 * k + 3))
                    pool.tensor_tensor(kt[:, k, KVC:HD], kr[:, 0, :], kr[:, 1, :],
                                       ALU.add).then_inc(kr_ready, 1)
                elif kind == "Q":
                    pool.wait_ge(front_act, n.at(NF, FRONT.index(j) + 1))
                    q, t, hf = qtok[k % 4][:, :, KVC:HD], k % 2, ROPE // 2
                    cos, sin = rope[:, t, 0, :], rope[:, t, 1, :]
                    pool.tensor_tensor(qr[k % 2][:, 0], q, cos.unsqueeze(1).to_broadcast([P, QUAD, ROPE]),
                                       ALU.mult).then_inc(qr_parts, 1)
                    pool.tensor_tensor(qr[k % 2][:, 1, :, 0:hf], q[:, :, hf:ROPE],
                                       sin[:, 0:hf].unsqueeze(1).to_broadcast([P, QUAD, hf]),
                                       ALU.mult).then_inc(qr_parts, 1)
                    pool.tensor_tensor(qr[k % 2][:, 1, :, hf:ROPE], q[:, :, 0:hf],
                                       sin[:, hf:ROPE].unsqueeze(1).to_broadcast([P, QUAD, hf]),
                                       ALU.mult).then_inc(qr_parts, 1)
                    pool.wait_ge(qr_parts, n.at(24, 3 * k + 3))
                    pool.tensor_tensor(q, qr[k % 2][:, 0], qr[k % 2][:, 1], ALU.add).then_inc(qtok_ready, 1)
                elif kind == "up":
                    wait(pool, gt_ready, n.at(4, k))
                    u = gu[k % 2][:]
                    pool.wait_ge(gv_ready, n.at(4, k + 1))
                    pool.tensor_tensor(gw[:], gv[:], gelu_k[:].unsqueeze(1).to_broadcast([P, 2, S]),
                                       ALU.add).then_inc(gw_ready, 1)
                    pool.wait_ge(gw_ready, n.at(4, k + 1))
                    pool.tensor_tensor(gz[:], gw[:], u, ALU.mult).then_inc(gz_ready, 1)

            maximum(0)
            pool.wait_ge(consts_set, 4)
            run_prologue(task, prep_task)
            def iteration(b):
                for slot in range(NH):
                    for i in range(2):
                        for j in preparations(b, slot, i):
                            prep_task(j)
                        for n, j in part(b, slot, i):
                            task(n, j)

            pool.wait_ge(vec_loaded, 16 * 4)
            iteration(Batch(0))
            iteration(Batch(1))
            with pool.Fori(0, B // 2 - 2) as pair:
                iteration(Batch(2, pair))
                iteration(Batch(3, pair))
            for b in range(B - 2, B + 1):
                iteration(Batch(b))

        @block.scalar
        def _(act):
            act.dma_start(xf[:], dram(xr, Batch(0))).then_inc(xf_loaded, 16)
            act.dma_start(qn_a, q_norm_w[0:P].unsqueeze(1)).then_inc(norms_loaded, 16)
            act.dma_start(qn_b, q_norm_w[P:QC].unsqueeze(1)).then_inc(norms_loaded, 16)
            act.dma_start(kvn_r[:], kv_norm_w.unsqueeze(0).to_broadcast([P, KVC])).then_inc(norms_loaded, 16)
            act.dma_start(rope[:], rope_table.rearrange("(t p) w c -> p t w c", p=P)).then_inc(rope_loaded, 16)
            act.wait_ge(ident_made, 1)
            act.activation(ident16[:], ident[:], ACT.Copy).then_inc(ident16_made, 1)

            def read_out(kind, k):
                i = prep_at[kind, k]
                if prep[i][2] != "act":
                    return
                act.wait_ge(prep_filled, i + 1)
                src = prep_bank(i)
                if kind == "wd":
                    ins = act.activation(wdT[:, k, :], src[:, 0:DOWN], ACT.Copy)
                elif kind in ("ra", "rb"):
                    rows, s, dst = (P, qr_a, wf_a) if kind == "ra" else (QB, qr_b, wf_b)
                    act.wait_ge(norms_scaled, 1)
                    ins = act.activation(dst[0:rows, 8 * k:8 * k + 8, KVC:HD],
                                         src[0:rows].rearrange("p (h c) -> p h c", h=8), ACT.Copy, scale=s)
                elif kind == "ub":
                    ins = act.activation(ub[:], src[:, 0:FT], ACT.Copy)
                elif kind == "wo":
                    ins = act.activation(woT[:, k % 2].rearrange("p h c -> p (h c)"), src[:], ACT.Copy)
                elif kind == "n":
                    if k == 0:
                        act.wait_ge(vec_loaded, 16 * 4)
                    ins = act.activation(nf[:, 2 * k:2 * k + 2, :].rearrange("p j c -> p (j c)"), src[:],
                                         ACT.Copy, scale=kvn_c)
                elif kind in ("upT", "dnT"):
                    ins = act.activation(w_T[:, 512 * k:512 * (k + 1)], src[:], ACT.Copy)
                elif kind == "upB":
                    ins = act.activation(up_q[:, k, :], src[:].bitcast(BF16), ACT.Copy)
                else:
                    ins = act.activation(dn_q[:, 4 * k:4 * k + 4, :].rearrange("p f d -> p (f d)"),
                                         src[:].bitcast(BF16), ACT.Copy)
                ins.then_inc(prep_act, 1)

            def prep_task(j):
                kind, k = j
                if kind in PREP_ROLES:
                    read_out(kind, k)
                elif kind == "wsplit":
                    split_high(k)
                elif kind == "abs":
                    act.wait_ge(prep_act, prep_count(prep_at["upT" if k == 0 else "dnT", 3]))
                    if k:
                        act.wait_ge(prep_filled, prep_at["upB", CT - 1] + 1)
                    act.activation(w_16[:], w_T, ACT.Sign).then_inc(sign_ready, 1)
                    act.wait_ge(x_scaled, k + 1)
                    act.activation(w_x, w_x, ACT.Abs).then_inc(x_abs, 1)

            def task(n, j):
                kind, k = j
                if kind in ("xT", "D", "KT", "cT", "Q", "QT"):
                    src = front_bank(n, j)
                    act.wait_ge(front_filled, n.at(NF, FRONT.index(j) + 1))
                    if kind == "xT":
                        act.activation(xT[:], src[:].rearrange("p (m s) -> p m s", m=CT),
                                       ACT.Copy).then_inc(front_act, 1)
                    elif kind == "D":
                        act.activation(sq[:, k, 0:QC], src[:, 0:QC], ACT.Square, scale=QC ** -0.5,
                                       accum_out=ssq[:, k, 0:1])
                        act.activation(sq[:, k, QC:QC + KVC], src[:, QC:QC + KVC], ACT.Square, scale=KVC ** -0.5,
                                       accum_out=ssq[:, k, 1:2])
                        act.activation(raw[:, k, :], src[:, 0:DOWN], ACT.Copy).then_inc(front_act, 1)
                    elif kind == "KT":
                        act.activation(k_hi[n.parity][:], src[:, 0:S], ACT.Copy,
                                       scale=UP).then_inc(front_act, 1)
                    elif kind == "cT":
                        act.activation(ca_hi[:], src[:, 0:S], ACT.Copy, scale=UP)
                        act.activation(cb[0:QB, :], src[0:QB, S:2 * S], ACT.Copy,
                                       scale=UP).then_inc(front_act, 1)
                    elif kind == "Q":
                        act.activation(qtok[k % 4][:].rearrange("p h c -> p (h c)"), src[:],
                                       ACT.Copy).then_inc(front_act, 1)
                    else:
                        g, t = k // 2, k % 2
                        act.activation(q_hi[n.parity][:, QUAD * g:QUAD * g + QUAD, tok(t)],
                                       src[:].rearrange("p (h s) -> p h s", h=QUAD),
                                       ACT.Copy, scale=1.0 / UP).then_inc(front_act, 1)
                elif kind in ("OT", "x2T", "up"):
                    act.wait_ge(back_filled, n.at(NB_, BACK.index(j) + 1))
                    if kind == "OT":
                        t, half = k % 2, k // 2
                        act.activation(ot_hi[:, 4 * half:4 * half + 4, tok(t)],
                                       b_bank[:].rearrange("p (j s) -> p j s", j=4),
                                       ACT.Copy, scale=1.0 / PLIFT).then_inc(back_act, 1)
                    elif kind == "x2T":
                        act.activation(x2_hi[:], b_bank[:].rearrange("p (m s) -> p m s", m=CT), ACT.Copy,
                                       scale=UP).then_inc(back_act, 1)
                    else:
                        if k >= 2:
                            act.wait_ge(g_ready, n.at(4, k - 1))
                        for i in range(2):
                            last = act.activation(gu[k % 2][:, i, :], b_bank[:, S * i:S * (i + 1)],
                                                  ACT.Identity, scale=1.0 / UP,
                                                  bias=ub[:, 2 * k + i:2 * k + i + 1])
                        last.then_inc(back_act, 1)
                        act.wait_ge(back_act, n.at(NBA, BACK_ACT.index(j) + 1))
                        wait(act, gw_ready, n.at(4, k))
                        act.activation(gv[:], gu[k % 2][:], ACT.Square).then_inc(gv_ready, 1)
                elif kind == "gelu":
                    act.wait_ge(gz_ready, n.at(4, k + 1))
                    wait(act, g_ready, n.at(4, k))
                    act.activation(gt[:], gz[:], ACT.Tanh, scale=GELU_C * GELU_A).then_inc(gt_ready, 1)

            def exps(n, h):
                act.wait_ge(bias_ready, n.at(NH, h + 1))
                wait(act, probsT_ready, n.at(NH, h - 1))
                for t in range(QT):
                    last = act.activation(pr[h % 2][:, t, :], l_bank[h % 2][:, S * t:S * (t + 1)], ACT.Exp,
                                          scale=inv_s, bias=ebias[:, h % 2, t:t + 1],
                                          accum_out=rsum[:, h, t:t + 1])
                last.then_inc(probs_ready, 1)

            def pt_high(n, h):
                act.wait_ge(probsT_ready, n.at(NH, h + 1))
                wait(act, pv_done, n.at(NH, h - 1))
                act.activation(pt_hi[h % 2][:].rearrange("p k s -> p (k s)"), t_bank[h % 2][:],
                               ACT.Copy, scale=PLIFT).then_inc(pt_hi_ready, 1)

            def split_high(g):
                cols = slice(512 * g, 512 * (g + 1))
                if g == 0:
                    act.wait_ge(w_scaled, 1)
                act.activation(wa_hi[:, cols], flat(wf_a)[:, cols], ACT.Copy, scale=s_w)
                act.activation(wb_hh[0:QB, cols], flat(wf_b)[0:QB, cols], ACT.Copy, scale=s_w[0:QB])
                act.activation(wb_hh[QB:P, cols], flat(wf_b)[0:QB, cols], ACT.Copy,
                               scale=s_w[0:QB]).then_inc(w_high, 1)

            run_prologue(task, prep_task)

            def tasks(b, slot, i):
                for j in preparations(b, slot, i):
                    prep_task(j)
                for n, j in part(b, slot, i):
                    task(n, j)

            def iteration(b):
                for slot in range(NH):
                    if head(b, slot - 1):
                        exps(*head(b, slot - 1))
                    if head(b, slot - 2):
                        pt_high(*head(b, slot - 2))
                    tasks(b, slot - 1, 1)
                    tasks(b, slot, 0)

            iteration(Batch(0))
            iteration(Batch(1))
            with act.Fori(0, B // 2 - 2) as pair:
                iteration(Batch(2, pair))
                iteration(Batch(3, pair))
            for b in range(B - 2, B + 1):
                iteration(Batch(b))

        @block.vector
        def _(dve):
            steps = [0]

            def step(ins):
                steps[0] += 1
                ins.then_inc(prep_step, 1)
                dve.wait_ge(prep_step, steps[0])

            def low(dst, src, high, factor):
                return dve.scalar_tensor_tensor(out=dst, in0=src, scalar=factor, in1=high, op0=ALU.mult,
                                                op1=ALU.subtract)

            def over_partitions(k):
                step(dve.tensor_scalar(mx[:, 2 * k:2 * k + 2], mx[:, 2 * k:2 * k + 2], 1e-30, None, ALU.max))
                dve.sem_inc(max_asked, 1)
                dve.wait_ge(max_given, k + 1)
                return mx[:, 2 * k + 8:2 * k + 9], mx[:, 2 * k + 9:2 * k + 10]

            def power(ap):
                step(dve.tensor_scalar(ap.bitcast(I32), ap.bitcast(I32), 0x7F800000, None, ALU.bitwise_and))

            def scale_of(m, s, inv, top):
                power(m)
                step(dve.reciprocal(s, m))
                step(dve.tensor_scalar(s, s, top, None, ALU.mult))
                step(dve.tensor_scalar(inv, m, 1.0 / top, None, ALU.mult))

            step(dve.memset(mx[:], 0.0))
            dve.wait_ge(wd_loaded, 16 * 4)
            step(dve.tensor_reduce(mx[0:ROPE, 0:1], wd_n[0:ROPE, 2, :], AX.X, ALU.max,
                                   apply_absolute_value=True))
            m, _m = over_partitions(0)
            scale_of(m, small[:, 32:33], inv_kr, 1.0)
            step(dve.tensor_scalar(wd_n[0:ROPE, 2, :], wd_n[0:ROPE, 2, :], small[0:ROPE, 32:33], None,
                                   ALU.mult))
            dve.sem_inc(kr_scaled, 1)

            def scale_norms():
                dve.wait_ge(norms_loaded, 16 * 3)
                for q, s, r in ((qn_a, qs_a, qr_a), (qn_b, qs_b, qr_b)):
                    step(dve.tensor_scalar(s, q, SCALE, None, ALU.mult))
                    step(dve.tensor_scalar(r, s, inv_kr[0:q.shape[0]], None, ALU.mult))
                dve.sem_inc(norms_scaled, 1)

            def product(kind, k):
                i = prep_at[kind, k]
                dve.wait_ge(prep_filled, i + 1)
                src = prep_bank(i)
                hs = slice(8 * k, 8 * k + 8)
                rows, s, dst = (P, qs_a, wf_a) if kind == "ma" else (QB, qs_b, wf_b)
                dve.scalar_tensor_tensor(
                    out=dst[0:rows, hs, 0:KVC], in0=src[0:rows].rearrange("p (h c) -> p h c", h=8),
                    scalar=s, in1=kvn_r[0:rows].unsqueeze(1).to_broadcast([rows, 8, KVC]),
                    op0=ALU.mult, op1=ALU.mult).then_inc(prep_dve, 1)

            def scale_weights():
                dve.wait_ge(prep_dve, sum(j[2] == "dve" for j in prep))
                dve.wait_ge(prep_act, prep_count(prep_at["rb", 1]))
                step(dve.tensor_reduce(mx[:, 2:3], flat(wf_a), AX.X, ALU.max, apply_absolute_value=True))
                step(dve.tensor_reduce(mx[0:QB, 3:4], flat(wf_b)[0:QB], AX.X, ALU.max,
                                       apply_absolute_value=True))
                m, m2 = over_partitions(1)
                step(dve.tensor_tensor(m, m, m2, ALU.max))
                scale_of(m, s_w, inv_s, WMAX)
                step(dve.tensor_scalar(inv_s, inv_s, 1.0 / UP, None, ALU.mult))
                dve.sem_inc(w_scaled, 1)

            def split_low(g):
                cols = slice(512 * g, 512 * (g + 1))
                dve.wait_ge(w_high, g + 1)
                low(wb_lo[:, cols], flat(wf_b)[0:QB, cols], wb_hh[0:QB, cols], s_w[0:QB])
                low(wa_lo[:, cols], flat(wf_a)[:, cols], wa_hi[:, cols], s_w).then_inc(w_split, 1)

            def prep_task(j):
                kind, k = j
                if kind in ("ma", "mb"):
                    if prep_count(prep_at[j]) == 1:
                        scale_norms()
                    product(kind, k)
                elif kind == "wscale":
                    scale_weights()
                elif kind == "wsplit":
                    split_low(k)
                elif kind == "blocks":
                    amax, sc, inv, half = (blk[:, i, :] for i in range(4))
                    dve.wait_ge(prep_act, prep_count(prep_at["upT" if k == 0 else "dnT", 3]))
                    if k:
                        dve.wait_ge(step_ready, k)
                    step(dve.tensor_reduce(amax, blocks_of(w_T), AX.X, ALU.max, apply_absolute_value=True))
                    if k == 0:
                        step(dve.tensor_reduce(mx[:, 4:5], amax, AX.X, ALU.max))
                    step(dve.tensor_scalar(sc, amax, 1e-30, None, ALU.max))
                    power(sc)
                    step(dve.tensor_scalar(sc, sc, 0.25, None, ALU.mult))
                    step(dve.reciprocal(inv, sc))
                    step(dve.tensor_scalar(half, sc, 0.5, None, ALU.mult))
                    dve.sem_inc(blocks_ready, 1)
                elif kind == "levels":
                    i = k % len(MIDPOINTS)
                    if i == 0:
                        dve.wait_ge(x_abs, k // len(MIDPOINTS) + 1)
                        step(dve.tensor_scalar(w_c, w_x, MIDPOINTS[0], 2.0, ALU.is_ge, ALU.mult))
                    else:
                        if i == 3:
                            step(dve.tensor_scalar(w_c, w_c, 2.0, None, ALU.mult))
                        step(dve.scalar_tensor_tensor(out=w_c, in0=w_x, scalar=MIDPOINTS[i], in1=w_c,
                                                      op0=ALU.is_ge, op1=ALU.add))
                elif kind == "values":
                    dve.wait_ge(step_ready, k + 1)
                    dve.tensor_tensor(w_16[:], w_16[:], w_c, ALU.mult).then_inc(quantised, 1)
                elif kind == "bound":
                    dve.wait_ge(prep_act, prep_count(prep_at["ub", 0]))
                    step(dve.tensor_reduce(mx[:, 5:6], ub[:], AX.X, ALU.max, apply_absolute_value=True))
                    m, m2 = over_partitions(2)
                    step(dve.tensor_scalar(m, m, 2 * 1.5 * HID, None, ALU.mult))
                    step(dve.tensor_scalar(m2, m2, 2.0, None, ALU.mult))
                    step(dve.tensor_tensor(m, m, m2, ALU.add))
                    scale_of(m, s_g, inv_g, 2.0 ** 14)
                    step(dve.tensor_scalar(inv_g, inv_g, 0.5, None, ALU.mult))
                elif kind == "nscale":
                    dve.wait_ge(prep_act, prep_count(prep_at["n", 3]))
                    step(dve.tensor_reduce(mx[:, 6:7], flat(nf), AX.X, ALU.max, apply_absolute_value=True))
                    m, _m = over_partitions(3)
                    s_n = small[:, 34:35]
                    scale_of(m, s_n, inv_n, WMAX)
                    step(dve.tensor_scalar(inv_n, inv_n, 1.0 / UP, None, ALU.mult))
                    step(dve.tensor_scalar(flat(n_hi[:]), flat(nf), s_n, None, ALU.mult))
                    low(flat(n_lo[:]), flat(nf), flat(n_hi[:]), s_n).then_inc(n_split, 1)

            def ln(n, which, src):
                for t in range(QT):
                    dve.bn_stats(st[:, which, t, :], src[:, t, :]).then_inc(ln_stats[which], 1)
                dve.wait_ge(ln_stats[which], n.at(QT, QT))
                dve.memset(nothing[:], 0.0)
                for t in range(QT):
                    dve.bn_aggr(mv[:, which, t, :], st[:, which, t, :]).then_inc(ln_aggr[which], 1)

            def ln_apply(n, which, src, dst, ready):
                dve.wait_ge(ln_rstd[which], n.at(1, 1))
                for t in range(QT):
                    dve.tensor_scalar(dst[:, t, :], src[:, t, :], mv[:, which, t, 0:1],
                                      rstd[:, which, t:t + 1], ALU.subtract, ALU.mult).then_inc(ready, 1)

            def task(n, j):
                kind, k = j
                if kind == "ln1":
                    dve.wait_ge(xf_loaded, n.at(16, 16))
                    ln(n, 0, xf)
                elif kind == "ln1x":
                    ln_apply(n, 0, xf, xn, xn_ready)
                elif kind in ("KT", "cT", "QT"):
                    dve.wait_ge(front_act, n.at(NF, FRONT.index(j) + 1))
                    src = front_bank(n, j)
                    if kind == "KT":
                        low(k_lo[n.parity][:], src[:, 0:S], k_hi[n.parity][:], UP).then_inc(front_dve, 1)
                    elif kind == "cT":
                        low(cb[QB:P, :], src[0:QB, S:2 * S], cb[0:QB, :], UP)
                        low(ca_lo[:], src[:, 0:S], ca_hi[:], UP).then_inc(front_dve, 1)
                    else:
                        g, t = k // 2, k % 2
                        low(q_lo[n.parity][:, QUAD * g:QUAD * g + QUAD, tok(t)],
                            src[:].rearrange("p (h s) -> p h s", h=QUAD),
                            q_hi[n.parity][:, QUAD * g:QUAD * g + QUAD, tok(t)],
                            1.0 / UP).then_inc(front_dve, 1)
                elif kind == "scale":
                    dve.wait_ge(rms_ready, n.at(QT, k + 1))
                    dve.tensor_scalar(cq[:, k, :], raw[:, k, 0:QC], rms[:, k, 0:1], None,
                                      ALU.mult)
                    dve.tensor_scalar(kt[:, k, 0:KVC], raw[:, k, QC:QC + KVC], rms[:, k, 1:2], None,
                                      ALU.mult).then_inc(latents_ready, 1)
                    dve.wait_ge(latents_ready, n.at(QT, k + 1))
                    dve.tensor_scalar(c_hi[n.parity][:, k, :], kt[:, k, 0:KVC], UP, None,
                                      ALU.mult).then_inc(c_hi_ready, 1)
                    dve.wait_ge(c_hi_ready, n.at(QT, k + 1))
                    low(c_lo[n.parity][:, k, :], kt[:, k, 0:KVC], c_hi[n.parity][:, k, :],
                        UP).then_inc(c_ready, 1)
                elif kind == "OT":
                    t, half = k % 2, k // 2
                    dve.wait_ge(back_act, n.at(NBA, BACK_ACT.index(j) + 1))
                    hs = slice(4 * half, 4 * half + 4)
                    low(ot_lo[:, hs, tok(t)], b_bank[:].rearrange("p (j s) -> p j s", j=4),
                        ot_hi[:, hs, tok(t)], 1.0 / PLIFT).then_inc(back_dve, 1)
                elif kind == "proj":
                    dve.wait_ge(back_filled, n.at(NB_, BACK.index(j) + 1))
                    dve.wait_ge(xb_loaded, n.at(16, 16))
                    dve.scalar_tensor_tensor(out=x1[:], in0=b_bank[:].rearrange("p (t c) -> p t c", t=QT),
                                             scalar=inv_n, in1=xb[:], op0=ALU.mult,
                                             op1=ALU.add).then_inc(x1_ready, 1)
                    dve.wait_ge(x1_ready, n.at(1, 1))
                    dve.sem_inc(back_dve, 1)
                    ln(n, 1, x1)
                elif kind == "ln2":
                    ln_apply(n, 1, x1, x2n, x2n_ready)
                elif kind == "x2T":
                    dve.wait_ge(back_act, n.at(NBA, BACK_ACT.index(j) + 1))
                    low(x2_lo[:], b_bank[:].rearrange("p (m s) -> p m s", m=CT), x2_hi[:],
                        UP).then_inc(back_dve, 1)
                elif kind == "split":
                    dve.wait_ge(gt_ready, n.at(4, k + 1))
                    dve.scalar_tensor_tensor(out=gt[:], in0=gt[:], scalar=1.0, in1=gu[k % 2][:],
                                             op0=ALU.add, op1=ALU.mult).then_inc(g_raw, 1)
                    dve.wait_ge(g_raw, n.at(4, k + 1))
                    dve.tensor_scalar(g_hi[:, 2 * k:2 * k + 2, :], gt[:], s_g, None,
                                      ALU.mult).then_inc(g_hi_ready, 1)
                    dve.wait_ge(g_hi_ready, n.at(4, k + 1))
                    low(g_lo[:, 2 * k:2 * k + 2, :], gt[:], g_hi[:, 2 * k:2 * k + 2, :],
                        s_g).then_inc(g_ready, 1)
                elif kind == "down":
                    dve.wait_ge(back_filled, n.at(NB_, BACK.index(j) + 1))
                    dve.wait_ge(x1b_ready, n.at(1, 1))
                    wait(dve, stored, n.at(16, 0))
                    dve.scalar_tensor_tensor(out=ob[:], in0=b_bank[:].rearrange("p (t c) -> p t c", t=QT),
                                             scalar=inv_g, in1=x1b[:], op0=ALU.mult,
                                             op1=ALU.add).then_inc(ob_ready, 1)
                    dve.wait_ge(ob_ready, n.at(1, 1))
                    dve.sem_inc(back_dve, 1)

            def maxes(n, h):
                dve.wait_ge(logits_ready, n.at(NH, h + 1))
                dve.tensor_reduce(nmax[:, h % 2, :], l_bank[h % 2][:].rearrange("p (t s) -> p t s", t=QT),
                                  AX.X, ALU.max, negate=True).then_inc(max_found, 1)
                dve.wait_ge(max_found, n.at(NH, h + 1))
                dve.tensor_scalar(ebias[:, h % 2, :], nmax[:, h % 2, :], inv_s, None, ALU.mult).then_inc(bias_ready, 1)

            def pt_low(n, h):
                dve.wait_ge(pt_hi_ready, n.at(NH, h + 1))
                low(pt_lo[h % 2][:].rearrange("p k s -> p (k s)"), t_bank[h % 2][:],
                    pt_hi[h % 2][:].rearrange("p k s -> p (k s)"), PLIFT).then_inc(pt_lo_ready, 1)

            def normalise(n, g):
                hs = slice(QUAD * g, QUAD * g + QUAD)
                dve.wait_ge(pv_done, n.at(NH, QUAD * g + QUAD))
                if g == 0 and not n.first():
                    dve.wait_ge(back_filled, n.at(NB_, 4 - NB_))
                dve.reciprocal(rinv[:, hs, :], rsum[:, hs, :]).then_inc(rinv_ready, 1)
                dve.wait_ge(rinv_ready, n.at(NQ, g + 1))
                dve.tensor_tensor(otok[:, :, hs, :].rearrange("p t h c -> p h t c"),
                                  o_bank[:].rearrange("p (h t c) -> p h t c", h=QUAD, t=QT),
                                  rinv[:, hs, :].unsqueeze(3).to_broadcast([P, QUAD, QT, KVC]),
                                  ALU.mult).then_inc(o_ready, 1)

            run_prologue(task, prep_task)

            def tasks(b, slot, i):
                for j in preparations(b, slot, i):
                    prep_task(j)
                for n, j in part(b, slot, i):
                    task(n, j)

            def iteration(b):
                for slot in range(NH):
                    tasks(b, slot - 1, 0)
                    if head(b, slot):
                        maxes(*head(b, slot))
                    if head(b, slot - 3) and slot % QUAD == 2:
                        n, h = head(b, slot - 3)
                        normalise(n, h // QUAD)
                    if head(b, slot - 2):
                        pt_low(*head(b, slot - 2))
                    tasks(b, slot - 1, 1)

            iteration(Batch(0))
            iteration(Batch(1))
            with dve.Fori(0, B // 2 - 2) as pair:
                iteration(Batch(2, pair))
                iteration(Batch(3, pair))
            for b in range(B - 2, B + 1):
                iteration(Batch(b))

        @block.tensor
        def _(pe):
            def pairs(out_, terms):
                for i, (a, b) in enumerate(terms):
                    last = pe.matmul(out_, a, b, start=(i == 0), stop=(i == len(terms) - 1))
                return last

            pe.wait_ge(ident_made, 1)

            def prepare(kind, k):
                i = prep_at[kind, k]
                prep_free(pe, i)
                dst = prep_bank(i)
                if kind == "wd":
                    if k == 0:
                        pe.wait_ge(wd_loaded, 16 * 4)
                        pe.wait_ge(kr_scaled, 1)
                    for r, rows in enumerate((P, P, ROPE)):
                        last = pe.transpose(dst[:, P * r:P * r + rows], wd_n[0:rows, r, tok(k)],
                                            ident[0:rows, 0:rows])
                elif kind in ("ma", "mb"):
                    pe.wait_ge(wq_loaded, 16 * 3)
                    rows, cols = (P, slice(0, P)) if kind == "ma" else (QB, slice(P, QC))
                    for h in range(8):
                        last = pe.matmul(dst[0:rows, KVC * h:KVC * (h + 1)], wqn[:, 8 * k + h, cols],
                                         wkn[:, 8 * k + h, :], start=True, stop=True)
                elif kind in ("ra", "rb"):
                    pe.wait_ge(wq_loaded, 16 * 3)
                    rows, cols = (P, slice(0, P)) if kind == "ra" else (QB, slice(P, QC))
                    for j in range(4):
                        last = pe.transpose(dst[0:rows, P * j:P * (j + 1)], wqr[:, 4 * k + j, cols], ident[:])
                elif kind == "ub":
                    pe.wait_ge(vec_loaded, 16 * 4)
                    last = pe.transpose(dst[:, 0:FT], ub_n[:], ident[0:FT, 0:FT])
                elif kind == "wo":
                    pe.wait_ge(wo_loaded[k // 2 % 2], 16 * (k // 4 + 1))
                    for h in range(2):
                        for m in range(CT):
                            at = P * (2 * (k % 2) + h)
                            last = pe.transpose(dst[:, HID * h + P * m:HID * h + P * (m + 1)],
                                                wo_n[:, k // 2 % 2, m, at:at + P], ident[:])
                elif kind == "n":
                    pe.wait_ge(prep_act, prep_count(prep_at["wo", 2 * k + 1]))
                    pe.wait_ge(wv_loaded, 16)
                    for j in range(2):
                        for odd in range(2):
                            h = 2 * (2 * k + j) + odd
                            last = pe.matmul(dst[KVC * odd:KVC * (odd + 1), HID * j:HID * (j + 1)],
                                             wvn[:, h, :], woT[:, j, odd, :], start=True, stop=True)
                elif kind == "upT":
                    pe.wait_ge(up_loaded, 16)
                    for f in range(2):
                        for m in range(CT):
                            at = FF * m + P * (2 * k + f)
                            last = pe.transpose(dst[:, HID * f + P * m:HID * f + P * (m + 1)],
                                                w_nat[:, at:at + P], ident[:])
                elif kind == "upB":
                    pe.wait_ge(ident16_made, 1)
                    pe.wait_ge(quantised, 1)
                    for f in range(FT):
                        at = HID * f + P * k
                        last = pe.transpose(dst[:].bitcast(BF16)[:, P * f:P * (f + 1)], w_16[:, at:at + P],
                                            ident16[:])
                elif kind == "dnT":
                    pe.wait_ge(dn_loaded, 16)
                    for f in range(4):
                        at = HID * (4 * (k % 2) + f) + P * (k // 2)
                        last = pe.transpose(dst[:, P * f:P * (f + 1)], w_nat[:, at:at + P], ident[:])
                else:
                    pe.wait_ge(quantised, 2)
                    for f in range(4):
                        for d in range(CT):
                            at = FF * d + P * (4 * k + f)
                            to = HID * f + P * d
                            last = pe.transpose(dst[:].bitcast(BF16)[:, to:to + P], w_16[:, at:at + P],
                                                ident16[:])
                last.then_inc(prep_filled, 1)

            def job(n, j):
                kind, k = j
                if j in FRONT:
                    free_front(pe, n, j)
                    dst = front_bank(n, j)
                    if kind == "xT":
                        pe.wait_ge(xn_ready, n.at(QT, QT))
                        for t in range(QT):
                            for m in range(CT):
                                last = pe.transpose(dst[:, S * m + P * t:S * m + P * (t + 1)],
                                                    xn[:, t, tok(m)], ident[:])
                    elif kind == "D":
                        if n.first():
                            pe.wait_ge(prep_act, prep_count(prep_at["wd", CT - 1]))
                        pe.wait_ge(front_act, n.at(NF, 1))
                        last = pairs(dst[:, 0:DOWN], [(xT[:, m, tok(k)], wdT[:, m, :]) for m in range(CT)])
                    elif kind == "KT":
                        pe.wait_ge(latents_ready, n.at(QT, QT))
                        pe.wait_ge(kr_ready, n.at(QT, QT))
                        for t in range(QT):
                            last = pe.transpose(dst[:, tok(t)], kt[:, t, :], ident[:])
                    elif kind == "cT":
                        pe.wait_ge(latents_ready, n.at(QT, QT))
                        for t in range(QT):
                            pe.transpose(dst[:, tok(t)], cq[:, t, 0:P], ident[:])
                            last = pe.transpose(dst[0:QB, S + P * t:S + P * (t + 1)], cq[:, t, P:QC], ident[:])
                    elif kind == "Q":
                        g, t = k // 2, k % 2
                        if k == 0:
                            pe.wait_ge(front_dve, n.at(NFD, FRONT_DVE.index(("cT", 0)) + 1))
                        if n.first() and t == 0:
                            pe.wait_ge(w_split, g + 1)
                        cols = slice(512 * g, 512 * (g + 1))
                        last = pairs(dst[:], [(ca_hi[:, tok(t)], wa_hi[:, cols]),
                                              (ca_hi[:, tok(t)], wa_lo[:, cols]),
                                              (ca_lo[:, tok(t)], wa_hi[:, cols]),
                                              (cb[:, tok(t)], wb_hh[:, cols]),
                                              (cb[0:QB, tok(t)], wb_lo[:, cols])])
                    else:
                        pe.wait_ge(qtok_ready, n.at(8, k + 1))
                        for h in range(QUAD):
                            last = pe.transpose(dst[:, tok(h)], qtok[k % 4][:, h, :], ident[:])
                    last.then_inc(front_filled, 1)
                else:
                    if kind in ("projA", "downA"):
                        free_back(pe, n, (kind[:4], 0))
                    elif kind not in ("proj", "down"):
                        free_back(pe, n, j)
                    if kind == "OT":
                        t, half = k % 2, k // 2
                        pe.wait_ge(o_ready, n.at(NQ, 2 * half + 2))
                        for i in range(4):
                            h = 8 * half + 2 * i
                            last = pe.transpose(b_bank[:, tok(i)],
                                                otok[:, t, h:h + 2, :].rearrange("p h c -> p (h c)"), ident[:])
                    elif kind in ("projA", "proj"):
                        if n.first():
                            pe.wait_ge(n_split, 1)
                        t = int(kind == "proj")
                        last = pairs(b_bank[:, HID * t:HID * (t + 1)],
                                     [(a[:, i, tok(t)], w[:, i, :]) for i in range(PAIRS)
                                      for a, w in ((ot_hi, n_hi), (ot_hi, n_lo), (ot_lo, n_hi))])
                    elif kind == "x2T":
                        pe.wait_ge(x2n_ready, n.at(QT, QT))
                        for t in range(QT):
                            for m in range(CT):
                                last = pe.transpose(b_bank[:, S * m + P * t:S * m + P * (t + 1)],
                                                    x2n[:, t, tok(m)], ident[:])
                    elif kind == "up":
                        for i in range(2):
                            f = 2 * k + i
                            last = pairs(b_bank[:, S * i:S * (i + 1)],
                                         [(up_q[:, m, tok(f)], a[:, m, :]) for m in range(CT)
                                          for a in (x2_hi, x2_lo)])
                    else:
                        pe.wait_ge(g_ready, n.at(4, 4))
                        t = int(kind == "down")
                        last = pairs(b_bank[:, HID * t:HID * (t + 1)],
                                     [(a[:, f, tok(t)], dn_q[:, f, :]) for f in range(FT)
                                      for a in (g_hi, g_lo)])
                    if kind not in ("projA", "downA"):
                        last.then_inc(back_filled, 1)

            def logits(n, h):
                if h % QUAD == 0:
                    k = 2 * (h // QUAD)
                    at = max(FRONT_DVE.index(("QT", k)), FRONT_DVE.index(("QT", k + 1)))
                    pe.wait_ge(front_dve, n.at(NFD, at + 1))
                wait(pe, probs_ready, n.at(NH, h - 1))
                p = n.parity
                for t in range(QT):
                    last = pairs(l_bank[h % 2][:, S * t:S * (t + 1)],
                                 [(q_hi[p][:, h, tok(t)], k_hi[p][:]), (q_hi[p][:, h, tok(t)], k_lo[p][:]),
                                  (q_lo[p][:, h, tok(t)], k_hi[p][:])])
                last.then_inc(logits_ready, 1)

            def transpose_probs(n, h):
                pe.wait_ge(probs_ready, n.at(NH, h + 1))
                wait(pe, pt_lo_ready, n.at(NH, h - 1))
                for t in range(QT):
                    for k in range(QT):
                        last = pe.transpose(t_bank[h % 2][:, S * k + P * t:S * k + P * (t + 1)],
                                            pr[h % 2][:, t, tok(k)], ident[:])
                last.then_inc(probsT_ready, 1)

            def values(n, h):
                pe.wait_ge(pt_lo_ready, n.at(NH, h + 1))
                if h == 0:
                    pe.wait_ge(c_ready, n.at(QT, QT))
                if h % QUAD == 0:
                    wait(pe, o_ready, n.at(NQ, h // QUAD))
                p = n.parity
                for t in range(QT):
                    at = KVC * (2 * (h % QUAD) + t)
                    last = pairs(o_bank[:, at:at + KVC],
                                 [(w[h % 2][:, k, tok(t)], c[p][:, k, :]) for k in range(QT)
                                  for w, c in ((pt_hi, c_hi), (pt_hi, c_lo), (pt_lo, c_hi))])
                last.then_inc(pv_done, 1)

            def prep_task(j):
                if j[0] in PREP_ROLES:
                    prepare(*j)

            def task(n, j):
                if j in FRONT + BACK or j[0] in ("projA", "downA"):
                    job(n, j)

            run_prologue(task, prep_task)

            def jobs(b, slot, i):
                for j in preparations(b, slot, i):
                    prep_task(j)
                for n, j in part(b, slot, i):
                    task(n, j)

            def iteration(b):
                for slot in range(NH):
                    if head(b, slot):
                        logits(*head(b, slot))
                    if head(b, slot - 3):
                        values(*head(b, slot - 3))
                    jobs(b, slot, 0)
                    if head(b, slot - 1):
                        transpose_probs(*head(b, slot - 1))
                    jobs(b, slot, 1)

            iteration(Batch(0))
            iteration(Batch(1))
            with pe.Fori(0, B // 2 - 2) as pair:
                iteration(Batch(2, pair))
                iteration(Batch(3, pair))
            for b in range(B - 2, B + 1):
                iteration(Batch(b))


_NAMES = ["L0_attn_x", "L0_attn_w_q_down", "L0_attn_q_norm_w", "L0_attn_w_q_nope", "L0_attn_w_q_rope",
          "L0_attn_w_kv_down", "L0_attn_kv_norm_w", "L0_attn_w_k_nope", "L0_attn_w_v_up", "L0_attn_w_k_rope",
          "L0_attn_w_o", "L0_ffn_up_kernel", "L0_ffn_up_bias", "L0_ffn_down_kernel", "L0_ffn_down_bias"]


def _rope_table():
    import numpy as np
    inv = (np.float32(1.0) / np.power(np.float32(10000.0), np.arange(0, ROPE, 2, dtype=np.float32)
                                      / np.float32(ROPE))).astype(np.float32)
    f = np.arange(S, dtype=np.float32)[:, None] * inv[None, :]
    c, s = np.cos(f).astype(np.float32), np.sin(f).astype(np.float32)
    return np.stack([np.concatenate([c, c], 1), np.concatenate([-s, s], 1)], 1)


def kernel(**inputs):
    import numpy as np
    import concourse.bacc as bacc
    from concourse.bass_utils import run_bass_kernel_spmd

    nc = bacc.Bacc("TRN2", target_bir_lowering=False, num_devices=1)
    arrays, args = {}, []
    for name in _NAMES:
        a = np.ascontiguousarray(inputs[name])
        arrays[name + "_in"] = a
        args.append(nc.dram_tensor(name + "_in", a.shape, mybir.dt.from_np(a.dtype), kind="ExternalInput").ap())
    table = _rope_table()
    arrays["rope_table"] = table
    args.append(nc.dram_tensor("rope_table", table.shape, F32, kind="ExternalInput").ap())
    args.append(nc.dram_tensor("out", (B, S, HID), F32, kind="ExternalOutput").ap())
    build(nc, *args)
    r = run_bass_kernel_spmd(nc, [arrays], core_ids=[0])
    return r.results[0]["out"]
```
